# Optimizing a Trainium2 kernel written in Bass

```python
import numpy as np
import jax
import jax.numpy as jnp

def _softmax(x, axis=-1):
    return jax.nn.softmax(x, axis=axis)

def _gelu(x):
    return jax.nn.gelu(x, approximate=True)

def _silu(x):
    return jax.nn.silu(x)

def _sigmoid(x):
    return jax.nn.sigmoid(x)

def _layernorm(x, axis=-1, eps=1e-05):
    m = jnp.mean(x, axis=axis, keepdims=True)
    v = jnp.var(x, axis=axis, keepdims=True)
    return (x - m) / jnp.sqrt(v + eps)

def _scatter_add(tgt, idx, src, axis=0):
    return tgt.at[idx].add(src)

def _segment_sum(src, seg, n):
    return jax.ops.segment_sum(src, seg, n)
kernel_name = 'mk_gnn_resnorm_d4_gnn_r32_c3471a'

def setup_inputs(seed: int=0):
    np.random.seed(seed)
    _w = jnp.asarray

    def _rec_inputs():
        import jax
        import jax.numpy as jnp
        _gk = jax.random.key(seed)
        x = -0.0003713 + 1 * jax.random.normal(jax.random.fold_in(_gk, 1), (3125, 128), jnp.float32)
        _s = jax.random.randint(jax.random.fold_in(_gk, 2), (50000,), 0, 3125, jnp.int32)
        _d = jax.random.randint(jax.random.fold_in(_gk, 3), (50000,), 0, 3125, jnp.int32)
        _loop = jnp.arange(3125, dtype=jnp.int32)
        src = jnp.concatenate([_s, _d, _loop])
        dst = jnp.concatenate([_d, _s, _loop])
        _o = jnp.argsort(dst, stable=True)
        src = src[_o]
        dst = dst[_o]
        edge_attr_16 = -1.02531e-05 + 0.999808 * jax.random.normal(jax.random.fold_in(_gk, 12), (103125, 16), jnp.float32)
        edge_weight = jax.random.uniform(jax.random.fold_in(_gk, 14), (103125,), jnp.float32, 0.0, 1)
        return (x, src, dst, edge_attr_16, edge_weight)
    x, src, dst, edge_attr_16, edge_weight = _rec_inputs()

    def _L0_gnn_setup():
        import jax, jax.numpy as jnp
        import numpy as np
        N_NODES = 3125
        N_EDGES = 50000
        D_IN = 128
        D_OUT = 128
        key = jax.random.key(seed)
        ks = jax.random.split(key, 8)
        h = jax.random.normal(ks[0], (N_NODES, D_IN), dtype=jnp.float32)
        edge_src = jax.random.randint(ks[1], (N_EDGES,), 0, N_NODES, dtype=jnp.int32)
        edge_dst = jax.random.randint(ks[2], (N_EDGES,), 0, N_NODES, dtype=jnp.int32)
        edge_val = jnp.ones((N_EDGES,), dtype=jnp.float32)
        s1 = 1.0 / np.sqrt(D_IN)
        s2 = 1.0 / np.sqrt(D_OUT)
        W1 = jax.random.uniform(ks[3], (D_IN, D_OUT), jnp.float32, -s1, s1)
        b1 = jax.random.uniform(ks[4], (D_OUT,), jnp.float32, -s1, s1)
        W2 = jax.random.uniform(ks[5], (D_OUT, D_OUT), jnp.float32, -s2, s2)
        b2 = jax.random.uniform(ks[6], (D_OUT,), jnp.float32, -s2, s2)
        eps = jnp.zeros((), dtype=jnp.float32)
        return {'h': h, 'edge_src': edge_src, 'edge_dst': edge_dst, 'edge_val': edge_val, 'W1': W1, 'b1': b1, 'W2': W2, 'b2': b2, 'eps': eps}
    _L0_gnn_all = _L0_gnn_setup()
    _L0_gnn_in = {k: v for k, v in _L0_gnn_all.items() if k in ('W1', 'b1', 'W2', 'b2', 'eps')}
    del _L0_gnn_all

    def _L1_gnn_setup():
        import jax, jax.numpy as jnp
        import numpy as np
        N_NODES = 3125
        DIM = 128
        N_EDGES = 20000
        key = jax.random.key(seed)
        k_x, k_e, k_w1, k_b1, k_w2, k_b2 = jax.random.split(key, 6)
        x = jax.random.normal(k_x, (N_NODES, DIM), dtype=jnp.float32)
        edge_index = jax.random.randint(k_e, (2, N_EDGES), 0, N_NODES, dtype=jnp.int64)
        s = 1.0 / np.sqrt(DIM)
        W1 = jax.random.uniform(k_w1, (DIM, DIM), minval=-s, maxval=s, dtype=jnp.float32)
        b1 = jax.random.uniform(k_b1, (DIM,), minval=-s, maxval=s, dtype=jnp.float32)
        W2 = jax.random.uniform(k_w2, (DIM, DIM), minval=-s, maxval=s, dtype=jnp.float32)
        b2 = jax.random.uniform(k_b2, (DIM,), minval=-s, maxval=s, dtype=jnp.float32)
        return {'x': x, 'edge_index': edge_index, 'W1': W1, 'b1': b1, 'W2': W2, 'b2': b2}
    _L1_gnn_all = _L1_gnn_setup()
    _L1_gnn_in = {k: v for k, v in _L1_gnn_all.items() if k in ('W1', 'b1', 'W2', 'b2')}
    del _L1_gnn_all

    def _L2_gnn_setup():
        import jax, jax.numpy as jnp
        import numpy as np
        NEG_SLOPE = 0.2

        def gat_conv(x, src, dst, W, att_src, att_dst, bias, heads, out_c, concat):
            N = x.shape[0]
            xh = (x @ W).reshape(N, heads, out_c)
            a_src = jnp.sum(xh * att_src, axis=-1)
            a_dst = jnp.sum(xh * att_dst, axis=-1)
            alpha = a_src[src] + a_dst[dst]
            alpha = jax.nn.leaky_relu(alpha, NEG_SLOPE)
            m = jax.ops.segment_max(alpha, dst, num_segments=N)
            e = jnp.exp(alpha - m[dst])
            s = jax.ops.segment_sum(e, dst, num_segments=N)
            coef = e / s[dst]
            msg = xh[src] * coef[:, :, None]
            out = jax.ops.segment_sum(msg, dst, num_segments=N)
            if concat:
                out = out.reshape(N, heads * out_c)
            else:
                out = out.mean(axis=1)
            return out + bias
        key = jax.random.key(seed)
        ks = jax.random.split(key, 12)
        N, E = (50000, 12500)
        Fin, Hc, H, Fout = (128, 16, 8, 128)
        x = jax.random.normal(ks[0], (N, Fin), dtype=jnp.float32)
        src = jax.random.randint(ks[1], (E,), 0, N, dtype=jnp.int32)
        dst = jax.random.randint(ks[2], (E,), 0, N, dtype=jnp.int32)
        g = lambda k, shp, fan: (jax.random.normal(k, shp, dtype=jnp.float32) * (1.0 / np.sqrt(fan))).astype(jnp.float32)
        return {'x': x, 'src': src, 'dst': dst, 'W1': g(ks[3], (Fin, H * Hc), Fin), 'att_src1': g(ks[4], (H, Hc), Hc), 'att_dst1': g(ks[5], (H, Hc), Hc), 'b1': jnp.zeros((H * Hc,), dtype=jnp.float32), 'W2': g(ks[6], (H * Hc, Fout), H * Hc), 'att_src2': g(ks[7], (1, Fout), Fout), 'att_dst2': g(ks[8], (1, Fout), Fout), 'b2': jnp.zeros((Fout,), dtype=jnp.float32)}
    _L2_gnn_all = _L2_gnn_setup()
    _L2_gnn_in = {k: v for k, v in _L2_gnn_all.items() if k in ('W1', 'att_src1', 'att_dst1', 'b1', 'W2', 'att_src2', 'att_dst2', 'b2')}
    del _L2_gnn_all

    def _L3_gnn_setup():
        import jax, jax.numpy as jnp
        import numpy as np
        N = 50000
        E = 18750
        D = 128
        FE = 16
        L = 5

        def _sage_conv(x, edge_attr, src, dst, W, b, ew, eb):
            n = x.shape[0]
            edge_emb = edge_attr @ ew.T + eb
            msg = x[src] + edge_emb
            agg = jax.ops.segment_sum(msg, dst, num_segments=n)
            agg = agg + x + eb
            deg = jax.ops.segment_sum(jnp.ones((src.shape[0],), x.dtype), dst, num_segments=n) + 1.0
            mean = agg / deg[:, None]
            return mean @ W + b
        key = jax.random.key(seed)
        ks = jax.random.split(key, 6)
        x = jax.random.normal(ks[0], (N, D), dtype=jnp.float32)
        edge_attr = jax.random.normal(ks[1], (E, FE), dtype=jnp.float32)
        src = jax.random.randint(ks[2], (E,), 0, N, dtype=jnp.int32)
        dst = (src + 1 + jax.random.randint(ks[3], (E,), 0, N - 1, dtype=jnp.int32)) % N
        g = float(np.sqrt(6.0 / (D + D)))
        Ws = jax.random.uniform(ks[4], (L, D, D), jnp.float32, -g, g)
        bs = jnp.zeros((L, D), jnp.float32)
        ge = float(np.sqrt(6.0 / (D + FE)))
        ews = jax.random.uniform(ks[5], (L, D, FE), jnp.float32, -ge, ge)
        ebs = jnp.zeros((L, D), jnp.float32)
        return {'x': x, 'edge_attr': edge_attr, 'src': src, 'dst': dst, 'Ws': Ws, 'bs': bs, 'ews': ews, 'ebs': ebs}
    _L3_gnn_all = _L3_gnn_setup()
    _L3_gnn_in = {k: v for k, v in _L3_gnn_all.items() if k in ('Ws', 'bs', 'ews', 'ebs')}
    del _L3_gnn_all
    return {'x': x, 'src': src, 'dst': dst, 'edge_attr_16': edge_attr_16, 'edge_weight': edge_weight, 'L0_gnn_W1': _L0_gnn_in['W1'], 'L0_gnn_b1': _L0_gnn_in['b1'], 'L0_gnn_W2': _L0_gnn_in['W2'], 'L0_gnn_b2': _L0_gnn_in['b2'], 'L0_gnn_eps': _L0_gnn_in['eps'], 'L1_gnn_W1': _L1_gnn_in['W1'], 'L1_gnn_b1': _L1_gnn_in['b1'], 'L1_gnn_W2': _L1_gnn_in['W2'], 'L1_gnn_b2': _L1_gnn_in['b2'], 'L2_gnn_W1': _L2_gnn_in['W1'], 'L2_gnn_att_src1': _L2_gnn_in['att_src1'], 'L2_gnn_att_dst1': _L2_gnn_in['att_dst1'], 'L2_gnn_b1': _L2_gnn_in['b1'], 'L2_gnn_W2': _L2_gnn_in['W2'], 'L2_gnn_att_src2': _L2_gnn_in['att_src2'], 'L2_gnn_att_dst2': _L2_gnn_in['att_dst2'], 'L2_gnn_b2': _L2_gnn_in['b2'], 'L3_gnn_Ws': _L3_gnn_in['Ws'], 'L3_gnn_bs': _L3_gnn_in['bs'], 'L3_gnn_ews': _L3_gnn_in['ews'], 'L3_gnn_ebs': _L3_gnn_in['ebs']}

def reference(x, src, dst, edge_attr_16, edge_weight, L0_gnn_W1, L0_gnn_b1, L0_gnn_W2, L0_gnn_b2, L0_gnn_eps, L1_gnn_W1, L1_gnn_b1, L1_gnn_W2, L1_gnn_b2, L2_gnn_W1, L2_gnn_att_src1, L2_gnn_att_dst1, L2_gnn_b1, L2_gnn_W2, L2_gnn_att_src2, L2_gnn_att_dst2, L2_gnn_b2, L3_gnn_Ws, L3_gnn_bs, L3_gnn_ews, L3_gnn_ebs):
    import jax
    import jax.numpy as jnp

    def _L0_gnn_ref(h, edge_src, edge_dst, edge_val, W1, b1, W2, b2, eps):
        import jax, jax.numpy as jnp
        import numpy as np
        N_NODES = 3125
        N_EDGES = 50000
        D_IN = 128
        D_OUT = 128
        neigh = jax.ops.segment_sum(h[edge_src] * edge_val[:, None], edge_dst, num_segments=N_NODES)
        x = (1.0 + eps) * h + neigh
        x = jax.nn.relu(x @ W1 + b1)
        x = x @ W2 + b2
        return jax.nn.relu(x)

    def _L1_gnn_ref(x, edge_index, W1, b1, W2, b2):
        import jax, jax.numpy as jnp
        import numpy as np
        N_NODES = 3125
        DIM = 128
        N_EDGES = 20000
        row, col = (edge_index[0], edge_index[1])
        n = x.shape[0]
        msg = x[col]
        summed = jax.ops.segment_sum(msg, row, num_segments=n)
        deg = jax.ops.segment_sum(jnp.ones((row.shape[0],), x.dtype), row, num_segments=n)
        agg = summed / jnp.maximum(deg, 1.0)[:, None]
        h = jax.nn.relu(agg @ W1.T + b1)
        return h @ W2.T + b2

    def _L2_gnn_ref(x, src, dst, W1, att_src1, att_dst1, b1, W2, att_src2, att_dst2, b2):
        import jax, jax.numpy as jnp
        import numpy as np
        NEG_SLOPE = 0.2

        def gat_conv(x, src, dst, W, att_src, att_dst, bias, heads, out_c, concat):
            N = x.shape[0]
            xh = (x @ W).reshape(N, heads, out_c)
            a_src = jnp.sum(xh * att_src, axis=-1)
            a_dst = jnp.sum(xh * att_dst, axis=-1)
            alpha = a_src[src] + a_dst[dst]
            alpha = jax.nn.leaky_relu(alpha, NEG_SLOPE)
            m = jax.ops.segment_max(alpha, dst, num_segments=N)
            e = jnp.exp(alpha - m[dst])
            s = jax.ops.segment_sum(e, dst, num_segments=N)
            coef = e / s[dst]
            msg = xh[src] * coef[:, :, None]
            out = jax.ops.segment_sum(msg, dst, num_segments=N)
            if concat:
                out = out.reshape(N, heads * out_c)
            else:
                out = out.mean(axis=1)
            return out + bias
        N = x.shape[0]
        loops = jnp.arange(N, dtype=src.dtype)
        s = jnp.concatenate([src, loops])
        d = jnp.concatenate([dst, loops])
        h = gat_conv(x, s, d, W1, att_src1, att_dst1, b1, heads=8, out_c=16, concat=True)
        h = jax.nn.elu(h)
        out = gat_conv(h, s, d, W2, att_src2, att_dst2, b2, heads=1, out_c=128, concat=False)
        return out

    def _L3_gnn_ref(x, edge_attr, src, dst, Ws, bs, ews, ebs):
        import jax, jax.numpy as jnp
        import numpy as np
        N = 50000
        E = 18750
        D = 128
        FE = 16
        L = 5

        def _sage_conv(x, edge_attr, src, dst, W, b, ew, eb):
            n = x.shape[0]
            edge_emb = edge_attr @ ew.T + eb
            msg = x[src] + edge_emb
            agg = jax.ops.segment_sum(msg, dst, num_segments=n)
            agg = agg + x + eb
            deg = jax.ops.segment_sum(jnp.ones((src.shape[0],), x.dtype), dst, num_segments=n) + 1.0
            mean = agg / deg[:, None]
            return mean @ W + b
        h = x
        for l in range(L):
            h = _sage_conv(h, edge_attr, src, dst, Ws[l], bs[l], ews[l], ebs[l])
            if l < L - 1:
                h = jax.nn.relu(h)
        return h
    edge_index = jnp.stack([src, dst])
    x = _layernorm(x + _L0_gnn_ref(x, src, dst, edge_weight, L0_gnn_W1, L0_gnn_b1, L0_gnn_W2, L0_gnn_b2, L0_gnn_eps), axis=-1)
    x = _layernorm(x + _L1_gnn_ref(x, edge_index, L1_gnn_W1, L1_gnn_b1, L1_gnn_W2, L1_gnn_b2), axis=-1)
    x = _layernorm(x + _L2_gnn_ref(x, src, dst, L2_gnn_W1, L2_gnn_att_src1, L2_gnn_att_dst1, L2_gnn_b1, L2_gnn_W2, L2_gnn_att_src2, L2_gnn_att_dst2, L2_gnn_b2), axis=-1)
    x = _layernorm(x + _L3_gnn_ref(x, edge_attr_16, src, dst, L3_gnn_Ws, L3_gnn_bs, L3_gnn_ews, L3_gnn_ebs), axis=-1)
    return x

_drawn_inputs = setup_inputs


def setup_inputs(seed=0):
    import zlib

    import numpy as np

    out = dict(_drawn_inputs(seed))
    spreads = {'L2_gnn_b1': (0.0, 0.1),
     'L2_gnn_b2': (0.0, 0.1),
     'L3_gnn_bs': (0.0, 0.1),
     'L3_gnn_ebs': (0.0, 0.1)}
    factors = {'L0_gnn_b1': 3.947,
     'L2_gnn_att_dst1': 3.541,
     'L2_gnn_att_src2': 6.864,
     'L2_gnn_att_dst2': 8.0}
    for name, (base, spread) in spreads.items():
        noise = np.random.default_rng([zlib.crc32(name.encode()), seed]).standard_normal(out[name].shape)
        drawn = base * np.exp(spread * noise) if base else spread * noise
        out[name] = jnp.asarray(drawn.astype(out[name].dtype))
    for name, factor in factors.items():
        out[name] = (out[name] * factor).astype(out[name].dtype)
    return out
```

```python
from contextlib import ExitStack

import concourse.bass as bass
from concourse import mybir

F32 = mybir.dt.float32
BF16 = mybir.dt.bfloat16
I16 = mybir.dt.int16
I32 = mybir.dt.int32
ALU = mybir.AluOpType
ACT = mybir.ActivationFunctionType
AX_X = mybir.AxisListType.X

P = 128
N_NODES = 3125
N_EDGES = 103125
D = 128
FE = 16
TILES = -(-N_NODES // P)
NP = TILES * P
STRIP = 5
STRIPS = TILES // STRIP
SW = STRIP * P
BANK = 512
CPG = 4
GROUPS = -(-N_EDGES // (CPG * P))
CHUNKS = GROUPS * CPG
E_PAD = CHUNKS * P
NO_NODE = 4095
CB = 448
CBANKS = 7
CW = CB * CBANKS
AGG = D + FE + 1
HEADS = 8
HC = D // HEADS
LAYERS = 5
LN_EPS = 1e-5
SLOPE = 0.2
FAR = 1.0e30
BIG = 3.0e38

assert CW >= N_NODES and TILES % STRIP == 0 and 2 * P >= GROUPS > P


class Memory:

    def __init__(self, nc, ctx, phase):
        self.nc, self.ctx, self.phase, self.sems = nc, ctx, phase, []
        ctx.callback(self.free_sems)

    def sb(self, name, shape, dtype):
        return self.ctx.enter_context(self.nc.sbuf_tensor(f"{self.phase}_{name}", shape, dtype))

    def ps(self, name, shape, dtype=F32):
        return self.ctx.enter_context(self.nc.psum_tensor(f"{self.phase}_{name}", shape, dtype))

    def sem(self, name):
        self.sems.append(self.nc.alloc_semaphore(f"{self.phase}_{name}"))
        return self.sems[-1]

    def free_sems(self):
        if self.sems:
            self.nc.clear_and_free_semaphores(self.sems)
            with self.nc.Block():
                pass


class Chain:

    def __init__(self, eng, sem, before=0):
        self.eng, self.sem, self.n, self.before = eng, sem, 0, before

    def __call__(self, ins):
        self.n += 1
        ins.then_inc(self.sem, 1)
        self.eng.wait_ge(self.sem, self.before + self.n)


def mid(row, n):
    p, w = row.shape
    return row.unsqueeze(1).broadcast_to([p, n, w])


def last(cols, n):
    p, k = cols.shape
    return cols.unsqueeze(2).broadcast_to([p, k, n])


def halves(w):
    return [(0, BANK), (BANK, w)]


def edge_tables(nc, a, k):
    with ExitStack() as ctx:
        m = Memory(nc, ctx, "tab")
        names = ("src", "dst", "w")
        low = P
        high = GROUPS - P
        raw = {(n, h): m.sb(f"raw_{n}{h}", [P, CPG * P], F32 if n == "w" else I32)
               for n in names for h in (0, 1)}
        val = {(n, h): m.sb(f"val_{n}{h}", [P, CPG * P], F32) for n in names[:2] for h in (0, 1)}
        val.update({("w", h): raw["w", h] for h in (0, 1)})
        ext = m.sb("ext", [P, 4], F32)
        grp = m.sb("grp", [TILES, GROUPS], F32)
        t_lo = m.sb("t_lo", [TILES, 1], F32)
        t_hi = m.sb("t_hi", [TILES, 1], F32)
        c0 = m.sb("c0", [TILES, GROUPS], F32)
        c1 = m.sb("c1", [TILES, GROUPS], F32)
        c2 = m.sb("c2", [TILES, GROUPS], F32)
        lohi = m.sb("lohi", [TILES, 2], F32)
        lohi_i = m.sb("lohi_i", [TILES, 2], I32)
        pT = m.ps("pT", [P, 6, BANK])
        pG = m.ps("pG", [TILES, 2, 256])
        loaded, iotas, cast = m.sem("loaded"), m.sem("iotas"), m.sem("cast")
        turned, rows_done = m.sem("turned"), m.sem("rows_done")
        chain, ranges, moved = m.sem("chain"), m.sem("ranges"), m.sem("moved")
        size = [low, high]
        with nc.Block() as block:
            @block.sync
            def _(sp):
                for n in names:
                    rows = a[n].rearrange("(g e) -> g e", e=CPG * P)
                    sp.dma_start(raw[n, 0][:, :], rows[0:low]).then_inc(loaded, 16)
                    sp.dma_start(raw[n, 1][0:high, :], rows[low:GROUPS]).then_inc(loaded, 16)
                sp.wait_ge(ranges, 1)
                sp.dma_start(k.ranges_dram, lohi_i[:, :]).then_inc(moved, 16)
                sp.wait_ge(moved, 16)
                sp.dma_start(k.ranges[:, :], k.ranges_dram.rearrange("t k -> (t k)")
                             .rearrange("(a n) -> a n", a=1)).then_inc(moved, 16)
                sp.wait_ge(moved, 32)

            @block.gpsimd
            def _(pool):
                pool.memset(k.ident[:, :], 0.0).then_inc(k.made, 1)
                pool.wait_ge(k.made, 1)
                pool.affine_select(out=k.ident[:, :], in_=k.ident[:, :], compare_op=ALU.not_equal,
                                   fill=1.0, base=0, pattern=[[-1, P]], channel_multiplier=1).then_inc(k.made, 1)
                pool.iota(k.iota[:, :], [[1, CW]], base=0, channel_multiplier=0,
                          allow_small_or_imprecise_dtypes=True)
                pool.iota(k.tile_base[:, :], [[P, TILES]], base=0, channel_multiplier=0,
                          allow_small_or_imprecise_dtypes=True)
                pool.iota(grp[:, :], [[1, GROUPS]], base=0, channel_multiplier=0,
                          allow_small_or_imprecise_dtypes=True)
                pool.iota(t_lo[:, :], [[1, 1]], base=0, channel_multiplier=P,
                          allow_small_or_imprecise_dtypes=True)
                pool.iota(t_hi[:, :], [[1, 1]], base=P - 1, channel_multiplier=P,
                          allow_small_or_imprecise_dtypes=True).then_inc(iotas, 1)

            @block.vector
            def _(dve):
                dve.memset(k.zeros[:, :], 0.0)
                dve.wait_ge(loaded, 16 * 6)
                for n in names[:2]:
                    for h in (0, 1):
                        dve.tensor_copy(val[n, h][0:size[h], :], raw[n, h][0:size[h], :]).then_inc(cast, 1)
                dve.wait_ge(cast, 4)
                for h in (0, 1):
                    v = val["dst", h][0:size[h], :]
                    dve.tensor_reduce(ext[0:size[h], 2 * h:2 * h + 1], v, AX_X, ALU.min)
                    dve.tensor_reduce(ext[0:size[h], 2 * h + 1:2 * h + 2], v, AX_X, ALU.max).then_inc(cast, 1)
                link = Chain(dve, chain)
                dve.wait_ge(iotas, 1)
                dve.wait_ge(rows_done, 1)
                link(dve.tensor_scalar(c0[:, :], pG[:, 0, 0:GROUPS], t_hi[:, :], None, ALU.is_le))
                link(dve.scalar_tensor_tensor(out=c1[:, :], in0=pG[:, 1, 0:GROUPS], scalar=t_lo[:, :],
                                              in1=c0[:, :], op0=ALU.is_ge, op1=ALU.mult))
                link(dve.scalar_tensor_tensor(out=c0[:, :], in0=grp[:, :], scalar=1.0, in1=c1[:, :],
                                              op0=ALU.add, op1=ALU.mult))
                link(dve.scalar_tensor_tensor(out=c2[:, :], in0=grp[:, :], scalar=float(GROUPS), in1=c1[:, :],
                                              op0=ALU.subtract, op1=ALU.mult))
                link(dve.tensor_reduce(lohi[:, 1:2], c0[:, :], AX_X, ALU.max))
                link(dve.tensor_reduce(lohi[:, 0:1], c2[:, :], AX_X, ALU.min))
                link(dve.tensor_scalar(lohi[:, 1:2], lohi[:, 1:2], 1.0, None, ALU.max))
                link(dve.tensor_scalar(c2[:, 0:1], lohi[:, 1:2], -1.0, None, ALU.add))
                link(dve.scalar_tensor_tensor(out=lohi[:, 0:1], in0=lohi[:, 0:1], scalar=float(GROUPS),
                                              in1=c2[:, 0:1], op0=ALU.add, op1=ALU.min))
                dve.tensor_copy(lohi_i[:, :], lohi[:, :]).then_inc(ranges, 1)
                for i, (n, h) in enumerate([(n, h) for n in names for h in (0, 1)]):
                    dve.wait_ge(turned, i + 1)
                    s = size[h]
                    dst = k.table[n][:, :].rearrange("p (g q) -> p g q", q=CPG)[:, low * h:low * h + s, :]
                    dve.tensor_copy(dst, pT[:, i, 0:CPG * s].rearrange("p (q g) -> p g q", q=CPG)).then_inc(cast, 1)
                dve.wait_ge(cast, 12)
                dve.tensor_copy(k.src_i[:, :], k.table["src"][:, :])

            @block.tensor
            def _(pe):
                pe.wait_ge(k.made, 2)
                pe.wait_ge(cast, 6)
                for h in (0, 1):
                    s = size[h]
                    for j in (0, 1):
                        ins = pe.matmul(pG[:, j, low * h:low * h + s],
                                        ext[0:s, 2 * h + j:2 * h + j + 1].broadcast_to([s, TILES]),
                                        k.ident[0:s, 0:s], start=(h == 0 and j == 0), stop=True,
                                        skip_group_check=True)
                ins.then_inc(rows_done, 1)
                for i, (n, h) in enumerate([(n, h) for n in names for h in (0, 1)]):
                    s = size[h]
                    for q in range(CPG):
                        ins = pe.transpose(pT[:, i, q * s:(q + 1) * s], val[n, h][0:s, q * P:(q + 1) * P],
                                           k.ident[0:s, 0:s])
                    ins.then_inc(turned, 1)


def build_counts(nc, a, k):
    with ExitStack() as ctx:
        m = Memory(nc, ctx, "cnt")
        rows = m.sb("rows", [P, CPG, D], F32)
        row_idx = m.sb("row_idx", [P, CPG], I32)
        src_hot = m.sb("src_hot", [P, 2, CW], BF16)
        dst_hot = m.sb("dst_hot", [P, CPG, P], BF16)
        dst_hot32 = m.sb("dst_hot32", [P, CPG, P], F32)
        msg = m.sb("msg", [P, CPG, AGG], F32)
        stage = m.sb("stage", [P, AGG], F32)
        acc = m.ps("acc", [P, 8, BANK])
        rows_free, idx_ready = m.sem("rows_free"), m.sem("idx_ready")
        rows_in = [m.sem(f"rows_in{q}") for q in range(CPG)]
        feat_in = [m.sem(f"feat_in{q}") for q in range(CPG)]
        hot_ready, msg_ready = m.sem("hot_ready"), m.sem("msg_ready")
        chunks_done = m.sem("chunks_done")
        dve_out, act_out, stored = m.sem("dve_out"), m.sem("act_out"), m.sem("stored")
        ones_set = m.sem("ones_set")

        def tile_range(eng, t):
            return (eng.value_load(k.ranges[0:1, bass.ds(t * 2, 1)], min_val=0, max_val=GROUPS - 1),
                    eng.value_load(k.ranges[0:1, bass.ds(t * 2 + 1, 1)], min_val=1, max_val=GROUPS))

        def counter(eng, name):
            r = eng.alloc_register(name)
            eng.reg_mov(r, 0)
            return r

        with nc.Block() as block:
            @block.gpsimd
            def _(pool):
                n = counter(pool, "pool_chunks")
                with pool.Fori(0, TILES) as t:
                    lo, hi = tile_range(pool, t)
                    with pool.Fori(lo, hi) as g:
                        c = pool.snap(n)
                        for q in range(CPG):
                            pool.wait_ge(rows_free, c + (q + 1))
                            pool.tensor_copy(row_idx[:, q:q + 1],
                                             k.src_i[:, bass.ds(g * CPG + q, 1)]).then_inc(idx_ready, 1)
                            pool.wait_ge(idx_ready, c + (q + 1))
                            pool.nop(nofuse=True)
                            pool.indirect_dma_start(rows[:, q, :], None, a["x"],
                                                    bass.IndirectOffsetOnAxis(ap=row_idx[:, q:q + 1], axis=0)
                                                    ).then_inc(rows_in[q], 16)
                        pool.reg_add(n, n, CPG)

            @block.sync
            def _(sp):
                n = counter(sp, "sp_chunks")
                feats = a["edge_attr"].rearrange("(c p) f -> c p f", p=P)
                with sp.Fori(0, TILES) as t:
                    lo, hi = tile_range(sp, t)
                    with sp.Fori(lo, hi) as g:
                        c = sp.snap(n)
                        for q in range(CPG):
                            sp.wait_ge(chunks_done, c + (q + 1))
                            sp.dma_start(msg[:, q, D:D + FE], feats[bass.ds(g * CPG + q, 1), :, :]
                                         .rearrange("a p f -> (a p) f")).then_inc(feat_in[q], 16)
                        sp.reg_add(n, n, CPG)
                    sp.wait_ge(act_out, t * 4 + 8)
                    sp.dma_start(k.sums_dram[bass.ds(t, 1), :, :].rearrange("a p f -> (a p) f"),
                                 stage[:, :]).then_inc(stored, 16)
                sp.wait_ge(stored, 16 * TILES)

            @block.vector
            def _(dve):
                dve.memset(msg[:, :, AGG - 1:AGG], 1.0).then_inc(ones_set, 1)
                dve.memset(k.C[:, :, CW:NP], 0.0)
                dve.sem_inc(dve_out, 4)
                n = counter(dve, "dve_chunks")
                with dve.Fori(0, TILES) as t:
                    lo, hi = tile_range(dve, t)
                    with dve.Fori(lo, hi) as g:
                        c = dve.snap(n)
                        for q in range(CPG):
                            dve.wait_ge(chunks_done, c + (q + CPG - 1))
                            dve.tensor_scalar(dst_hot[:, q, :], k.iota[:, 0:P], k.tile_base[:, bass.ds(t, 1)],
                                              k.table["dst"][:, bass.ds(g * CPG + q, 1)], ALU.add, ALU.is_equal)
                            dve.tensor_scalar(src_hot[:, q % 2, :], k.iota[:, :],
                                              k.table["src"][:, bass.ds(g * CPG + q, 1)], None,
                                              ALU.is_equal).then_inc(hot_ready, 1)
                        dve.reg_add(n, n, CPG)
                    dve.wait_ge(chunks_done, dve.snap(n) + CPG)
                    for b in range(4):
                        dve.tensor_copy(k.C[:, bass.ds(t, 1), b * CB:(b + 1) * CB].rearrange("p a n -> p (a n)"),
                                        acc[:, b, 0:CB]).then_inc(dve_out, 1)

            @block.scalar
            def _(act):
                act.sem_inc(rows_free, CPG)
                act.sem_inc(act_out, 4)
                n = counter(act, "act_chunks")
                with act.Fori(0, TILES) as t:
                    lo, hi = tile_range(act, t)
                    with act.Fori(lo, hi) as g:
                        c = act.snap(n)
                        for q in range(CPG):
                            act.wait_ge(chunks_done, c + (q + 1))
                            act.wait_ge(rows_in[q], (c + CPG) * (16 // CPG))
                            nc.scalar.activation(msg[:, q, 0:D], rows[:, q, :], ACT.Copy,
                                                 scale=k.table["w"][:, bass.ds(g * CPG + q, 1)]
                                                 ).then_inc(rows_free, 1)
                            act.wait_ge(hot_ready, c + (q + 1))
                            nc.scalar.activation(dst_hot32[:, q, :], dst_hot[:, q, :],
                                                 ACT.Copy).then_inc(msg_ready, 1)
                        act.reg_add(n, n, CPG)
                    act.wait_ge(chunks_done, act.snap(n) + CPG)
                    for b in range(4, CBANKS):
                        nc.scalar.activation(k.C[:, bass.ds(t, 1), b * CB:(b + 1) * CB].rearrange("p a n -> p (a n)"),
                                             acc[:, b, 0:CB], ACT.Copy).then_inc(act_out, 1)
                    act.wait_ge(stored, t * 16)
                    nc.scalar.activation(stage[:, :], acc[:, 7, 0:AGG], ACT.Copy).then_inc(act_out, 1)

            @block.tensor
            def _(pe):
                pe.sem_inc(chunks_done, CPG)
                n = counter(pe, "pe_chunks")
                pe.wait_ge(ones_set, 1)
                with pe.Fori(0, TILES) as t:
                    lo, hi = tile_range(pe, t)
                    pe.wait_ge(dve_out, t * 4 + 4)
                    pe.wait_ge(act_out, t * 4 + 4)
                    for b in range(8):
                        pe.matmul(acc[:, b, 0:1], k.zeros[:, 0:P], k.zeros[:, 0:1], start=True, stop=False,
                                  skip_group_check=True)
                    with pe.Fori(lo, hi) as g:
                        c = pe.snap(n)
                        for q in range(CPG):
                            pe.wait_ge(hot_ready, c + (q + 1))
                            for b in range(CBANKS):
                                pe.matmul(acc[:, b, 0:CB], dst_hot[:, q, :],
                                          src_hot[:, q % 2, b * CB:(b + 1) * CB], start=False, stop=False,
                                          skip_group_check=True)
                            pe.wait_ge(msg_ready, c + (q + 1))
                            pe.wait_ge(feat_in[q], (c + CPG) * (16 // CPG))
                            pe.matmul(acc[:, 7, 0:AGG], dst_hot32[:, q, :], msg[:, q, :], start=False, stop=False,
                                      skip_group_check=True).then_inc(chunks_done, 1)
                        pe.reg_add(n, n, CPG)



def strip_of(dram, i):
    return dram.rearrange("(s t p) f -> s p t f", t=STRIP, p=P)[bass.ds(i, 1)].rearrange("a p t f -> p (a t) f")


def flat(ap):
    return ap.rearrange("p t f -> p (t f)")


def normalize(link, act_link, dve, y, sq, st, out):
    link(dve.tensor_reduce(st[:, 0, :], y, AX_X, ALU.add))
    link(dve.tensor_scalar(st[:, 0, :], st[:, 0, :], 1.0 / D, None, ALU.mult))
    link(dve.tensor_tensor(y, y, last(st[:, 0, :], D), ALU.subtract))
    link(dve.tensor_tensor(sq, y, y, ALU.mult))
    link(dve.tensor_reduce(st[:, 1, :], sq, AX_X, ALU.add))
    act_link(dve.tensor_scalar(st[:, 1, :], st[:, 1, :], 1.0 / D, LN_EPS, ALU.mult, ALU.add))
    link(dve.reciprocal(st[:, 2, :], st[:, 2, :]))
    return dve.tensor_tensor(out, y, last(st[:, 2, :], D), ALU.mult)


NORM_LINKS = 6


def gin_nodes(nc, a, k):
    with ExitStack() as ctx:
        m = Memory(nc, ctx, "gin")
        w1, w2 = m.sb("w1", [P, D], F32), m.sb("w2", [P, D], F32)
        b1, b2 = m.sb("b1", [P, 1], F32), m.sb("b2", [P, D], F32)
        eps = m.sb("eps", [P, 1], F32)
        x, sums = m.sb("x", [P, STRIP, D], F32), m.sb("sums", [P, STRIP, AGG], F32)
        v, y, sq = (m.sb(n, [P, STRIP, D], F32) for n in ("v", "y", "sq"))
        out = m.sb("out", [P, STRIP, D], F32)
        vT, hT = m.sb("vT", [P, SW], F32), m.sb("hT", [P, SW], F32)
        eT = m.sb("eT", [FE + 1, SW], F32)
        st = m.sb("st", [P, 3, STRIP], F32)
        pV, pH, pO, pE = (m.ps(n, [P, 2 * BANK]) for n in ("pV", "pH", "pO", "pE"))
        consts, loaded, one_eps = m.sem("consts"), m.sem("loaded"), m.sem("one_eps")
        v_ready, turned, vT_ready = m.sem("v_ready"), m.sem("turned"), m.sem("vT_ready")
        h_ready, hT_ready, o_ready = m.sem("h_ready"), m.sem("hT_ready"), m.sem("o_ready")
        eT_ready, var, std = m.sem("eT_ready"), m.sem("var"), m.sem("std")
        chain, normed, stored, e_stored = m.sem("chain"), m.sem("normed"), m.sem("stored"), m.sem("e_stored")
        with nc.Block() as block:
            @block.sync
            def _(sp):
                sp.dma_start(w1[:, :], a["w1_0"]).then_inc(consts, 16)
                sp.dma_start(w2[:, :], a["w2_0"]).then_inc(consts, 16)
                with nc.allow_non_contiguous_dma(reason="one value per partition"):
                    sp.dma_start(b1[:, :], a["b1_0"].rearrange("(d a) -> d a", a=1)).then_inc(consts, 16)
                sp.dma_start(b2[:, :], a["b2_0"].partition_broadcast(P)).then_inc(consts, 16)
                sp.dma_start(eps[:, :], a["eps"].partition_broadcast(P)).then_inc(consts, 16)
                with sp.Fori(0, STRIPS) as i:
                    sp.wait_ge(normed, i)
                    sp.wait_ge(eT_ready, i)
                    sp.dma_start(x[:, :, :], strip_of(a["x"], i)).then_inc(loaded, 16)
                    sp.dma_start(sums[:, :, :], strip_of(k.sums_dram.rearrange("t p f -> (t p) f"), i)
                                 ).then_inc(loaded, 16)
                    sp.wait_ge(normed, i + 1)
                    sp.dma_start(strip_of(k.x1, i), out[:, :, :]).then_inc(stored, 16)
                    sp.wait_ge(eT_ready, i + 1)
                    sp.dma_start(k.edgeT[:, bass.ds(i * SW, SW)], eT[:, :]).then_inc(e_stored, 16)
                sp.wait_ge(stored, 16 * STRIPS)
                sp.wait_ge(e_stored, 16 * STRIPS)

            @block.vector
            def _(dve):
                links = 4 + NORM_LINKS
                dve.wait_ge(consts, 16 * 5)
                dve.tensor_scalar(eps[:, :], eps[:, :], 1.0, None, ALU.add).then_inc(one_eps, 1)
                dve.wait_ge(one_eps, 1)
                with dve.Fori(0, STRIPS) as i:
                    link = Chain(dve, chain, i * links)
                    dve.wait_ge(loaded, i * 32 + 32)
                    link(dve.tensor_scalar(sums[:, :, AGG - 1:AGG], sums[:, :, AGG - 1:AGG], 1.0, None, ALU.add))
                    dve.reciprocal(k.rdeg[:, bass.ds(i * STRIP, STRIP)],
                                   sums[:, :, AGG - 1:AGG].rearrange("p t f -> p (t f)"))
                    dve.scalar_tensor_tensor(out=v[:, :, :], in0=x[:, :, :], scalar=eps[:, :],
                                             in1=sums[:, :, 0:D], op0=ALU.mult, op1=ALU.add).then_inc(v_ready, 1)
                    dve.wait_ge(o_ready, i + 1)
                    link(dve.tensor_tensor(y[:, :, :], pO[:, 0:SW].rearrange("p (t f) -> p t f", f=D),
                                           mid(b2[:, :], STRIP), ALU.add))
                    link(dve.scalar_tensor_tensor(out=y[:, :, :], in0=y[:, :, :], scalar=0.0, in1=x[:, :, :],
                                                  op0=ALU.max, op1=ALU.add))

                    def act_link(ins):
                        ins.then_inc(var, 1)
                        dve.wait_ge(std, i + 1)
                    last_ins = normalize(link, act_link, dve, y[:, :, :], sq[:, :, :], st, v[:, :, :])
                    link(last_ins)
                    dve.wait_ge(stored, i * 16)
                    dve.tensor_copy(out[:, :, :], v[:, :, :]).then_inc(normed, 1)
                    assert link.n == links, link.n

            @block.scalar
            def _(act):
                with act.Fori(0, STRIPS) as i:
                    act.wait_ge(turned, i + 1)
                    nc.scalar.activation(vT[:, :], pV[:, 0:SW], ACT.Copy).then_inc(vT_ready, 1)
                    act.wait_ge(e_stored, i * 16)
                    nc.scalar.activation(eT[:, :], pE[0:FE + 1, 0:SW], ACT.Copy).then_inc(eT_ready, 1)
                    act.wait_ge(h_ready, i + 1)
                    nc.scalar.activation(hT[:, :], pH[:, 0:SW], ACT.Relu, bias=b1[:, :]).then_inc(hT_ready, 1)
                    act.wait_ge(var, i + 1)
                    nc.scalar.activation(st[:, 2, :], st[:, 1, :], ACT.Sqrt).then_inc(std, 1)

            @block.tensor
            def _(pe):
                pe.wait_ge(consts, 16 * 5)
                with pe.Fori(0, STRIPS) as i:
                    pe.wait_ge(v_ready, i + 1)
                    for c in range(STRIP):
                        pe.transpose(pV[:, c * P:(c + 1) * P], v[:, c, :], k.ident[:, :])
                    for c in range(STRIP):
                        ins = pe.transpose(pE[0:FE + 1, c * P:(c + 1) * P], sums[:, c, D:AGG], k.ident[:, :])
                    ins.then_inc(turned, 1)
                    pe.wait_ge(vT_ready, i + 1)
                    for lo, hi in halves(SW):
                        ins = pe.matmul(pH[:, lo:hi], w1[:, :], vT[:, lo:hi], start=True, stop=True)
                    ins.then_inc(h_ready, 1)
                    pe.wait_ge(hT_ready, i + 1)
                    for c in range(STRIP):
                        ins = pe.matmul(pO[:, c * P:(c + 1) * P], hT[:, c * P:(c + 1) * P], w2[:, :],
                                        start=True, stop=True)
                    ins.then_inc(o_ready, 1)


def split_features(nc, x_dram, parts, tag):
    with ExitStack() as ctx:
        m = Memory(nc, ctx, tag)
        x = m.sb("x", [P, STRIP, D], F32)
        loaded, high, rest, middle, low = (m.sem(n) for n in ("loaded", "high", "rest", "middle", "low"))
        with nc.Block() as block:
            @block.sync
            def _(sp):
                with sp.Fori(0, STRIPS) as i:
                    sp.wait_ge(low, i)
                    sp.dma_start(x[:, :, :], strip_of(x_dram, i)).then_inc(loaded, 16)

            @block.scalar
            def _(act):
                with act.Fori(0, STRIPS) as i:
                    act.wait_ge(loaded, i * 16 + 16)
                    nc.scalar.activation(parts[:, 0, bass.ds(i * STRIP, STRIP), :], x[:, :, :],
                                         ACT.Copy).then_inc(high, 1)
                    act.wait_ge(rest, i + 1)
                    nc.scalar.activation(parts[:, 1, bass.ds(i * STRIP, STRIP), :], x[:, :, :],
                                         ACT.Copy).then_inc(middle, 1)

            @block.vector
            def _(dve):
                with dve.Fori(0, STRIPS) as i:
                    dve.wait_ge(high, i + 1)
                    dve.tensor_tensor(x[:, :, :], x[:, :, :], parts[:, 0, bass.ds(i * STRIP, STRIP), :],
                                      ALU.subtract).then_inc(rest, 1)
                    dve.wait_ge(middle, i + 1)
                    dve.tensor_tensor(parts[:, 2, bass.ds(i * STRIP, STRIP), :], x[:, :, :],
                                      parts[:, 1, bass.ds(i * STRIP, STRIP), :], ALU.subtract).then_inc(low, 1)


def aggregate_strip(pe, pA, k, parts, i, begun):
    if not begun:
        for lo, _ in halves(SW):
            pe.matmul(pA[:, lo:lo + 1], k.zeros[:, 0:P], k.zeros[:, 0:1], start=True, stop=False,
                      skip_group_check=True)
    with pe.Fori(0, STRIPS) as s:
        for t in range(STRIP):
            for part in range(3):
                for lo, hi in halves(SW):
                    ins = pe.matmul(pA[:, lo:hi],
                                    parts[:, part, bass.ds(s * STRIP + t, 1), :].rearrange("p a f -> p (a f)"),
                                    k.C[:, bass.ds(s * STRIP + t, 1), bass.ds(i * SW + lo, hi - lo)]
                                    .rearrange("p a n -> p (a n)"),
                                    start=False, stop=False, skip_group_check=True)
    return pe.matmul(pA[:, 0:1], k.zeros[:, 0:P], k.zeros[:, 0:1], start=False, stop=True,
                     skip_group_check=True)


def mean_layer(nc, a, k):
    with ExitStack() as ctx:
        m = Memory(nc, ctx, "mean")
        parts = m.sb("parts", [P, 3, TILES, D], BF16)
        split_features(nc, k.x1, parts, "mean_split")
        w, wT = m.sb("w", [P, 2, D], F32), m.sb("wT", [P, 2, D], F32)
        b = m.sb("b", [P, 2, D], F32)
        rdeg = m.sb("rdeg", [P, TILES], F32)
        ones = m.sb("ones", [P, 1], BF16)
        x, h, y, sq = (m.sb(n, [P, STRIP, D], F32) for n in ("x", "h", "y", "sq"))
        out = m.sb("out", [P, STRIP, D], F32)
        aggT, hT = m.sb("aggT", [P, SW], F32), m.sb("hT", [P, SW], F32)
        st = m.sb("st", [P, 3, STRIP], F32)
        pA, pB, pC = (m.ps(n, [P, 2 * BANK]) for n in ("pA", "pB", "pC"))
        pW, pD = m.ps("pW", [P, BANK]), m.ps("pD", [P, BANK])
        consts, loaded, w_turned, w_ready = (m.sem(n) for n in ("consts", "loaded", "w_turned", "w_ready"))
        ones_set, deg, rdeg_ready = m.sem("ones_set"), m.sem("deg"), m.sem("rdeg_ready")
        agg, aggT_ready, p1, h_ready, turned, hT_ready, p2 = (
            m.sem(n) for n in ("agg", "aggT_ready", "p1", "h_ready", "turned", "hT_ready", "p2"))
        chain, var, std, normed, stored = (m.sem(n) for n in ("chain", "var", "std", "normed", "stored"))
        with nc.Block() as block:
            @block.sync
            def _(sp):
                for j in (0, 1):
                    sp.dma_start(w[:, j, :], a[f"w{j + 1}_1"]).then_inc(consts, 16)
                    sp.dma_start(b[:, j, :], a[f"b{j + 1}_1"].partition_broadcast(P)).then_inc(consts, 16)
                with sp.Fori(0, STRIPS) as i:
                    sp.wait_ge(normed, i)
                    sp.dma_start(x[:, :, :], strip_of(k.x1, i)).then_inc(loaded, 16)
                    sp.wait_ge(normed, i + 1)
                    sp.dma_start(strip_of(k.x2, i), out[:, :, :]).then_inc(stored, 16)
                sp.wait_ge(stored, 16 * STRIPS)

            @block.vector
            def _(dve):
                links = 2 + NORM_LINKS
                dve.memset(ones[:, :], 1.0).then_inc(ones_set, 1)
                dve.wait_ge(w_turned, 1)
                dve.tensor_copy(wT[:, :, :], pW[:, 0:2 * D].rearrange("p (j f) -> p j f", j=2)).then_inc(w_ready, 1)
                dve.wait_ge(deg, 1)
                dve.tensor_scalar(rdeg[:, :], pD[:, 0:TILES], 1.0, None, ALU.max).then_inc(rdeg_ready, 1)
                dve.wait_ge(rdeg_ready, 1)
                dve.reciprocal(rdeg[:, :], rdeg[:, :]).then_inc(rdeg_ready, 1)
                dve.wait_ge(rdeg_ready, 2)
                dve.wait_ge(consts, 16 * 4)
                with dve.Fori(0, STRIPS) as i:
                    link = Chain(dve, chain, i * links)
                    dve.wait_ge(p1, i + 1)
                    for c in range(STRIP):
                        ins = dve.scalar_tensor_tensor(out=h[:, c, :], in0=pB[:, c * D:(c + 1) * D],
                                                       scalar=rdeg[:, bass.ds(i * STRIP + c, 1)], in1=b[:, 0, :],
                                                       op0=ALU.mult, op1=ALU.add)
                    ins.then_inc(h_ready, 1)
                    dve.wait_ge(p2, i + 1)
                    dve.wait_ge(loaded, i * 16 + 16)
                    link(dve.tensor_tensor(y[:, :, :], pC[:, 0:SW].rearrange("p (t f) -> p t f", f=D),
                                           mid(b[:, 1, :], STRIP), ALU.add))
                    link(dve.tensor_tensor(y[:, :, :], y[:, :, :], x[:, :, :], ALU.add))

                    def act_link(ins):
                        ins.then_inc(var, 1)
                        dve.wait_ge(std, i + 1)
                    dve.wait_ge(stored, i * 16)
                    normalize(link, act_link, dve, y[:, :, :], sq[:, :, :], st, out[:, :, :]).then_inc(normed, 1)
                    assert link.n == links, link.n
                with dve.Fori(0, TILES) as t:
                    diag = k.C[:, bass.ds(t, 1), bass.ds(t * P, P)].rearrange("p a n -> p (a n)")
                    dve.tensor_tensor(diag, diag, k.ident[:, :], ALU.add)

            @block.scalar
            def _(act):
                with act.Fori(0, STRIPS) as i:
                    act.wait_ge(agg, i + 1)
                    nc.scalar.activation(aggT[:, :], pA[:, 0:SW], ACT.Copy).then_inc(aggT_ready, 1)
                    act.wait_ge(turned, i + 1)
                    nc.scalar.activation(hT[:, :], pB[:, 0:SW], ACT.Relu).then_inc(hT_ready, 1)
                    act.wait_ge(var, i + 1)
                    nc.scalar.activation(st[:, 2, :], st[:, 1, :], ACT.Sqrt).then_inc(std, 1)

            @block.tensor
            def _(pe):
                pe.wait_ge(consts, 16 * 4)
                for j in (0, 1):
                    ins = pe.transpose(pW[:, j * D:(j + 1) * D], w[:, j, :], k.ident[:, :])
                ins.then_inc(w_turned, 1)
                pe.wait_ge(ones_set, 1)
                pe.matmul(pD[:, 0:TILES], k.zeros[:, 0:P], k.zeros[:, 0:TILES], start=True, stop=False,
                          skip_group_check=True)
                with pe.Fori(0, TILES) as s:
                    for t in range(TILES):
                        pe.matmul(pD[:, bass.ds(s, 1)],
                                  k.C[:, t, bass.ds(s * P, P)], ones[:, :], start=False, stop=False,
                                  skip_group_check=True)
                pe.matmul(pD[:, 0:1], k.zeros[:, 0:P], k.zeros[:, 0:1], start=False, stop=True,
                          skip_group_check=True).then_inc(deg, 1)
                pe.wait_ge(w_ready, 1)
                with pe.Fori(0, STRIPS) as i:
                    aggregate_strip(pe, pA, k, parts, i, False).then_inc(agg, 1)
                    pe.wait_ge(aggT_ready, i + 1)
                    for c in range(STRIP):
                        ins = pe.matmul(pB[:, c * P:(c + 1) * P], aggT[:, c * P:(c + 1) * P], wT[:, 0, :],
                                        start=True, stop=True)
                    ins.then_inc(p1, 1)
                    pe.wait_ge(h_ready, i + 1)
                    for c in range(STRIP):
                        ins = pe.transpose(pB[:, c * P:(c + 1) * P], h[:, c, :], k.ident[:, :])
                    ins.then_inc(turned, 1)
                    pe.wait_ge(hT_ready, i + 1)
                    for c in range(STRIP):
                        ins = pe.matmul(pC[:, c * P:(c + 1) * P], hT[:, c * P:(c + 1) * P], wT[:, 1, :],
                                        start=True, stop=True)
                    ins.then_inc(p2, 1)


def gat_linear(nc, a, k, g):
    heads, hc, w_tab = g.heads, D // g.heads, D + g.heads
    with ExitStack() as ctx:
        m = Memory(nc, ctx, f"lin{g.n}")
        w = m.sb("w", [P, D], F32)
        att = m.sb("att", [P, 2, D], F32)
        x = m.sb("x", [P, STRIP, D], F32)
        xT = m.sb("xT", [P, SW], F32)
        tab = m.sb("tab", [P, STRIP, heads, hc + 1], F32)
        prod = m.sb("prod", [P, 2, STRIP, D], F32)
        pT, pX = m.ps("pT", [P, 2 * BANK]), m.ps("pX", [P, 2 * BANK])
        consts, loaded, ones_set, turned, xT_ready, xh, tab_ready, terms, stored, chain = (
            m.sem(n) for n in ("consts", "loaded", "ones_set", "turned", "xT_ready", "xh", "tab_ready", "terms",
                               "stored", "chain"))
        with nc.Block() as block:
            @block.sync
            def _(sp):
                sp.dma_start(w[:, :], a[f"w{g.n}_2"]).then_inc(consts, 16)
                for j, n in enumerate(("att_src", "att_dst")):
                    sp.dma_start(att[:, j, :], a[f"{n}{g.n}"].rearrange("h c -> (h c)").partition_broadcast(P)
                                 ).then_inc(consts, 16)
                with sp.Fori(0, STRIPS) as i:
                    sp.wait_ge(turned, i)
                    sp.dma_start(x[:, :, :], strip_of(g.x, i)).then_inc(loaded, 16)
                    sp.wait_ge(tab_ready, i + 1)
                    sp.dma_start(g.table[:, bass.ds(i * STRIP, STRIP), :],
                                 tab[:, :, :, :].rearrange("p t h c -> p t (h c)")).then_inc(stored, 16)
                sp.wait_ge(stored, 16 * STRIPS)

            @block.scalar
            def _(act):
                act.wait_ge(ones_set, 1)
                with act.Fori(0, STRIPS) as i:
                    act.wait_ge(turned, i + 1)
                    nc.scalar.activation(xT[:, :], pT[:, 0:SW], ACT.Copy).then_inc(xT_ready, 1)
                    act.wait_ge(xh, i + 1)
                    act.wait_ge(stored, i * 16)
                    for c in range(STRIP):
                        ins = nc.scalar.activation(tab[:, c, :, 0:hc], pX[:, c * D:(c + 1) * D]
                                                   .rearrange("p (h c) -> p h c", h=heads), ACT.Copy)
                    ins.then_inc(tab_ready, 1)

            @block.vector
            def _(dve):
                dve.memset(tab[:, :, :, hc:hc + 1], 1.0).then_inc(ones_set, 1)
                dve.wait_ge(consts, 16 * 3)
                with dve.Fori(0, STRIPS) as i:
                    dve.wait_ge(tab_ready, i + 1)
                    link = Chain(dve, chain, i * 3)
                    for j in (0, 1):
                        link(dve.tensor_tensor(prod[:, j, :, :], pX[:, 0:SW].rearrange("p (t f) -> p t f", f=D),
                                               mid(att[:, j, :], STRIP), ALU.mult))
                    for j in (0, 1):
                        ins = dve.tensor_reduce(g.att[:, j, bass.ds(i * STRIP * heads, STRIP * heads)],
                                                prod[:, j, :, :].rearrange("p t (h c) -> p (t h) c", h=heads),
                                                AX_X, ALU.add)
                    link(ins)
                    dve.tensor_scalar(g.att[:, 4, bass.ds(i * STRIP * heads, STRIP * heads)],
                                      g.att[:, 0, bass.ds(i * STRIP * heads, STRIP * heads)], SLOPE, None,
                                      ALU.mult).then_inc(terms, 1)

            @block.tensor
            def _(pe):
                pe.wait_ge(consts, 16 * 3)
                with pe.Fori(0, STRIPS) as i:
                    pe.wait_ge(loaded, i * 16 + 16)
                    for c in range(STRIP):
                        ins = pe.transpose(pT[:, c * P:(c + 1) * P], x[:, c, :], k.ident[:, :])
                    ins.then_inc(turned, 1)
                    pe.wait_ge(xT_ready, i + 1)
                    pe.wait_ge(tab_ready, i)
                    pe.wait_ge(terms, i)
                    for c in range(STRIP):
                        ins = pe.matmul(pX[:, c * D:(c + 1) * D], xT[:, c * P:(c + 1) * P], w[:, :],
                                        start=True, stop=True)
                    ins.then_inc(xh, 1)


def store_rows(nc, k, g, shares, tag):
    heads = g.heads
    with ExitStack() as ctx:
        m = Memory(nc, ctx, tag)
        rows = m.sb("rows", [TILES, len(shares), heads, P], F32)
        pT = m.ps("pT", [TILES, len(shares), 2 * BANK])
        turned, ready, stored = m.sem("turned"), m.sem("ready"), m.sem("stored")
        with nc.Block() as block:
            @block.tensor
            def _(pe):
                for i, (j, _) in enumerate(shares):
                    by_head = g.att[:, j, :].rearrange("p (t h) -> p h t", h=heads)
                    for h in range(heads):
                        ins = pe.transpose(pT[:, i, h * P:(h + 1) * P], by_head[:, h, :], k.ident[:, :])
                ins.then_inc(turned, 1)

            @block.scalar
            def _(act):
                act.wait_ge(turned, 1)
                for i in range(len(shares)):
                    nc.scalar.activation(rows[:, i, :, :].rearrange("t h p -> t (h p)"),
                                         pT[:, i, 0:heads * P], ACT.Copy).then_inc(ready, 1)

            @block.sync
            def _(sp):
                for i, (_, dram) in enumerate(shares):
                    sp.wait_ge(ready, i + 1)
                    sp.dma_start(dram.rearrange("h (t p) -> t h p", p=P), rows[:, i, :, :]).then_inc(stored, 16)
                sp.wait_ge(stored, 16 * len(shares))


def gat_max(nc, k, g):
    heads = g.heads
    with ExitStack() as ctx:
        m = Memory(nc, ctx, f"max{g.n}")
        row = m.sb("row", [P, NP], F32)
        far = m.sb("far", [P, 2, NP], BF16)
        best = m.sb("best", [P, TILES * heads], F32)
        z = m.sb("z", [P, 2, TILES * heads], F32)
        scratch = m.ps("scratch", [P, NP])
        bias = m.sb("bias", [P, 1], F32)
        one = m.sb("one", [P, 1], F32)
        bias_set, loaded, far_ready, far_used, kept, chain = (
            m.sem(n) for n in ("bias_set", "loaded", "far_ready", "far_used", "kept", "chain"))
        steps = heads * TILES
        with nc.Block() as block:
            @block.sync
            def _(sp):
                with sp.Fori(0, heads) as h:
                    sp.wait_ge(far_used, h * TILES)
                    sp.dma_start(row[:, :], g.src_rows[bass.ds(h, 1), :].rearrange("a n -> (a n)")
                                 .partition_broadcast(P)).then_inc(loaded, 16)

            @block.scalar
            def _(act):
                act.wait_ge(bias_set, 1)

                def mask(n, t, slot):
                    nc.scalar.activation(far[:, slot, :], k.C[:, bass.ds(t, 1), :].rearrange("p a n -> p (a n)"),
                                         ACT.Relu, bias=bias[:, :], scale=-FAR).then_inc(far_ready, 1)

                with act.Fori(0, heads) as h:
                    with act.Fori(0, TILES // 2) as u:
                        for s in (0, 1):
                            n = h * TILES + u * 2 + s
                            if s == 0:
                                act.wait_ge(far_used, n)
                            else:
                                act.wait_ge(far_used, h * TILES + u * 2)
                            mask(n, u * 2 + s, s)
                    act.wait_ge(far_used, h * TILES + (TILES - 1))
                    mask(None, TILES - 1, 0)

            @block.vector
            def _(dve):
                dve.memset(bias[:, :], FAR).then_inc(bias_set, 1)

                def greatest(n, h, t, slot):
                    dve.wait_ge(far_ready, n + 1)
                    dve.wait_ge(kept, n)
                    dve.nop(nofuse=True)
                    dve.tensor_tensor_reduce(scratch[:, :], row[:, :], far[:, slot, :], 1.0, -BIG,
                                             ALU.subtract, ALU.max, one[:, :]).then_inc(far_used, 1)
                    dve.wait_ge(far_used, n + 1)
                    dve.tensor_copy(best[:, bass.ds(t * heads + h, 1)], one[:, :]).then_inc(kept, 1)

                with dve.Fori(0, heads) as h:
                    dve.wait_ge(loaded, h * 16 + 16)
                    dve.nop(nofuse=True)
                    with dve.Fori(0, TILES // 2) as u:
                        for s in (0, 1):
                            greatest(h * TILES + u * 2 + s, h, u * 2 + s, s)
                    greatest(h * TILES + (TILES - 1), h, TILES - 1, 0)
                dve.wait_ge(kept, steps)
                link = Chain(dve, chain)
                link(dve.tensor_tensor(z[:, 0, :], best[:, :], g.att[:, 1, :], ALU.add))
                link(dve.scalar_tensor_tensor(out=z[:, 1, :], in0=z[:, 0, :], scalar=SLOPE, in1=z[:, 0, :],
                                              op0=ALU.mult, op1=ALU.max))
                dve.tensor_tensor(g.att[:, 2, :], g.att[:, 1, :], z[:, 1, :], ALU.subtract)
                dve.scalar_tensor_tensor(out=g.att[:, 3, :], in0=g.att[:, 1, :], scalar=SLOPE, in1=z[:, 1, :],
                                         op0=ALU.mult, op1=ALU.subtract)


def turn_counts(nc, k, tag):
    with ExitStack() as ctx:
        m = Memory(nc, ctx, tag)
        pI = m.ps("pI", [P, STRIP, 2 * BANK], BF16)
        identb = m.sb("identb", [P, P], BF16)
        made, turned, upper, lower = m.sem("made"), m.sem("turned"), m.sem("upper"), m.sem("lower")
        d_turned, d_put = m.sem("d_turned"), m.sem("d_put")

        def block_of(r, c):
            return k.C[:, bass.ds(r, 1), bass.ds(c * P, P)].rearrange("p a n -> p (a n)")

        pairs = [(x, y) for y in range(1, STRIPS) for x in range(y)]
        with nc.Block() as block:
            @block.vector
            def _(dve):
                dve.tensor_copy(identb[:, :], k.ident[:, :]).then_inc(made, 1)
                for n, (x, y) in enumerate(pairs):
                    with dve.Fori(0, STRIP) as r:
                        dve.wait_ge(turned, r + (n * STRIP + 1))
                        dve.tensor_copy(k.C[:, y * STRIP:(y + 1) * STRIP, bass.ds((r + x * STRIP) * P, P)],
                                        pI[:, 0, 0:SW].rearrange("p (c n) -> p c n", n=P)).then_inc(upper, 1)
                with dve.Fori(0, STRIPS) as x:
                    dve.wait_ge(d_turned, x + 1)
                    for r in range(STRIP):
                        ins = dve.tensor_copy(k.C[:, bass.ds(x * STRIP + r, 1), bass.ds(x * SW, SW)]
                                              .rearrange("p a n -> p (a n)"), pI[:, r, 0:SW])
                    ins.then_inc(d_put, 1)

            @block.scalar
            def _(act):
                for n, (x, y) in enumerate(pairs):
                    with act.Fori(0, STRIP) as r:
                        act.wait_ge(turned, r + (n * STRIP + 1))
                        nc.scalar.activation(k.C[:, bass.ds(r + x * STRIP, 1), y * SW:(y + 1) * SW]
                                             .rearrange("p a n -> p (a n)"), pI[:, 1, 0:SW],
                                             ACT.Copy).then_inc(lower, 1)

            @block.tensor
            def _(pe):
                pe.wait_ge(made, 1)
                for n, (x, y) in enumerate(pairs):
                    with pe.Fori(0, STRIP) as r:
                        pe.wait_ge(upper, r + n * STRIP)
                        pe.wait_ge(lower, r + n * STRIP)
                        for c in range(STRIP):
                            pe.transpose(pI[:, 0, c * P:(c + 1) * P], block_of(r + x * STRIP, y * STRIP + c),
                                         identb[:, :])
                        for c in range(STRIP):
                            ins = pe.transpose(pI[:, 1, c * P:(c + 1) * P], block_of(y * STRIP + c, r + x * STRIP),
                                               identb[:, :])
                        ins.then_inc(turned, 1)
                pe.wait_ge(upper, len(pairs) * STRIP)
                pe.wait_ge(lower, len(pairs) * STRIP)
                with pe.Fori(0, STRIPS) as x:
                    pe.wait_ge(d_put, x)
                    for r in range(STRIP):
                        for c in range(STRIP):
                            ins = pe.transpose(pI[:, r, c * P:(c + 1) * P],
                                               block_of(x * STRIP + c, x * STRIP + r), identb[:, :])
                    ins.then_inc(d_turned, 1)


def gat_sums(nc, k, g, sums):
    heads, w1 = g.heads, D // g.heads + 1
    per_bank = min(STRIP, BANK // w1)
    with ExitStack() as ctx:
        m = Memory(nc, ctx, f"sum{g.n}")
        tab = m.sb("tab", [P, TILES, heads * w1], F32)
        shares = m.sb("shares", [P, 2, 2, SW], F32)
        e = m.sb("e", [P, 2, 2, SW], F32)
        acc = m.ps("acc", [P, 2, 2 * BANK])
        tab_in = m.sem("tab_in")
        shares_in = [[m.sem(f"shares_in{s}{x}") for x in (0, 1)] for s in (0, 1)]
        exps, larger, weights, steps_done, acc_ready, acc_out = (
            m.sem(n) for n in ("exps", "larger", "weights", "steps_done", "acc_ready", "acc_out"))

        def acc_tile(slot, c):
            at = (c // per_bank) * BANK + (c % per_bank) * w1
            return acc[:, slot, at:at + w1]

        def each_step(eng, fn, h, j):
            first = h * (STRIPS * TILES) + j * TILES
            with eng.Fori(0, TILES // 2) as u:
                fn(first + u * 2, u * 2, 0, first + u * 2)
                fn(first + u * 2 + 1, u * 2 + 1, 1, first + u * 2)
            fn(first + (TILES - 1), TILES - 1, 0, first + (TILES - 2))

        def loads(h, j):
            return (h * (3 - j % 2) + (j // 2 + 1)) * 16

        with nc.Block() as block:
            @block.sync
            def _(sp):
                sp.dma_start(tab[:, :, :], g.table).then_inc(tab_in, 16)
                with sp.Fori(0, heads) as h:
                    for j in range(STRIPS):
                        n = h * (STRIPS * TILES) + max(0, j - 1) * TILES
                        sp.wait_ge(exps, n)
                        for x in (0, 1):
                            row = g.dst_rows[x][bass.ds(h, 1), j * SW:(j + 1) * SW].rearrange("a n -> (a n)")
                            sp.dma_start(shares[:, j % 2, x, :], row.partition_broadcast(P)
                                         ).then_inc(shares_in[j % 2][x], 16)

            @block.scalar
            def _(act):
                with act.Fori(0, heads) as h:
                    for j in range(STRIPS):
                        for x in (0, 1):
                            act.wait_ge(shares_in[j % 2][x], loads(h, j))

                        def step(n, s, slot, free):
                            act.wait_ge(steps_done, free)
                            act.nop(nofuse=True)
                            for x, term in ((0, 0), (1, 4)):
                                ins = nc.scalar.activation(e[:, slot, x, :], shares[:, j % 2, x, :], ACT.Exp,
                                                           bias=g.att[:, term, bass.ds(s * heads + h, 1)])
                            ins.then_inc(exps, 1)
                        each_step(act, step, h, j)
                        act.wait_ge(acc_ready, h * STRIPS + (j + 1))
                        for c in range(0, STRIP, per_bank):
                            c1 = min(STRIP, c + per_bank)
                            at = c // per_bank * BANK
                            ins = nc.scalar.activation(
                                sums[:, j * STRIP + c:j * STRIP + c1, bass.ds(h * w1, w1)],
                                acc[:, j % 2, at:at + (c1 - c) * w1].rearrange("p (t c) -> p t c", c=w1), ACT.Copy)
                        ins.then_inc(acc_out, 1)

            @block.vector
            def _(dve):
                with dve.Fori(0, heads) as h:
                    for j in range(STRIPS):
                        def step(n, s, slot, free):
                            dve.wait_ge(exps, n + 1)
                            dve.tensor_tensor(e[:, slot, 0, :], e[:, slot, 0, :], e[:, slot, 1, :],
                                              ALU.max).then_inc(larger, 1)
                            dve.wait_ge(larger, n + 1)
                            dve.scalar_tensor_tensor(
                                out=e[:, slot, 0, :], in0=e[:, slot, 0, :], scalar=BIG,
                                in1=k.C[:, bass.ds(s, 1), j * SW:(j + 1) * SW].rearrange("p a n -> p (a n)"),
                                op0=ALU.min, op1=ALU.mult).then_inc(weights, 1)
                        each_step(dve, step, h, j)

            @block.tensor
            def _(pe):
                pe.wait_ge(tab_in, 16)
                with pe.Fori(0, heads) as h:
                    for j in range(STRIPS):
                        pe.wait_ge(acc_out, h * STRIPS + max(0, j - 1))
                        for x in range(-(-STRIP // per_bank)):
                            pe.matmul(acc[:, j % 2, x * BANK:x * BANK + 1], k.zeros[:, :], k.zeros[:, 0:1],
                                      start=True, stop=False, skip_group_check=True)

                        def step(n, s, slot, free):
                            pe.wait_ge(weights, n + 1)
                            for c in range(STRIP):
                                ins = pe.matmul(acc_tile(j % 2, c), e[:, slot, 0, c * P:(c + 1) * P],
                                                tab[:, bass.ds(s, 1), bass.ds(h * w1, w1)].rearrange("p a c -> p (a c)"),
                                                start=False, stop=False, skip_group_check=True)
                            ins.then_inc(steps_done, 1)
                        each_step(pe, step, h, j)
                        pe.matmul(acc[:, j % 2, 0:1], k.zeros[:, :], k.zeros[:, 0:1], start=False, stop=True,
                                  skip_group_check=True).then_inc(acc_ready, 1)


def gat_nodes(nc, a, k, g, sums):
    heads, hc = g.heads, D // g.heads
    with ExitStack() as ctx:
        m = Memory(nc, ctx, f"post{g.n}")
        b = m.sb("b", [P, D], F32)
        x, y, sq, out = (m.sb(n, [P, STRIP, D], F32) for n in ("x", "y", "sq", "out"))
        st = m.sb("st", [P, 3, STRIP], F32)
        rw = m.sb("rw", [P, STRIP * heads], F32)
        consts, loaded, chain, to_act, from_act, normed, stored = (
            m.sem(n) for n in ("consts", "loaded", "chain", "to_act", "from_act", "normed", "stored"))
        first = g.n == 1
        with nc.Block() as block:
            @block.sync
            def _(sp):
                sp.dma_start(b[:, :], a[f"b{g.n}_2"].partition_broadcast(P)).then_inc(consts, 16)
                with sp.Fori(0, STRIPS) as i:
                    sp.wait_ge(normed, i)
                    sp.dma_start(x[:, :, :], strip_of(k.x2, i)).then_inc(loaded, 16)
                    sp.wait_ge(normed, i + 1)
                    sp.dma_start(strip_of(g.out, i), out[:, :, :]).then_inc(stored, 16)
                sp.wait_ge(stored, 16 * STRIPS)

            @block.scalar
            def _(act):
                with act.Fori(0, STRIPS) as i:
                    act.wait_ge(to_act, i + 1)
                    if first:
                        nc.scalar.activation(sq[:, :, :], sq[:, :, :], ACT.Exp).then_inc(from_act, 1)
                    else:
                        nc.scalar.activation(st[:, 2, :], st[:, 1, :], ACT.Sqrt).then_inc(from_act, 1)

            @block.vector
            def _(dve):
                links = 3 + 1 if first else 4 + NORM_LINKS
                dve.wait_ge(consts, 16)
                with dve.Fori(0, STRIPS) as i:
                    link = Chain(dve, chain, i * links)
                    s4 = sums[:, bass.ds(i * STRIP, STRIP), :].rearrange("p t (h c) -> p (t h) c", h=heads)
                    link(dve.reciprocal(rw[:, :], s4[:, :, hc:hc + 1].rearrange("p h c -> p (h c)")))
                    link(dve.tensor_tensor(y[:, :, :].rearrange("p t (h c) -> p (t h) c", h=heads),
                                           s4[:, :, 0:hc], last(rw[:, :], hc), ALU.mult))
                    link(dve.tensor_tensor(y[:, :, :], y[:, :, :], mid(b[:, :], STRIP), ALU.add))
                    dve.wait_ge(loaded, i * 16 + 16)

                    def act_link(ins):
                        ins.then_inc(to_act, 1)
                        dve.wait_ge(from_act, i + 1)
                    if first:
                        act_link(dve.tensor_scalar(sq[:, :, :], y[:, :, :], 0.0, None, ALU.min))
                        link(dve.scalar_tensor_tensor(out=y[:, :, :], in0=y[:, :, :], scalar=0.0,
                                                      in1=sq[:, :, :], op0=ALU.max, op1=ALU.add))
                        dve.wait_ge(stored, i * 16)
                        dve.tensor_scalar(out[:, :, :], y[:, :, :], -1.0, None, ALU.add).then_inc(normed, 1)
                    else:
                        link(dve.tensor_tensor(y[:, :, :], y[:, :, :], x[:, :, :], ALU.add))
                        dve.wait_ge(stored, i * 16)
                        normalize(link, act_link, dve, y[:, :, :], sq[:, :, :], st, out[:, :, :]).then_inc(normed, 1)
                    assert link.n == links, link.n


def sage_layers(nc, a, k, out_dram):
    with ExitStack() as ctx:
        m = Memory(nc, ctx, "sage")
        parts = m.sb("parts", [P, 2, 3, TILES, D], BF16)
        split_features(nc, k.x3, parts[:, 0], "sage_split")
        ew = m.sb("ew", [P, 2, FE], F32)
        ewT = m.sb("ewT", [FE + 1, 2, D], F32)
        w, b = m.sb("w", [P, 2, D], F32), m.sb("b", [P, 2, D], F32)
        edges = m.sb("edges", [FE + 1, SW], F32)
        aggT = m.sb("aggT", [P, SW], F32)
        y = m.sb("y", [P, STRIP, D], F32)
        st = m.sb("st", [P, 3, STRIP], F32)
        spare = parts[:, 1].rearrange("p s t f -> p (s t f)").bitcast(F32)
        x, sq, out = (spare[:, n * SW:(n + 1) * SW].rearrange("p (t f) -> p t f", f=D) for n in range(3))
        pA = m.ps("pA", [P, 2, 2 * BANK])
        pO = m.ps("pO", [P, 2 * BANK])
        pW = m.ps("pW", [FE, D])
        loaded, ew_turned, ew_ready, edges_in = (m.sem(n) for n in ("loaded", "ew_turned", "ew_ready", "edges_in"))
        agg, aggT_ready, lin, y_ready = (m.sem(n) for n in ("agg", "aggT_ready", "lin", "y_ready"))
        high, rest, middle, low = (m.sem(n) for n in ("high", "rest", "middle", "low"))
        x_in, chain, var, std, normed, stored = (
            m.sem(n) for n in ("x_in", "chain", "var", "std", "normed", "stored"))

        def layers(eng, fn):
            with eng.Fori(0, LAYERS // 2) as u:
                fn(u * 2, 0, False)
                fn(u * 2 + 1, 1, False)
            fn(LAYERS - 1, 0, True)

        with nc.Block() as block:
            @block.sync
            def _(sp):
                def one(l, par, is_last):
                    at = bass.ds(l, 1)
                    sp.dma_start(w[:, par, :], a["Ws"][at].rearrange("a f d -> (a f) d")).then_inc(loaded, 16)
                    sp.dma_start(ew[:, par, :], a["ews"][at].rearrange("a d f -> (a d) f")).then_inc(loaded, 16)
                    sp.dma_start(b[:, par, :], a["bs"][at].rearrange("a d -> (a d)").partition_broadcast(P)
                                 ).then_inc(loaded, 16)
                    sp.dma_start(ewT[FE:FE + 1, par, :], a["ebs"][at]).then_inc(loaded, 16)
                    for i in range(STRIPS):
                        sp.wait_ge(agg, l * STRIPS + i)
                        sp.dma_start(edges[:, :], k.edgeT[:, i * SW:(i + 1) * SW]).then_inc(edges_in, 16)
                        if is_last:
                            sp.wait_ge(normed, i)
                            sp.dma_start(x, strip_of(k.x3, i)).then_inc(x_in, 16)
                            if i:
                                sp.dma_start(strip_of(out_dram, i - 1), out).then_inc(stored, 16)
                layers(sp, one)
                sp.wait_ge(normed, STRIPS)
                sp.dma_start(strip_of(out_dram, STRIPS - 1), out).then_inc(stored, 16)
                sp.wait_ge(stored, 16 * STRIPS)

            @block.tensor
            def _(pe):
                def linear(l, par, i):
                    it = l * STRIPS + i
                    pe.wait_ge(aggT_ready, it + 1)
                    pe.wait_ge(y_ready, it)
                    for c in range(STRIP):
                        ins = pe.matmul(pO[:, c * P:(c + 1) * P], aggT[:, c * P:(c + 1) * P], w[:, par, :],
                                        start=True, stop=True)
                    ins.then_inc(lin, 1)

                def one(l, par, is_last):
                    pe.wait_ge(loaded, l * 64 + 64)
                    pe.transpose(pW[:, :], ew[:, par, :], k.ident[:, :]).then_inc(ew_turned, 1)
                    pe.wait_ge(ew_ready, l + 1)
                    pe.wait_ge(low, l * STRIPS)
                    for i in range(STRIPS):
                        pe.wait_ge(aggT_ready, l * STRIPS + max(0, i - 1))
                        pe.wait_ge(edges_in, (l * STRIPS + i) * 16 + 16)
                        for lo, hi in halves(SW):
                            pe.matmul(pA[:, i % 2, lo:hi], ewT[:, par, :], edges[:, lo:hi], start=True, stop=False,
                                      skip_group_check=True)
                        aggregate_strip(pe, pA[:, i % 2], k, parts[:, par], i, True).then_inc(agg, 1)
                        if i:
                            linear(l, par, i - 1)
                    linear(l, par, STRIPS - 1)
                layers(pe, one)

            @block.scalar
            def _(act):
                def one(l, par, is_last):
                    def split(i):
                        it = l * STRIPS + i
                        if is_last:
                            act.wait_ge(var, i + 1)
                            nc.scalar.activation(st[:, 2, :], st[:, 1, :], ACT.Sqrt).then_inc(std, 1)
                            return
                        act.wait_ge(y_ready, it + 1)
                        nc.scalar.activation(parts[:, 1 - par, 0, i * STRIP:(i + 1) * STRIP, :], y[:, :, :],
                                             ACT.Relu).then_inc(high, 1)
                        act.wait_ge(rest, it + 1)
                        nc.scalar.activation(parts[:, 1 - par, 1, i * STRIP:(i + 1) * STRIP, :], y[:, :, :],
                                             ACT.Copy).then_inc(middle, 1)

                    for i in range(STRIPS):
                        it = l * STRIPS + i
                        act.wait_ge(agg, it + 1)
                        act.wait_ge(lin, it)
                        nc.scalar.activation(aggT[:, :], pA[:, i % 2, 0:SW], ACT.Copy).then_inc(aggT_ready, 1)
                        if i:
                            split(i - 1)
                    split(STRIPS - 1)
                layers(act, one)

            @block.vector
            def _(dve):
                links = 1 + NORM_LINKS

                def one(l, par, is_last):
                    dve.wait_ge(ew_turned, l + 1)
                    dve.tensor_copy(ewT[0:FE, par, :], pW[:, :]).then_inc(ew_ready, 1)
                    for i in range(STRIPS):
                        it = l * STRIPS + i
                        dve.wait_ge(lin, it + 1)
                        dve.wait_ge(low, l * STRIPS if is_last else it)
                        if is_last:
                            dve.wait_ge(normed, i)
                        for c in range(STRIP):
                            ins = dve.scalar_tensor_tensor(
                                out=y[:, c, :], in0=pO[:, c * D:(c + 1) * D],
                                scalar=k.rdeg[:, i * STRIP + c:i * STRIP + c + 1], in1=b[:, par, :],
                                op0=ALU.mult, op1=ALU.add)
                        ins.then_inc(y_ready, 1)
                        if is_last:
                            link = Chain(dve, chain, i * links)
                            dve.wait_ge(y_ready, it + 1)
                            dve.wait_ge(x_in, i * 16 + 16)
                            link(dve.tensor_tensor(y[:, :, :], y[:, :, :], x, ALU.add))

                            def act_link(ins):
                                ins.then_inc(var, 1)
                                dve.wait_ge(std, i + 1)
                            if i:
                                dve.wait_ge(stored, i * 16)
                            normalize(link, act_link, dve, y[:, :, :], sq, st, out).then_inc(normed, 1)
                            assert link.n == links, link.n
                            continue
                        dve.wait_ge(high, it + 1)
                        dve.scalar_tensor_tensor(out=y[:, :, :], in0=y[:, :, :], scalar=0.0,
                                                 in1=parts[:, 1 - par, 0, i * STRIP:(i + 1) * STRIP, :],
                                                 op0=ALU.max, op1=ALU.subtract).then_inc(rest, 1)
                        dve.wait_ge(middle, it + 1)
                        dve.tensor_tensor(parts[:, 1 - par, 2, i * STRIP:(i + 1) * STRIP, :], y[:, :, :],
                                          parts[:, 1 - par, 1, i * STRIP:(i + 1) * STRIP, :],
                                          ALU.subtract).then_inc(low, 1)
                layers(dve, one)


def attention_layer(nc, a, k, n, heads, x_dram, out_dram):
    class G:
        pass

    g = G()
    g.n, g.heads, g.x, g.out = n, heads, x_dram, out_dram
    g.table = nc.dram_tensor(f"table{n}", [P, TILES, D + heads], F32).ap()
    g.src_rows = nc.dram_tensor(f"src_rows{n}", [heads, NP], F32).ap()
    g.dst_rows = [nc.dram_tensor(f"dst_rows{n}{x}", [heads, NP], F32).ap() for x in (0, 1)]
    with ExitStack() as ctx:
        m = Memory(nc, ctx, f"att{n}")
        g.att = m.sb("att", [P, 5, TILES * heads], F32)
        gat_linear(nc, a, k, g)
        store_rows(nc, k, g, [(0, g.src_rows)], f"srows{n}")
        gat_max(nc, k, g)
        store_rows(nc, k, g, [(2, g.dst_rows[0]), (3, g.dst_rows[1])], f"drows{n}")
        turn_counts(nc, k, f"turn{n}")
        sums = m.sb("sums", [P, TILES, D + heads], F32)
        gat_sums(nc, k, g, sums)
        gat_nodes(nc, a, k, g, sums)


def program(nc, a, out):
    class K:
        pass

    k = K()
    with ExitStack() as ctx:
        m = Memory(nc, ctx, "k")
        k.ranges_dram = nc.dram_tensor("ranges_dram", [TILES, 2], I32).ap()
        k.sums_dram = nc.dram_tensor("sums_dram", [TILES, P, AGG], F32).ap()
        k.edgeT = nc.dram_tensor("edgeT", [FE + 1, NP], F32).ap()
        k.x1, k.x2, k.h, k.x3 = (nc.dram_tensor(n, [NP, D], F32).ap() for n in ("x1", "x2", "h", "x3"))
        k.ident = m.sb("ident", [P, P], F32)
        k.zeros = m.sb("zeros", [P, P], BF16)
        k.rdeg = m.sb("rdeg", [P, TILES], F32)
        k.made = m.sem("made")
        k.C = m.sb("C", [P, TILES, NP], BF16)
        with ExitStack() as edge:
            me = Memory(nc, edge, "e")
            k.iota = me.sb("iota", [P, CW], I16)
            k.tile_base = me.sb("tile_base", [P, TILES], F32)
            k.table = {n: me.sb(f"table_{n}", [P, CHUNKS], F32) for n in ("src", "dst", "w")}
            k.src_i = me.sb("src_i", [P, CHUNKS], I32)
            k.ranges = me.sb("ranges", [1, 2 * TILES], I32)
            edge_tables(nc, a, k)
            build_counts(nc, a, k)
        gin_nodes(nc, a, k)
        mean_layer(nc, a, k)
        attention_layer(nc, a, k, 1, HEADS, k.x2, k.h)
        turn_counts(nc, k, "turn_back")
        attention_layer(nc, a, k, 2, 1, k.h, k.x3)
        sage_layers(nc, a, k, out)


def kernel(x, src, dst, edge_attr_16, edge_weight, L0_gnn_W1, L0_gnn_b1, L0_gnn_W2, L0_gnn_b2, L0_gnn_eps,
           L1_gnn_W1, L1_gnn_b1, L1_gnn_W2, L1_gnn_b2, L2_gnn_W1, L2_gnn_att_src1, L2_gnn_att_dst1, L2_gnn_b1,
           L2_gnn_W2, L2_gnn_att_src2, L2_gnn_att_dst2, L2_gnn_b2, L3_gnn_Ws, L3_gnn_bs, L3_gnn_ews, L3_gnn_ebs):
    import numpy as np
    from concourse import bacc
    from concourse.bass_utils import run_bass_kernel_spmd

    def padded(v, n, fill=0):
        v = np.asarray(v)
        return np.concatenate([v, np.full((n - v.shape[0],) + v.shape[1:], fill, v.dtype)])

    arrays = {
        "x": padded(x, NP),
        "src": padded(src, E_PAD),
        "dst": padded(dst, E_PAD, NO_NODE),
        "w": padded(edge_weight, E_PAD),
        "edge_attr": padded(edge_attr_16, E_PAD),
        "w1_0": L0_gnn_W1, "b1_0": L0_gnn_b1, "w2_0": L0_gnn_W2, "b2_0": L0_gnn_b2, "eps": L0_gnn_eps,
        "w1_1": L1_gnn_W1, "b1_1": L1_gnn_b1, "w2_1": L1_gnn_W2, "b2_1": L1_gnn_b2,
        "w1_2": L2_gnn_W1, "b1_2": L2_gnn_b1, "att_src1": L2_gnn_att_src1, "att_dst1": L2_gnn_att_dst1,
        "w2_2": L2_gnn_W2, "b2_2": L2_gnn_b2, "att_src2": L2_gnn_att_src2, "att_dst2": L2_gnn_att_dst2,
        "Ws": L3_gnn_Ws, "bs": L3_gnn_bs, "ews": L3_gnn_ews, "ebs": L3_gnn_ebs,
    }
    arrays = {n: np.ascontiguousarray(v) for n, v in arrays.items()}
    nc = bacc.Bacc("TRN2", target_bir_lowering=False, num_devices=1)
    a = {n: nc.dram_tensor(f"in_{n}", v.shape, mybir.dt.from_np(v.dtype), kind="ExternalInput").ap()
         for n, v in arrays.items()}
    out = nc.dram_tensor("out", [NP, D], F32, kind="ExternalOutput").ap()
    program(nc, a, out)
    r = run_bass_kernel_spmd(nc, [{f"in_{n}": v for n, v in arrays.items()}], core_ids=[0])
    return r.results[0]["out"][:N_NODES]
```

```python
from contextlib import ExitStack, contextmanager

import concourse.bass as bass
from concourse import mybir

F32 = mybir.dt.float32
BF16 = mybir.dt.bfloat16
I16 = mybir.dt.int16
I32 = mybir.dt.int32
ALU = mybir.AluOpType
ACT = mybir.ActivationFunctionType
AX_X = mybir.AxisListType.X

P = 128
N_NODES = 3125
N_EDGES = 103125
D = 128
FE = 16
TILES = -(-N_NODES // P)
NP = TILES * P
STRIP = 5
STRIPS = TILES // STRIP
SW = STRIP * P
BANK = 512
CPG = 4
GROUPS = -(-N_EDGES // (CPG * P))
CHUNKS = GROUPS * CPG
E_PAD = CHUNKS * P
NO_NODE = 4095
CB = 448
CBANKS = 7
CW = CB * CBANKS
AGG = D + FE + 1
HEADS = 8
HC = D // HEADS
LAYERS = 5
LN_EPS = 1e-5
SLOPE = 0.2
FAR = 1.0e30
BIG = 3.0e38
SPREAD = 60.0
HALVES = ((0, 4), (4, CBANKS))
V_PARTS = ((0, 7), (7, 13), (13, 19), (19, 25))


assert CW >= N_NODES and TILES % STRIP == 0 and 2 * P >= GROUPS > P


class Memory:

    def __init__(self, nc, ctx, phase):
        self.nc, self.ctx, self.phase, self.sems = nc, ctx, phase, []
        ctx.push(self.free_sems)

    def sb(self, name, shape, dtype):
        return self.ctx.enter_context(self.nc.sbuf_tensor(f"{self.phase}_{name}", shape, dtype))

    def ps(self, name, shape, dtype=F32):
        return self.ctx.enter_context(self.nc.psum_tensor(f"{self.phase}_{name}", shape, dtype))

    def sem(self, name):
        self.sems.append(self.nc.alloc_semaphore(f"{self.phase}_{name}"))
        return self.sems[-1]

    def free_sems(self, error, *_):
        if self.sems and not error:
            self.nc.clear_and_free_semaphores(self.sems)
            with self.nc.Block():
                pass


class Chain:

    def __init__(self, eng, sem, before=0):
        self.eng, self.sem, self.n, self.before = eng, sem, 0, before

    def __call__(self, ins):
        self.n += 1
        ins.then_inc(self.sem, 1)
        self.eng.wait_ge(self.sem, self.before + self.n)


@contextmanager
def on_path(eng, k, wide):
    if wide is None:
        yield
        return
    spread = eng.value_load(k.wide[0:1, 0:1], min_val=0, max_val=1)
    with eng.If(spread > 0 if wide else spread < 1):
        yield


def mid(row, n):
    p, w = row.shape
    return row.unsqueeze(1).broadcast_to([p, n, w])


def last(cols, n):
    p, k = cols.shape
    return cols.unsqueeze(2).broadcast_to([p, k, n])


def halves(w):
    return [(0, BANK), (BANK, w)]


def edge_tables(nc, a, k):
    with ExitStack() as ctx:
        m = Memory(nc, ctx, "tab")
        names = ("src", "dst", "w")
        low = P
        high = GROUPS - P
        raw = {(n, h): m.sb(f"raw_{n}{h}", [P, CPG * P], F32 if n == "w" else I32)
               for n in names for h in (0, 1)}
        val = {(n, h): m.sb(f"val_{n}{h}", [P, CPG * P], F32) for n in names[:2] for h in (0, 1)}
        val.update({("w", h): raw["w", h] for h in (0, 1)})
        ext = m.sb("ext", [P, 4], F32)
        grp = m.sb("grp", [TILES, GROUPS], F32)
        t_lo = m.sb("t_lo", [TILES, 1], F32)
        t_hi = m.sb("t_hi", [TILES, 1], F32)
        c0 = m.sb("c0", [TILES, GROUPS], F32)
        c1 = m.sb("c1", [TILES, GROUPS], F32)
        c2 = m.sb("c2", [TILES, GROUPS], F32)
        lohi = m.sb("lohi", [TILES, 2], F32)
        lohi_i = m.sb("lohi_i", [TILES, 2], I32)
        pT = m.ps("pT", [P, 6, BANK])
        pG = m.ps("pG", [TILES, 2, 256])
        loaded, iotas, cast = m.sem("loaded"), m.sem("iotas"), m.sem("cast")
        turned, rows_done = m.sem("turned"), m.sem("rows_done")
        chain, ranges, moved = m.sem("chain"), m.sem("ranges"), m.sem("moved")
        size = [low, high]
        with nc.Block() as block:
            @block.sync
            def _(sp):
                for n in names:
                    rows = a[n].rearrange("(g e) -> g e", e=CPG * P)
                    sp.dma_start(raw[n, 0][:, :], rows[0:low]).then_inc(loaded, 16)
                    sp.dma_start(raw[n, 1][0:high, :], rows[low:GROUPS]).then_inc(loaded, 16)
                sp.wait_ge(ranges, 1)
                sp.dma_start(k.ranges_dram, lohi_i[:, :]).then_inc(moved, 16)
                sp.wait_ge(moved, 16)
                sp.dma_start(k.ranges[:, :], k.ranges_dram.rearrange("t k -> (t k)")
                             .rearrange("(a n) -> a n", a=1)).then_inc(moved, 16)
                sp.wait_ge(moved, 32)

            @block.gpsimd
            def _(pool):
                pool.memset(k.ident[:, :], 0.0).then_inc(k.made, 1)
                pool.wait_ge(k.made, 1)
                pool.affine_select(out=k.ident[:, :], in_=k.ident[:, :], compare_op=ALU.not_equal,
                                   fill=1.0, base=0, pattern=[[-1, P]], channel_multiplier=1).then_inc(k.made, 1)
                pool.iota(k.iota[:, :], [[1, CW]], base=0, channel_multiplier=0,
                          allow_small_or_imprecise_dtypes=True)
                pool.iota(k.tile_base[:, :], [[P, TILES]], base=0, channel_multiplier=0,
                          allow_small_or_imprecise_dtypes=True)
                pool.iota(grp[:, :], [[1, GROUPS]], base=0, channel_multiplier=0,
                          allow_small_or_imprecise_dtypes=True)
                pool.iota(t_lo[:, :], [[1, 1]], base=0, channel_multiplier=P,
                          allow_small_or_imprecise_dtypes=True)
                pool.iota(t_hi[:, :], [[1, 1]], base=P - 1, channel_multiplier=P,
                          allow_small_or_imprecise_dtypes=True).then_inc(iotas, 1)

            @block.vector
            def _(dve):
                dve.memset(k.zeros[:, :], 0.0)
                dve.wait_ge(loaded, 16 * 6)
                for n in names[:2]:
                    for h in (0, 1):
                        dve.tensor_copy(val[n, h][0:size[h], :], raw[n, h][0:size[h], :]).then_inc(cast, 1)
                dve.wait_ge(cast, 4)
                for h in (0, 1):
                    v = val["dst", h][0:size[h], :]
                    dve.tensor_reduce(ext[0:size[h], 2 * h:2 * h + 1], v, AX_X, ALU.min)
                    dve.tensor_reduce(ext[0:size[h], 2 * h + 1:2 * h + 2], v, AX_X, ALU.max).then_inc(cast, 1)
                link = Chain(dve, chain)
                dve.wait_ge(iotas, 1)
                dve.wait_ge(rows_done, 1)
                link(dve.tensor_scalar(c0[:, :], pG[:, 0, 0:GROUPS], t_hi[:, :], None, ALU.is_le))
                link(dve.scalar_tensor_tensor(out=c1[:, :], in0=pG[:, 1, 0:GROUPS], scalar=t_lo[:, :],
                                              in1=c0[:, :], op0=ALU.is_ge, op1=ALU.mult))
                link(dve.scalar_tensor_tensor(out=c0[:, :], in0=grp[:, :], scalar=1.0, in1=c1[:, :],
                                              op0=ALU.add, op1=ALU.mult))
                link(dve.scalar_tensor_tensor(out=c2[:, :], in0=grp[:, :], scalar=float(GROUPS), in1=c1[:, :],
                                              op0=ALU.subtract, op1=ALU.mult))
                link(dve.tensor_reduce(lohi[:, 1:2], c0[:, :], AX_X, ALU.max))
                link(dve.tensor_reduce(lohi[:, 0:1], c2[:, :], AX_X, ALU.min))
                link(dve.tensor_scalar(lohi[:, 1:2], lohi[:, 1:2], 1.0, None, ALU.max))
                link(dve.tensor_scalar(c2[:, 0:1], lohi[:, 1:2], -1.0, None, ALU.add))
                link(dve.scalar_tensor_tensor(out=lohi[:, 0:1], in0=lohi[:, 0:1], scalar=float(GROUPS),
                                              in1=c2[:, 0:1], op0=ALU.add, op1=ALU.min))
                dve.tensor_copy(lohi_i[:, :], lohi[:, :]).then_inc(ranges, 1)
                for i, (n, h) in enumerate([(n, h) for n in names for h in (0, 1)]):
                    dve.wait_ge(turned, i + 1)
                    s = size[h]
                    dst = k.table[n][:, :].rearrange("p (g q) -> p g q", q=CPG)[:, low * h:low * h + s, :]
                    dve.tensor_copy(dst, pT[:, i, 0:CPG * s].rearrange("p (q g) -> p g q", q=CPG)).then_inc(cast, 1)
                dve.wait_ge(cast, 12)
                dve.tensor_copy(k.src_i[:, :], k.table["src"][:, :])

            @block.tensor
            def _(pe):
                pe.wait_ge(k.made, 2)
                pe.wait_ge(cast, 6)
                for h in (0, 1):
                    s = size[h]
                    for j in (0, 1):
                        ins = pe.matmul(pG[:, j, low * h:low * h + s],
                                        ext[0:s, 2 * h + j:2 * h + j + 1].broadcast_to([s, TILES]),
                                        k.ident[0:s, 0:s], start=(h == 0 and j == 0), stop=True,
                                        skip_group_check=True)
                ins.then_inc(rows_done, 1)
                for i, (n, h) in enumerate([(n, h) for n in names for h in (0, 1)]):
                    s = size[h]
                    for q in range(CPG):
                        ins = pe.transpose(pT[:, i, q * s:(q + 1) * s], val[n, h][0:s, q * P:(q + 1) * P],
                                           k.ident[0:s, 0:s])
                    ins.then_inc(turned, 1)


def build_counts(nc, a, k):
    with ExitStack() as ctx:
        m = Memory(nc, ctx, "cnt")
        rows = m.sb("rows", [P, CPG, D], F32)
        row_idx = m.sb("row_idx", [P, CPG], I32)
        src_hot = m.sb("src_hot", [P, 2, CW], BF16)
        dst_hot = m.sb("dst_hot", [P, CPG, P], BF16)
        dst_hot32 = m.sb("dst_hot32", [P, CPG, P], F32)
        msg = m.sb("msg", [P, CPG, AGG], F32)
        stage = m.sb("stage", [P, AGG], F32)
        acc = m.ps("acc", [P, 8, BANK])
        rows_free, idx_ready = m.sem("rows_free"), m.sem("idx_ready")
        rows_in = [m.sem(f"rows_in{q}") for q in range(CPG)]
        feat_in = [m.sem(f"feat_in{q}") for q in range(CPG)]
        hot_ready, msg_ready = m.sem("hot_ready"), m.sem("msg_ready")
        chunks_done = m.sem("chunks_done")
        dve_out, act_out, stored = m.sem("dve_out"), m.sem("act_out"), m.sem("stored")
        ones_set = m.sem("ones_set")

        def tile_range(eng, t):
            return (eng.value_load(k.ranges[0:1, bass.ds(t * 2, 1)], min_val=0, max_val=GROUPS - 1),
                    eng.value_load(k.ranges[0:1, bass.ds(t * 2 + 1, 1)], min_val=1, max_val=GROUPS))

        def counter(eng, name):
            r = eng.alloc_register(name)
            eng.reg_mov(r, 0)
            return r

        with nc.Block() as block:
            @block.gpsimd
            def _(pool):
                n = counter(pool, "pool_chunks")
                with pool.Fori(0, TILES) as t:
                    lo, hi = tile_range(pool, t)
                    with pool.Fori(lo, hi) as g:
                        c = pool.snap(n)
                        for q in range(CPG):
                            pool.wait_ge(rows_free, c + (q + 1))
                            pool.tensor_copy(row_idx[:, q:q + 1],
                                             k.src_i[:, bass.ds(g * CPG + q, 1)]).then_inc(idx_ready, 1)
                            pool.wait_ge(idx_ready, c + (q + 1))
                            pool.nop(nofuse=True)
                            pool.indirect_dma_start(rows[:, q, :], None, a["x"],
                                                    bass.IndirectOffsetOnAxis(ap=row_idx[:, q:q + 1], axis=0)
                                                    ).then_inc(rows_in[q], 16)
                        pool.reg_add(n, n, CPG)

            @block.sync
            def _(sp):
                n = counter(sp, "sp_chunks")
                feats = a["edge_attr"].rearrange("(c p) f -> c p f", p=P)
                with sp.Fori(0, TILES) as t:
                    lo, hi = tile_range(sp, t)
                    with sp.Fori(lo, hi) as g:
                        c = sp.snap(n)
                        for q in range(CPG):
                            sp.wait_ge(chunks_done, c + (q + 1))
                            sp.dma_start(msg[:, q, D:D + FE], feats[bass.ds(g * CPG + q, 1), :, :]
                                         .rearrange("a p f -> (a p) f")).then_inc(feat_in[q], 16)
                        sp.reg_add(n, n, CPG)
                    sp.wait_ge(act_out, t * 4 + 8)
                    sp.dma_start(k.sums_dram[bass.ds(t, 1), :, :].rearrange("a p f -> (a p) f"),
                                 stage[:, :]).then_inc(stored, 16)
                sp.wait_ge(stored, 16 * TILES)

            @block.vector
            def _(dve):
                dve.memset(msg[:, :, AGG - 1:AGG], 1.0).then_inc(ones_set, 1)
                dve.memset(k.C[:, :, CW:NP], 0.0)
                dve.sem_inc(dve_out, 4)
                n = counter(dve, "dve_chunks")
                with dve.Fori(0, TILES) as t:
                    lo, hi = tile_range(dve, t)
                    with dve.Fori(lo, hi) as g:
                        c = dve.snap(n)
                        for q in range(CPG):
                            dve.wait_ge(chunks_done, c + (q + CPG - 1))
                            dve.tensor_scalar(dst_hot[:, q, :], k.iota[:, 0:P], k.tile_base[:, bass.ds(t, 1)],
                                              k.table["dst"][:, bass.ds(g * CPG + q, 1)], ALU.add, ALU.is_equal)
                            dve.tensor_scalar(src_hot[:, q % 2, :], k.iota[:, :],
                                              k.table["src"][:, bass.ds(g * CPG + q, 1)], None,
                                              ALU.is_equal).then_inc(hot_ready, 1)
                        dve.reg_add(n, n, CPG)
                    dve.wait_ge(chunks_done, dve.snap(n) + CPG)
                    for b in range(4):
                        dve.tensor_copy(k.C[:, bass.ds(t, 1), b * CB:(b + 1) * CB].rearrange("p a n -> p (a n)"),
                                        acc[:, b, 0:CB]).then_inc(dve_out, 1)

            @block.scalar
            def _(act):
                act.sem_inc(rows_free, CPG)
                act.sem_inc(act_out, 4)
                n = counter(act, "act_chunks")
                with act.Fori(0, TILES) as t:
                    lo, hi = tile_range(act, t)
                    with act.Fori(lo, hi) as g:
                        c = act.snap(n)
                        for q in range(CPG):
                            act.wait_ge(chunks_done, c + (q + 1))
                            act.wait_ge(rows_in[q], (c + CPG) * (16 // CPG))
                            nc.scalar.activation(msg[:, q, 0:D], rows[:, q, :], ACT.Copy,
                                                 scale=k.table["w"][:, bass.ds(g * CPG + q, 1)]
                                                 ).then_inc(rows_free, 1)
                            act.wait_ge(hot_ready, c + (q + 1))
                            nc.scalar.activation(dst_hot32[:, q, :], dst_hot[:, q, :],
                                                 ACT.Copy).then_inc(msg_ready, 1)
                        act.reg_add(n, n, CPG)
                    act.wait_ge(chunks_done, act.snap(n) + CPG)
                    for b in range(4, CBANKS):
                        nc.scalar.activation(k.C[:, bass.ds(t, 1), b * CB:(b + 1) * CB].rearrange("p a n -> p (a n)"),
                                             acc[:, b, 0:CB], ACT.Copy).then_inc(act_out, 1)
                    act.wait_ge(stored, t * 16)
                    nc.scalar.activation(stage[:, :], acc[:, 7, 0:AGG], ACT.Copy).then_inc(act_out, 1)

            @block.tensor
            def _(pe):
                pe.sem_inc(chunks_done, CPG)
                n = counter(pe, "pe_chunks")
                pe.wait_ge(ones_set, 1)
                with pe.Fori(0, TILES) as t:
                    lo, hi = tile_range(pe, t)
                    pe.wait_ge(dve_out, t * 4 + 4)
                    pe.wait_ge(act_out, t * 4 + 4)
                    for b in range(8):
                        pe.matmul(acc[:, b, 0:1], k.zeros[:, 0:P], k.zeros[:, 0:1], start=True, stop=False,
                                  skip_group_check=True)
                    with pe.Fori(lo, hi) as g:
                        c = pe.snap(n)
                        for q in range(CPG):
                            pe.wait_ge(hot_ready, c + (q + 1))
                            for b in range(CBANKS):
                                pe.matmul(acc[:, b, 0:CB], dst_hot[:, q, :],
                                          src_hot[:, q % 2, b * CB:(b + 1) * CB], start=False, stop=False,
                                          skip_group_check=True)
                            pe.wait_ge(msg_ready, c + (q + 1))
                            pe.wait_ge(feat_in[q], (c + CPG) * (16 // CPG))
                            pe.matmul(acc[:, 7, 0:AGG], dst_hot32[:, q, :], msg[:, q, :], start=False, stop=False,
                                      skip_group_check=True).then_inc(chunks_done, 1)
                        pe.reg_add(n, n, CPG)



def strip_of(dram, i):
    return dram.rearrange("(s t p) f -> s p t f", t=STRIP, p=P)[bass.ds(i, 1)].rearrange("a p t f -> p (a t) f")


def flat(ap):
    return ap.rearrange("p t f -> p (t f)")


def normalize(link, act_link, dve, y, sq, st, out):
    link(dve.tensor_reduce(st[:, 0, :], y, AX_X, ALU.add))
    link(dve.tensor_scalar(st[:, 0, :], st[:, 0, :], 1.0 / D, None, ALU.mult))
    link(dve.tensor_tensor(y, y, last(st[:, 0, :], D), ALU.subtract))
    link(dve.tensor_tensor(sq, y, y, ALU.mult))
    link(dve.tensor_reduce(st[:, 1, :], sq, AX_X, ALU.add))
    act_link(dve.tensor_scalar(st[:, 1, :], st[:, 1, :], 1.0 / D, LN_EPS, ALU.mult, ALU.add))
    link(dve.reciprocal(st[:, 2, :], st[:, 2, :]))
    return dve.tensor_tensor(out, y, last(st[:, 2, :], D), ALU.mult)


NORM_LINKS = 6


def gin_nodes(nc, a, k):
    with ExitStack() as ctx:
        m = Memory(nc, ctx, "gin")
        w1, w2 = m.sb("w1", [P, D], F32), m.sb("w2", [P, D], F32)
        b1, b2 = m.sb("b1", [P, 1], F32), m.sb("b2", [P, D], F32)
        eps = m.sb("eps", [P, 1], F32)
        x, sums = m.sb("x", [P, STRIP, D], F32), m.sb("sums", [P, STRIP, AGG], F32)
        v, y, sq = (m.sb(n, [P, STRIP, D], F32) for n in ("v", "y", "sq"))
        out = m.sb("out", [P, STRIP, D], F32)
        vT, hT = m.sb("vT", [P, SW], F32), m.sb("hT", [P, SW], F32)
        eT = m.sb("eT", [FE + 1, SW], F32)
        st = m.sb("st", [P, 3, STRIP], F32)
        pV, pH, pO, pE = (m.ps(n, [P, 2 * BANK]) for n in ("pV", "pH", "pO", "pE"))
        consts, loaded, one_eps = m.sem("consts"), m.sem("loaded"), m.sem("one_eps")
        v_ready, turned, vT_ready = m.sem("v_ready"), m.sem("turned"), m.sem("vT_ready")
        h_ready, hT_ready, o_ready = m.sem("h_ready"), m.sem("hT_ready"), m.sem("o_ready")
        eT_ready, var, std = m.sem("eT_ready"), m.sem("var"), m.sem("std")
        chain, normed, stored, e_stored = m.sem("chain"), m.sem("normed"), m.sem("stored"), m.sem("e_stored")
        with nc.Block() as block:
            @block.sync
            def _(sp):
                sp.dma_start(w1[:, :], a["w1_0"]).then_inc(consts, 16)
                sp.dma_start(w2[:, :], a["w2_0"]).then_inc(consts, 16)
                with nc.allow_non_contiguous_dma(reason="one value per partition"):
                    sp.dma_start(b1[:, :], a["b1_0"].rearrange("(d a) -> d a", a=1)).then_inc(consts, 16)
                sp.dma_start(b2[:, :], a["b2_0"].partition_broadcast(P)).then_inc(consts, 16)
                sp.dma_start(eps[:, :], a["eps"].partition_broadcast(P)).then_inc(consts, 16)
                with sp.Fori(0, STRIPS) as i:
                    sp.wait_ge(normed, i)
                    sp.wait_ge(eT_ready, i)
                    sp.dma_start(x[:, :, :], strip_of(a["x"], i)).then_inc(loaded, 16)
                    sp.dma_start(sums[:, :, :], strip_of(k.sums_dram.rearrange("t p f -> (t p) f"), i)
                                 ).then_inc(loaded, 16)
                    sp.wait_ge(normed, i + 1)
                    sp.dma_start(strip_of(k.x1, i), out[:, :, :]).then_inc(stored, 16)
                    sp.wait_ge(eT_ready, i + 1)
                    sp.dma_start(k.edgeT[:, bass.ds(i * SW, SW)], eT[:, :]).then_inc(e_stored, 16)
                sp.wait_ge(stored, 16 * STRIPS)
                sp.wait_ge(e_stored, 16 * STRIPS)

            @block.vector
            def _(dve):
                links = 4 + NORM_LINKS
                dve.wait_ge(consts, 16 * 5)
                dve.tensor_scalar(eps[:, :], eps[:, :], 1.0, None, ALU.add).then_inc(one_eps, 1)
                dve.wait_ge(one_eps, 1)
                with dve.Fori(0, STRIPS) as i:
                    link = Chain(dve, chain, i * links)
                    dve.wait_ge(loaded, i * 32 + 32)
                    link(dve.tensor_scalar(sums[:, :, AGG - 1:AGG], sums[:, :, AGG - 1:AGG], 1.0, None, ALU.add))
                    dve.reciprocal(k.rdeg[:, bass.ds(i * STRIP, STRIP)],
                                   sums[:, :, AGG - 1:AGG].rearrange("p t f -> p (t f)"))
                    dve.scalar_tensor_tensor(out=v[:, :, :], in0=x[:, :, :], scalar=eps[:, :],
                                             in1=sums[:, :, 0:D], op0=ALU.mult, op1=ALU.add).then_inc(v_ready, 1)
                    dve.wait_ge(o_ready, i + 1)
                    link(dve.tensor_tensor(y[:, :, :], pO[:, 0:SW].rearrange("p (t f) -> p t f", f=D),
                                           mid(b2[:, :], STRIP), ALU.add))
                    link(dve.scalar_tensor_tensor(out=y[:, :, :], in0=y[:, :, :], scalar=0.0, in1=x[:, :, :],
                                                  op0=ALU.max, op1=ALU.add))

                    def act_link(ins):
                        ins.then_inc(var, 1)
                        dve.wait_ge(std, i + 1)
                    last_ins = normalize(link, act_link, dve, y[:, :, :], sq[:, :, :], st, v[:, :, :])
                    link(last_ins)
                    dve.wait_ge(stored, i * 16)
                    dve.tensor_copy(out[:, :, :], v[:, :, :]).then_inc(normed, 1)
                    assert link.n == links, link.n

            @block.scalar
            def _(act):
                with act.Fori(0, STRIPS) as i:
                    act.wait_ge(turned, i + 1)
                    nc.scalar.activation(vT[:, :], pV[:, 0:SW], ACT.Copy).then_inc(vT_ready, 1)
                    act.wait_ge(e_stored, i * 16)
                    nc.scalar.activation(eT[:, :], pE[0:FE + 1, 0:SW], ACT.Copy).then_inc(eT_ready, 1)
                    act.wait_ge(h_ready, i + 1)
                    nc.scalar.activation(hT[:, :], pH[:, 0:SW], ACT.Relu, bias=b1[:, :]).then_inc(hT_ready, 1)
                    act.wait_ge(var, i + 1)
                    nc.scalar.activation(st[:, 2, :], st[:, 1, :], ACT.Sqrt).then_inc(std, 1)

            @block.tensor
            def _(pe):
                pe.wait_ge(consts, 16 * 5)
                with pe.Fori(0, STRIPS) as i:
                    pe.wait_ge(v_ready, i + 1)
                    for c in range(STRIP):
                        pe.transpose(pV[:, c * P:(c + 1) * P], v[:, c, :], k.ident[:, :])
                    for c in range(STRIP):
                        ins = pe.transpose(pE[0:FE + 1, c * P:(c + 1) * P], sums[:, c, D:AGG], k.ident[:, :])
                    ins.then_inc(turned, 1)
                    pe.wait_ge(vT_ready, i + 1)
                    for lo, hi in halves(SW):
                        ins = pe.matmul(pH[:, lo:hi], w1[:, :], vT[:, lo:hi], start=True, stop=True)
                    ins.then_inc(h_ready, 1)
                    pe.wait_ge(hT_ready, i + 1)
                    for c in range(STRIP):
                        ins = pe.matmul(pO[:, c * P:(c + 1) * P], hT[:, c * P:(c + 1) * P], w2[:, :],
                                        start=True, stop=True)
                    ins.then_inc(o_ready, 1)


def split_features(nc, x_dram, parts, tag):
    with ExitStack() as ctx:
        m = Memory(nc, ctx, tag)
        x = m.sb("x", [P, STRIP, D], F32)
        loaded, high, rest, middle, low = (m.sem(n) for n in ("loaded", "high", "rest", "middle", "low"))
        with nc.Block() as block:
            @block.sync
            def _(sp):
                with sp.Fori(0, STRIPS) as i:
                    sp.wait_ge(low, i)
                    sp.dma_start(x[:, :, :], strip_of(x_dram, i)).then_inc(loaded, 16)

            @block.scalar
            def _(act):
                with act.Fori(0, STRIPS) as i:
                    act.wait_ge(loaded, i * 16 + 16)
                    nc.scalar.activation(parts[:, 0, bass.ds(i * STRIP, STRIP), :], x[:, :, :],
                                         ACT.Copy).then_inc(high, 1)
                    act.wait_ge(rest, i + 1)
                    nc.scalar.activation(parts[:, 1, bass.ds(i * STRIP, STRIP), :], x[:, :, :],
                                         ACT.Copy).then_inc(middle, 1)

            @block.vector
            def _(dve):
                with dve.Fori(0, STRIPS) as i:
                    dve.wait_ge(high, i + 1)
                    dve.tensor_tensor(x[:, :, :], x[:, :, :], parts[:, 0, bass.ds(i * STRIP, STRIP), :],
                                      ALU.subtract).then_inc(rest, 1)
                    dve.wait_ge(middle, i + 1)
                    dve.tensor_tensor(parts[:, 2, bass.ds(i * STRIP, STRIP), :], x[:, :, :],
                                      parts[:, 1, bass.ds(i * STRIP, STRIP), :], ALU.subtract).then_inc(low, 1)


def aggregate_strip(pe, pA, k, parts, i, features_ready=None, edge_terms=None):
    for lo, _ in halves(SW):
        pe.matmul(pA[:, lo:lo + 1], k.zeros[:, 0:P], k.zeros[:, 0:1], start=True, stop=False,
                  skip_group_check=True)
    with pe.Fori(0, STRIPS) as s:
        if features_ready:
            features_ready(s)
        for t in range(STRIP):
            for part in range(3):
                for lo, hi in halves(SW):
                    ins = pe.matmul(pA[:, lo:hi],
                                    parts[:, part, bass.ds(s * STRIP + t, 1), :].rearrange("p a f -> p (a f)"),
                                    k.C[:, bass.ds(s * STRIP + t, 1), bass.ds(i * SW + lo, hi - lo)]
                                    .rearrange("p a n -> p (a n)"),
                                    start=False, stop=False, skip_group_check=True)
    if edge_terms:
        edge_terms()
    return pe.matmul(pA[:, 0:1], k.zeros[:, 0:P], k.zeros[:, 0:1], start=False, stop=True,
                     skip_group_check=True)


def mean_layer(nc, a, k):
    with ExitStack() as ctx:
        m = Memory(nc, ctx, "mean")
        parts = m.sb("parts", [P, 3, TILES, D], BF16)
        split_features(nc, k.x1, parts, "mean_split")
        w, wT = m.sb("w", [P, 2, D], F32), m.sb("wT", [P, 2, D], F32)
        b = m.sb("b", [P, 2, D], F32)
        rdeg = m.sb("rdeg", [P, TILES], F32)
        ones = m.sb("ones", [P, 1], BF16)
        x, h, y, sq = (m.sb(n, [P, STRIP, D], F32) for n in ("x", "h", "y", "sq"))
        out = m.sb("out", [P, STRIP, D], F32)
        aggT, hT = m.sb("aggT", [P, SW], F32), m.sb("hT", [P, SW], F32)
        st = m.sb("st", [P, 3, STRIP], F32)
        pA, pB, pC = (m.ps(n, [P, 2 * BANK]) for n in ("pA", "pB", "pC"))
        pW, pD = m.ps("pW", [P, BANK]), m.ps("pD", [P, BANK])
        consts, loaded, w_turned, w_ready = (m.sem(n) for n in ("consts", "loaded", "w_turned", "w_ready"))
        ones_set, deg, rdeg_ready = m.sem("ones_set"), m.sem("deg"), m.sem("rdeg_ready")
        agg, aggT_ready, p1, h_ready, turned, hT_ready, p2 = (
            m.sem(n) for n in ("agg", "aggT_ready", "p1", "h_ready", "turned", "hT_ready", "p2"))
        chain, var, std, normed, stored = (m.sem(n) for n in ("chain", "var", "std", "normed", "stored"))
        with nc.Block() as block:
            @block.sync
            def _(sp):
                for j in (0, 1):
                    sp.dma_start(w[:, j, :], a[f"w{j + 1}_1"]).then_inc(consts, 16)
                    sp.dma_start(b[:, j, :], a[f"b{j + 1}_1"].partition_broadcast(P)).then_inc(consts, 16)
                with sp.Fori(0, STRIPS) as i:
                    sp.wait_ge(normed, i)
                    sp.dma_start(x[:, :, :], strip_of(k.x1, i)).then_inc(loaded, 16)
                    sp.wait_ge(normed, i + 1)
                    sp.dma_start(strip_of(k.x2, i), out[:, :, :]).then_inc(stored, 16)
                sp.wait_ge(stored, 16 * STRIPS)

            @block.vector
            def _(dve):
                links = 2 + NORM_LINKS
                dve.memset(ones[:, :], 1.0).then_inc(ones_set, 1)
                dve.wait_ge(w_turned, 1)
                dve.tensor_copy(wT[:, :, :], pW[:, 0:2 * D].rearrange("p (j f) -> p j f", j=2)).then_inc(w_ready, 1)
                dve.wait_ge(deg, 1)
                dve.tensor_scalar(rdeg[:, :], pD[:, 0:TILES], 1.0, None, ALU.max).then_inc(rdeg_ready, 1)
                dve.wait_ge(rdeg_ready, 1)
                dve.reciprocal(rdeg[:, :], rdeg[:, :]).then_inc(rdeg_ready, 1)
                dve.wait_ge(rdeg_ready, 2)
                dve.wait_ge(consts, 16 * 4)
                with dve.Fori(0, STRIPS) as i:
                    link = Chain(dve, chain, i * links)
                    dve.wait_ge(p1, i + 1)
                    for c in range(STRIP):
                        ins = dve.scalar_tensor_tensor(out=h[:, c, :], in0=pB[:, c * D:(c + 1) * D],
                                                       scalar=rdeg[:, bass.ds(i * STRIP + c, 1)], in1=b[:, 0, :],
                                                       op0=ALU.mult, op1=ALU.add)
                    ins.then_inc(h_ready, 1)
                    dve.wait_ge(p2, i + 1)
                    dve.wait_ge(loaded, i * 16 + 16)
                    link(dve.tensor_tensor(y[:, :, :], pC[:, 0:SW].rearrange("p (t f) -> p t f", f=D),
                                           mid(b[:, 1, :], STRIP), ALU.add))
                    link(dve.tensor_tensor(y[:, :, :], y[:, :, :], x[:, :, :], ALU.add))

                    def act_link(ins):
                        ins.then_inc(var, 1)
                        dve.wait_ge(std, i + 1)
                    dve.wait_ge(stored, i * 16)
                    normalize(link, act_link, dve, y[:, :, :], sq[:, :, :], st, out[:, :, :]).then_inc(normed, 1)
                    assert link.n == links, link.n
                with dve.Fori(0, TILES) as t:
                    diag = k.C[:, bass.ds(t, 1), bass.ds(t * P, P)].rearrange("p a n -> p (a n)")
                    dve.tensor_tensor(diag, diag, k.ident[:, :], ALU.add)

            @block.scalar
            def _(act):
                with act.Fori(0, STRIPS) as i:
                    act.wait_ge(agg, i + 1)
                    nc.scalar.activation(aggT[:, :], pA[:, 0:SW], ACT.Copy).then_inc(aggT_ready, 1)
                    act.wait_ge(turned, i + 1)
                    nc.scalar.activation(hT[:, :], pB[:, 0:SW], ACT.Relu).then_inc(hT_ready, 1)
                    act.wait_ge(var, i + 1)
                    nc.scalar.activation(st[:, 2, :], st[:, 1, :], ACT.Sqrt).then_inc(std, 1)

            @block.tensor
            def _(pe):
                pe.wait_ge(consts, 16 * 4)
                for j in (0, 1):
                    ins = pe.transpose(pW[:, j * D:(j + 1) * D], w[:, j, :], k.ident[:, :])
                ins.then_inc(w_turned, 1)
                pe.wait_ge(ones_set, 1)
                pe.matmul(pD[:, 0:TILES], k.zeros[:, 0:P], k.zeros[:, 0:TILES], start=True, stop=False,
                          skip_group_check=True)
                with pe.Fori(0, TILES) as s:
                    for t in range(TILES):
                        pe.matmul(pD[:, bass.ds(s, 1)],
                                  k.C[:, t, bass.ds(s * P, P)], ones[:, :], start=False, stop=False,
                                  skip_group_check=True)
                pe.matmul(pD[:, 0:1], k.zeros[:, 0:P], k.zeros[:, 0:1], start=False, stop=True,
                          skip_group_check=True).then_inc(deg, 1)
                pe.wait_ge(w_ready, 1)
                with pe.Fori(0, STRIPS) as i:
                    aggregate_strip(pe, pA, k, parts, i).then_inc(agg, 1)
                    pe.wait_ge(aggT_ready, i + 1)
                    for c in range(STRIP):
                        ins = pe.matmul(pB[:, c * P:(c + 1) * P], aggT[:, c * P:(c + 1) * P], wT[:, 0, :],
                                        start=True, stop=True)
                    ins.then_inc(p1, 1)
                    pe.wait_ge(h_ready, i + 1)
                    for c in range(STRIP):
                        ins = pe.transpose(pB[:, c * P:(c + 1) * P], h[:, c, :], k.ident[:, :])
                    ins.then_inc(turned, 1)
                    pe.wait_ge(hT_ready, i + 1)
                    for c in range(STRIP):
                        ins = pe.matmul(pC[:, c * P:(c + 1) * P], hT[:, c * P:(c + 1) * P], wT[:, 1, :],
                                        start=True, stop=True)
                    ins.then_inc(p2, 1)


def gat_linear(nc, a, k, g):
    heads, hc, w_tab = g.heads, D // g.heads, D + g.heads
    with ExitStack() as ctx:
        m = Memory(nc, ctx, f"lin{g.n}")
        w = m.sb("w", [P, D], F32)
        att = m.sb("att", [P, 2, D], F32)
        x = m.sb("x", [P, STRIP, D], F32)
        xT = m.sb("xT", [P, SW], F32)
        tab = m.sb("tab", [P, STRIP, heads, hc + 1], F32)
        prod = m.sb("prod", [P, 2, STRIP, D], F32)
        pT, pX = m.ps("pT", [P, 2 * BANK]), m.ps("pX", [P, 2 * BANK])
        consts, loaded, ones_set, turned, xT_ready, xh, tab_ready, terms, stored, chain = (
            m.sem(n) for n in ("consts", "loaded", "ones_set", "turned", "xT_ready", "xh", "tab_ready", "terms",
                               "stored", "chain"))
        with nc.Block() as block:
            @block.sync
            def _(sp):
                sp.dma_start(w[:, :], a[f"w{g.n}_2"]).then_inc(consts, 16)
                for j, n in enumerate(("att_src", "att_dst")):
                    sp.dma_start(att[:, j, :], a[f"{n}{g.n}"].rearrange("h c -> (h c)").partition_broadcast(P)
                                 ).then_inc(consts, 16)
                with sp.Fori(0, STRIPS) as i:
                    sp.wait_ge(turned, i)
                    sp.dma_start(x[:, :, :], strip_of(g.x, i)).then_inc(loaded, 16)
                    sp.wait_ge(tab_ready, i + 1)
                    sp.dma_start(g.table[:, bass.ds(i * STRIP, STRIP), :],
                                 tab[:, :, :, :].rearrange("p t h c -> p t (h c)")).then_inc(stored, 16)
                sp.wait_ge(stored, 16 * STRIPS)

            @block.scalar
            def _(act):
                act.wait_ge(ones_set, 1)
                with act.Fori(0, STRIPS) as i:
                    act.wait_ge(turned, i + 1)
                    nc.scalar.activation(xT[:, :], pT[:, 0:SW], ACT.Copy).then_inc(xT_ready, 1)
                    act.wait_ge(xh, i + 1)
                    act.wait_ge(stored, i * 16)
                    for c in range(STRIP):
                        ins = nc.scalar.activation(tab[:, c, :, 0:hc], pX[:, c * D:(c + 1) * D]
                                                   .rearrange("p (h c) -> p h c", h=heads), ACT.Copy)
                    ins.then_inc(tab_ready, 1)

            @block.vector
            def _(dve):
                dve.memset(tab[:, :, :, hc:hc + 1], 1.0).then_inc(ones_set, 1)
                dve.wait_ge(consts, 16 * 3)
                with dve.Fori(0, STRIPS) as i:
                    dve.wait_ge(tab_ready, i + 1)
                    link = Chain(dve, chain, i * 3)
                    for j in (0, 1):
                        link(dve.tensor_tensor(prod[:, j, :, :], pX[:, 0:SW].rearrange("p (t f) -> p t f", f=D),
                                               mid(att[:, j, :], STRIP), ALU.mult))
                    for j in (0, 1):
                        ins = dve.tensor_reduce(g.att[:, j, bass.ds(i * STRIP * heads, STRIP * heads)],
                                                prod[:, j, :, :].rearrange("p t (h c) -> p (t h) c", h=heads),
                                                AX_X, ALU.add)
                    link(ins)
                    dve.tensor_scalar(g.att[:, 4, bass.ds(i * STRIP * heads, STRIP * heads)],
                                      g.att[:, 0, bass.ds(i * STRIP * heads, STRIP * heads)], SLOPE, None,
                                      ALU.mult).then_inc(terms, 1)

            @block.tensor
            def _(pe):
                pe.wait_ge(consts, 16 * 3)
                with pe.Fori(0, STRIPS) as i:
                    pe.wait_ge(loaded, i * 16 + 16)
                    for c in range(STRIP):
                        ins = pe.transpose(pT[:, c * P:(c + 1) * P], x[:, c, :], k.ident[:, :])
                    ins.then_inc(turned, 1)
                    pe.wait_ge(xT_ready, i + 1)
                    pe.wait_ge(tab_ready, i)
                    pe.wait_ge(terms, i)
                    for c in range(STRIP):
                        ins = pe.matmul(pX[:, c * D:(c + 1) * D], xT[:, c * P:(c + 1) * P], w[:, :],
                                        start=True, stop=True)
                    ins.then_inc(xh, 1)


def store_rows(nc, k, g, shares, tag, path):
    heads = g.heads
    with ExitStack() as ctx:
        m = Memory(nc, ctx, tag)
        rows = m.sb("rows", [TILES, len(shares), heads, P], F32)
        pT = m.ps("pT", [TILES, len(shares), 2 * BANK])
        turned, ready, stored = m.sem("turned"), m.sem("ready"), m.sem("stored")
        with nc.Block() as block:
            @block.tensor
            def _(pe):
                with on_path(pe, k, path):
                    for i, (j, _) in enumerate(shares):
                        by_head = g.att[:, j, :].rearrange("p (t h) -> p h t", h=heads)
                        for h in range(heads):
                            ins = pe.transpose(pT[:, i, h * P:(h + 1) * P], by_head[:, h, :], k.ident[:, :])
                    ins.then_inc(turned, 1)

            @block.scalar
            def _(act):
                with on_path(act, k, path):
                    act.wait_ge(turned, 1)
                    for i in range(len(shares)):
                        nc.scalar.activation(rows[:, i, :, :].rearrange("t h p -> t (h p)"),
                                             pT[:, i, 0:heads * P], ACT.Copy).then_inc(ready, 1)

            @block.sync
            def _(sp):
                with on_path(sp, k, path):
                    for i, (_, dram) in enumerate(shares):
                        sp.wait_ge(ready, i + 1)
                        sp.dma_start(dram.rearrange("h (t p) -> t h p", p=P), rows[:, i, :, :]).then_inc(stored, 16)
                    sp.wait_ge(stored, 16 * len(shares))


def gat_max(nc, k, g):
    heads = g.heads
    with ExitStack() as ctx:
        m = Memory(nc, ctx, f"max{g.n}")
        row = m.sb("row", [P, NP], F32)
        far = m.sb("far", [P, 2, NP], BF16)
        scratch = m.ps("scratch", [P, NP])
        bias = m.sb("bias", [P, 1], F32)
        one = m.sb("one", [P, 1], F32)
        bias_set, loaded, far_ready, far_used, kept = (
            m.sem(n) for n in ("bias_set", "loaded", "far_ready", "far_used", "kept"))
        with nc.Block() as block:
            @block.sync
            def _(sp):
                with on_path(sp, k, True):
                    with sp.Fori(0, heads) as h:
                        sp.wait_ge(far_used, h * TILES)
                        sp.dma_start(row[:, :], g.src_rows[bass.ds(h, 1), :].rearrange("a n -> (a n)")
                                     .partition_broadcast(P)).then_inc(loaded, 16)

            @block.scalar
            def _(act):
                with on_path(act, k, True):
                    act.wait_ge(bias_set, 1)

                    def mask(n, t, slot):
                        nc.scalar.activation(far[:, slot, :], k.C[:, bass.ds(t, 1), :].rearrange("p a n -> p (a n)"),
                                             ACT.Relu, bias=bias[:, :], scale=-FAR).then_inc(far_ready, 1)

                    with act.Fori(0, heads) as h:
                        with act.Fori(0, TILES // 2) as u:
                            for s in (0, 1):
                                n = h * TILES + u * 2 + s
                                if s == 0:
                                    act.wait_ge(far_used, n)
                                else:
                                    act.wait_ge(far_used, h * TILES + u * 2)
                                mask(n, u * 2 + s, s)
                        act.wait_ge(far_used, h * TILES + (TILES - 1))
                        mask(None, TILES - 1, 0)

            @block.vector
            def _(dve):
                with on_path(dve, k, True):
                    dve.memset(bias[:, :], FAR).then_inc(bias_set, 1)

                    def greatest(n, h, t, slot):
                        dve.wait_ge(far_ready, n + 1)
                        dve.wait_ge(kept, n)
                        dve.nop(nofuse=True)
                        dve.tensor_tensor_reduce(scratch[:, :], row[:, :], far[:, slot, :], 1.0, -BIG,
                                                 ALU.subtract, ALU.max, one[:, :]).then_inc(far_used, 1)
                        dve.wait_ge(far_used, n + 1)
                        dve.tensor_copy(g.att[:, 2, bass.ds(t * heads + h, 1)], one[:, :]).then_inc(kept, 1)

                    with dve.Fori(0, heads) as h:
                        dve.wait_ge(loaded, h * 16 + 16)
                        dve.nop(nofuse=True)
                        with dve.Fori(0, TILES // 2) as u:
                            for s in (0, 1):
                                greatest(h * TILES + u * 2 + s, h, u * 2 + s, s)
                        greatest(h * TILES + (TILES - 1), h, TILES - 1, 0)


def target_shares(nc, k, g):
    with ExitStack() as ctx:
        m = Memory(nc, ctx, f"shares{g.n}")
        z = m.sb("z", [P, 2, TILES * g.heads], F32)
        chain = m.sem("chain")
        with nc.Block() as block:
            @block.vector
            def _(dve):
                link = Chain(dve, chain)
                link(dve.tensor_tensor(z[:, 0, :], g.att[:, 2, :], g.att[:, 1, :], ALU.add))
                link(dve.scalar_tensor_tensor(out=z[:, 1, :], in0=z[:, 0, :], scalar=SLOPE, in1=z[:, 0, :],
                                              op0=ALU.mult, op1=ALU.max))
                dve.tensor_tensor(g.att[:, 2, :], g.att[:, 1, :], z[:, 1, :], ALU.subtract)
                dve.scalar_tensor_tensor(out=g.att[:, 3, :], in0=g.att[:, 1, :], scalar=SLOPE, in1=z[:, 1, :],
                                         op0=ALU.mult, op1=ALU.subtract)


def source_bound(nc, k, g):
    with ExitStack() as ctx:
        m = Memory(nc, ctx, f"bound{g.n}")
        ends = m.sb("ends", [P, 2], F32)
        end = m.sb("end", [1, 3], F32)
        ones = m.sb("ones", [1, P], F32)
        pT, pB = m.ps("pT", [1, 2, P]), m.ps("pB", [P, 1])
        chain, ends_ready, turned, end_ready, spread = (
            m.sem(n) for n in ("chain", "ends_ready", "turned", "end_ready", "spread"))
        with nc.Block() as block:
            @block.vector
            def _(dve):
                link = Chain(dve, chain)
                dve.memset(ones[:, :], 1.0)
                dve.tensor_reduce(ends[:, 0:1], g.att[:, 0, :], AX_X, ALU.max)
                link(dve.tensor_reduce(ends[:, 1:2], g.att[:, 0, :], AX_X, ALU.min))
                dve.tensor_scalar(ends[:, 1:2], ends[:, 1:2], -1.0, None, ALU.mult).then_inc(ends_ready, 1)
                dve.wait_ge(turned, 1)
                dve.tensor_reduce(end[:, 0:2], pT[:, :, :], AX_X, ALU.max).then_inc(end_ready, 1)
                dve.wait_ge(end_ready, 1)
                link(dve.tensor_tensor(end[:, 2:3], end[:, 0:1], end[:, 1:2], ALU.add))
                dve.tensor_scalar(k.wide[:, :], end[:, 2:3], SPREAD, None, ALU.is_gt)
                dve.wait_ge(spread, 1)
                for j, scale in enumerate((1.0, SLOPE, -1.0, -SLOPE)):
                    dve.tensor_scalar(k.top[:, j:j + 1], pB[:, :], scale, None, ALU.mult)
                dve.tensor_copy(g.att[:, 2, :], pB[:, 0:1].broadcast_to([P, TILES * g.heads]))

            @block.tensor
            def _(pe):
                pe.wait_ge(ends_ready, 1)
                for j in (0, 1):
                    ins = pe.transpose(pT[:, j, :], ends[:, j:j + 1], k.ident[:, :])
                ins.then_inc(turned, 1)
                pe.wait_ge(end_ready, 1)
                pe.matmul(pB[:, :], ones[:, :], end[:, 0:1], start=True, stop=True).then_inc(spread, 1)


def turn_counts(nc, k, tag, wide_only=False):
    with ExitStack() as ctx:
        m = Memory(nc, ctx, tag)
        pI = m.ps("pI", [P, STRIP, 2 * BANK], BF16)
        identb = m.sb("identb", [P, P], BF16)
        made, turned, upper, lower = m.sem("made"), m.sem("turned"), m.sem("upper"), m.sem("lower")
        d_turned, d_put = m.sem("d_turned"), m.sem("d_put")

        def block_of(r, c):
            return k.C[:, bass.ds(r, 1), bass.ds(c * P, P)].rearrange("p a n -> p (a n)")

        pairs = [(x, y) for y in range(1, STRIPS) for x in range(y)]
        path = True if wide_only else None

        def each_row(eng, n, fn):
            fn(0, n * STRIP, 0, n * STRIP + 1)
            with eng.Fori(0, STRIP // 2) as u:
                for r in (1, 2):
                    fn(u * 2 + r, u * 2 + (n * STRIP + r), r % 2, u * 2 + (n * STRIP + r))

        with nc.Block() as block:
            @block.vector
            def _(dve):
                with on_path(dve, k, path):
                    dve.tensor_copy(identb[:, :], k.ident[:, :]).then_inc(made, 1)
                    dve.sem_inc(upper, 1)
                    for n, (x, y) in enumerate(pairs):
                        def row(r, step, slot, free):
                            dve.wait_ge(turned, step + 1)
                            dve.tensor_copy(k.C[:, y * STRIP:(y + 1) * STRIP, bass.ds((r + x * STRIP) * P, P)],
                                            pI[:, 2 * slot, 0:SW].rearrange("p (c n) -> p c n", n=P)
                                            ).then_inc(upper, 1)
                        each_row(dve, n, row)
                    with dve.Fori(0, STRIPS) as x:
                        dve.wait_ge(d_turned, x + 1)
                        for r in range(STRIP):
                            ins = dve.tensor_copy(k.C[:, bass.ds(x * STRIP + r, 1), bass.ds(x * SW, SW)]
                                                  .rearrange("p a n -> p (a n)"), pI[:, r, 0:SW])
                        ins.then_inc(d_put, 1)

            @block.scalar
            def _(act):
                with on_path(act, k, path):
                    act.sem_inc(lower, 1)
                    for n, (x, y) in enumerate(pairs):
                        def row(r, step, slot, free):
                            act.wait_ge(turned, step + 1)
                            nc.scalar.activation(k.C[:, bass.ds(r + x * STRIP, 1), y * SW:(y + 1) * SW]
                                                 .rearrange("p a n -> p (a n)"), pI[:, 2 * slot + 1, 0:SW],
                                                 ACT.Copy).then_inc(lower, 1)
                        each_row(act, n, row)

            @block.tensor
            def _(pe):
                with on_path(pe, k, path):
                    pe.wait_ge(made, 1)
                    for n, (x, y) in enumerate(pairs):
                        def row(r, step, slot, free):
                            pe.wait_ge(upper, free)
                            pe.wait_ge(lower, free)
                            for c in range(STRIP):
                                pe.transpose(pI[:, 2 * slot, c * P:(c + 1) * P],
                                             block_of(r + x * STRIP, y * STRIP + c), identb[:, :])
                            for c in range(STRIP):
                                ins = pe.transpose(pI[:, 2 * slot + 1, c * P:(c + 1) * P],
                                                   block_of(y * STRIP + c, r + x * STRIP), identb[:, :])
                            ins.then_inc(turned, 1)
                        each_row(pe, n, row)
                    pe.wait_ge(upper, len(pairs) * STRIP + 1)
                    pe.wait_ge(lower, len(pairs) * STRIP + 1)
                    with pe.Fori(0, STRIPS) as x:
                        pe.wait_ge(d_put, x)
                        for r in range(STRIP):
                            for c in range(STRIP):
                                ins = pe.transpose(pI[:, r, c * P:(c + 1) * P],
                                                   block_of(x * STRIP + c, x * STRIP + r), identb[:, :])
                        ins.then_inc(d_turned, 1)


def gat_sums(nc, k, g, path):
    heads, w1 = g.heads, D // g.heads + 1
    per_bank = min(STRIP, BANK // w1)
    SLOTS = 5
    assert TILES % SLOTS == 0
    with ExitStack() as ctx:
        m = Memory(nc, ctx, f"sum{g.n}")
        tab = m.sb("tab", [P, TILES, w1], F32)
        shares = m.sb("shares", [P, 2, 2, SW], F32)
        e = m.sb("e", [P, SLOTS, 2, SW], F32)
        sums = m.sb("sums", [P, STRIP, w1], F32)
        acc = m.ps("acc", [P, 2, 2 * BANK])
        tab_in, stored = m.sem("tab_in"), m.sem("stored")
        shares_in = [[m.sem(f"shares_in{s}{x}") for x in (0, 1)] for s in (0, 1)]
        exps, larger, weights, steps_done, acc_ready, acc_out = (
            m.sem(n) for n in ("exps", "larger", "weights", "steps_done", "acc_ready", "acc_out"))

        def acc_tile(slot, c):
            at = (c // per_bank) * BANK + (c % per_bank) * w1
            return acc[:, slot, at:at + w1]

        def each_step(eng, fn, h, j):
            first = h * (STRIPS * TILES) + j * TILES
            with eng.Fori(0, TILES // SLOTS) as u:
                for s in range(SLOTS):
                    fn(first + u * SLOTS + s, u * SLOTS + s, s)

        def loads(h, j):
            return (h * (3 - j % 2) + (j // 2 + 1)) * 16

        with nc.Block() as block:
            @block.sync
            def _(sp):
                with on_path(sp, k, path):
                    def store(h, j):
                        sp.wait_ge(acc_out, h * STRIPS + (j + 1))
                        sp.dma_start(g.sums[:, j * STRIP:(j + 1) * STRIP, bass.ds(h * w1, w1)],
                                     sums[:, :, :]).then_inc(stored, 16)

                    with sp.Fori(0, heads) as h:
                        sp.wait_ge(steps_done, h * (STRIPS * TILES) + SLOTS)
                        sp.dma_start(tab[:, :, :], g.table[:, :, bass.ds(h * w1, w1)]).then_inc(tab_in, 16)
                        for j in range(STRIPS):
                            if j > 1:
                                sp.wait_ge(exps, h * (STRIPS * TILES) + (j - 1) * TILES)
                            for x in (0, 1):
                                row = g.dst_rows[x][bass.ds(h, 1), j * SW:(j + 1) * SW].rearrange("a n -> (a n)")
                                sp.dma_start(shares[:, j % 2, x, :], row.partition_broadcast(P)
                                             ).then_inc(shares_in[j % 2][x], 16)
                            if j:
                                store(h, j - 1)
                        store(h, STRIPS - 1)
                    sp.wait_ge(stored, 16 * heads * STRIPS)

            @block.scalar
            def _(act):
                with on_path(act, k, path):
                    with act.Fori(0, heads) as h:
                        for j in range(STRIPS):
                            for x in (0, 1):
                                act.wait_ge(shares_in[j % 2][x], loads(h, j))
                            act.nop(nofuse=True)

                            def step(n, s, slot):
                                act.wait_ge(steps_done, n + 1)
                                act.nop(nofuse=True)
                                for x, term in ((0, 0), (1, 4)):
                                    ins = nc.scalar.activation(e[:, slot, x, :], shares[:, j % 2, x, :], ACT.Exp,
                                                               bias=g.att[:, term, bass.ds(s * heads + h, 1)])
                                ins.then_inc(exps, 1)
                            each_step(act, step, h, j)

            @block.vector
            def _(dve):
                with on_path(dve, k, path):
                    with dve.Fori(0, heads) as h:
                        for j in range(STRIPS):
                            def step(n, s, slot):
                                dve.wait_ge(exps, n + 1)
                                dve.tensor_tensor(e[:, slot, 0, :], e[:, slot, 0, :], e[:, slot, 1, :],
                                                  ALU.max).then_inc(larger, 1)
                                dve.wait_ge(larger, n + 1)
                                dve.scalar_tensor_tensor(
                                    out=e[:, slot, 0, :], in0=e[:, slot, 0, :], scalar=BIG,
                                    in1=k.C[:, bass.ds(s, 1), j * SW:(j + 1) * SW].rearrange("p a n -> p (a n)"),
                                    op0=ALU.min, op1=ALU.mult).then_inc(weights, 1)
                            each_step(dve, step, h, j)
                            dve.wait_ge(acc_ready, h * STRIPS + (j + 1))
                            if j:
                                dve.wait_ge(stored, h * (16 * STRIPS) + 16 * j)
                            for c in range(0, STRIP, per_bank):
                                c1 = min(STRIP, c + per_bank)
                                at = c // per_bank * BANK
                                ins = dve.tensor_copy(
                                    sums[:, c:c1, :],
                                    acc[:, j % 2, at:at + (c1 - c) * w1].rearrange("p (t c) -> p t c", c=w1))
                            ins.then_inc(acc_out, 1)
                        dve.wait_ge(stored, h * (16 * STRIPS) + 16 * STRIPS)

            @block.tensor
            def _(pe):
                with on_path(pe, k, path):
                    pe.sem_inc(steps_done, SLOTS)
                    with pe.Fori(0, heads) as h:
                        pe.wait_ge(tab_in, h * 16 + 16)
                        for j in range(STRIPS):
                            if j != 1:
                                pe.wait_ge(acc_out, h * STRIPS + max(0, j - 1))
                            for x in range(-(-STRIP // per_bank)):
                                pe.matmul(acc[:, j % 2, x * BANK:x * BANK + 1], k.zeros[:, :], k.zeros[:, 0:1],
                                          start=True, stop=False, skip_group_check=True)

                            def step(n, s, slot):
                                pe.wait_ge(weights, n + 1)
                                for c in range(STRIP):
                                    ins = pe.matmul(acc_tile(j % 2, c), e[:, slot, 0, c * P:(c + 1) * P],
                                                    tab[:, bass.ds(s, 1), :].rearrange("p a c -> p (a c)"),
                                                    start=False, stop=False, skip_group_check=True)
                                ins.then_inc(steps_done, 1)
                            each_step(pe, step, h, j)
                            pe.matmul(acc[:, j % 2, 0:1], k.zeros[:, :], k.zeros[:, 0:1], start=False, stop=True,
                                      skip_group_check=True).then_inc(acc_ready, 1)


def branch_sums(nc, k, g):
    heads, w1 = g.heads, D // g.heads + 1
    rows = 2 * 3 * w1
    GROUP = 2 * CB // P
    groups = [(n * GROUP, min(GROUP, TILES - n * GROUP)) for n in range(-(-TILES // GROUP))]
    with ExitStack() as ctx:
        m = Memory(nc, ctx, "branch")
        row = m.sb("row", [P, CW], F32)
        sign = m.sb("sign", [P, 2, CW], BF16)
        v = m.sb("v", [P, TILES, 4, 3, w1], BF16)
        rest = m.sb("rest", [P, V_PARTS[0][1], 2, w1], F32)
        tab = m.sb("tab", [P, TILES, w1], F32)
        src_part = m.sb("src_part", [P, 2, TILES * heads], F32)
        half = m.sb("half", [P, 2 * CB], F32)
        pick = m.sb("pick", [P, 2, w1], F32)
        prod = m.sb("prod", [P, GROUP, 2, w1], F32)
        sums = m.sb("sums", [P, TILES, w1], F32)
        acc = m.ps("acc", [P, CBANKS, BANK])
        turn = m.ps("turn", [P, GROUP, 2, w1])
        row_in, tab_in, stored = [m.sem(f"row_in{x}") for x in (0, 1)], m.sem("tab_in"), m.sem("stored")
        exps, parts_ready, pick_ready, v_chain, v_ready = (
            m.sem(n) for n in ("exps", "parts_ready", "pick_ready", "v_chain", "v_ready"))
        signs, signed, halves_done = m.sem("signs"), m.sem("signed"), m.sem("halves_done")
        acc_ready, half_ready, turned, prods, added = (
            m.sem(n) for n in ("acc_ready", "half_ready", "turned", "prods", "added"))

        def each_tile(eng, h, fn):
            first = h * (2 * TILES)
            fn(first, 0, 0, first + (2 * TILES - 1))
            with eng.Fori(0, TILES // 2) as u:
                for s in (1, 2):
                    n = first + u * 4 + 2 * s
                    fn(n, u * 2 + s, s % 2, n + (2 * TILES - 3))

        with nc.Block() as block:
            @block.sync
            def _(sp):
                with on_path(sp, k, False):
                    def load(h):
                        sp.wait_ge(v_ready, h * len(V_PARTS) + 1)
                        sp.dma_start(tab[:, :, :], g.table[:, :, bass.ds(h * w1, w1)]).then_inc(tab_in, 16)
                        for x, (lo, hi) in enumerate(HALVES):
                            sp.wait_ge(signs, h * (2 * TILES) + (x + 1))
                            sp.dma_start(row[:, lo * CB:hi * CB], g.dst_row[bass.ds(h, 1), lo * CB:hi * CB]
                                         .rearrange("a n -> (a n)").partition_broadcast(P)).then_inc(row_in[x], 16)

                    def store(h):
                        sp.wait_ge(added, (h + 1) * len(groups))
                        sp.dma_start(g.sums[:, :, bass.ds(h * w1, w1)], sums[:, :, :]).then_inc(stored, 16)

                    load(0)
                    with sp.Fori(1, heads) as h:
                        load(h)
                        store(h - 1)
                    store(heads - 1)
                    sp.wait_ge(stored, 16 * heads)

            @block.gpsimd
            def _(pool):
                with on_path(pool, k, False):
                    pool.sem_inc(v_ready, 1)
                    pool.wait_ge(parts_ready, 1)
                    with pool.Fori(0, heads) as h:
                        link = Chain(pool, v_chain, h * (len(V_PARTS) * 7))
                        pool.wait_ge(tab_in, h * 16 + 16)
                        for n, (lo, hi) in enumerate(V_PARTS):
                            pool.wait_ge(halves_done, h * (2 * TILES) + 2 * hi)
                            r = rest[:, 0:hi - lo]
                            for x in (0, 1):
                                share = src_part[:, x, :].rearrange("p (t h) -> p t h", h=heads)[:, lo:hi, bass.ds(h, 1)]
                                link(pool.tensor_tensor(r[:, :, x, :], tab[:, lo:hi, :],
                                                        share.broadcast_to([P, hi - lo, w1]), ALU.mult))
                            for part in (0, 1):
                                pool.nop(nofuse=True)
                                link(pool.tensor_copy(v[:, lo:hi, 0:2, part, :], r))
                                link(pool.tensor_tensor(r, r, v[:, lo:hi, 0:2, part, :], ALU.subtract))
                            pool.nop(nofuse=True)
                            link(pool.tensor_copy(v[:, lo:hi, 0:2, 2, :], r))
                            pool.nop(nofuse=True)
                            pool.tensor_copy(v[:, lo:hi, 2, :, :], v[:, lo:hi, 0, :, :])
                            pool.tensor_scalar(v[:, lo:hi, 3, :, :], v[:, lo:hi, 1, :, :], -1.0, None,
                                               ALU.mult).then_inc(v_ready, 1)

            @block.scalar
            def _(act):
                with on_path(act, k, False):
                    for x in (0, 1):
                        nc.scalar.activation(src_part[:, x, :], g.att[:, 4 * x, :], ACT.Exp, bias=k.top[:, 2 + x:3 + x])
                        ins = nc.scalar.activation(g.att[:, 2 + x, :], g.att[:, 2 + x, :], ACT.Exp, bias=k.top[:, x:x + 1])
                    ins.then_inc(exps, 1)
                    act.sem_inc(signs, 2)
                    with act.Fori(0, heads) as h:
                        for x in (0, 1):
                            act.wait_ge(row_in[x], h * 16 + 16)

                        def step(n, s, slot, free):
                            for x, (lo, hi) in enumerate(HALVES):
                                act.wait_ge(halves_done, free + x)
                                act.nop(nofuse=True)
                                nc.scalar.activation(sign[:, slot, lo * CB:hi * CB], row[:, lo * CB:hi * CB], ACT.Sign,
                                                     bias=g.att[:, 0, bass.ds(s * heads + h, 1)]).then_inc(signs, 1)
                        each_tile(act, h, step)
                        act.wait_ge(acc_ready, h + 1)
                        for n, (t, size) in enumerate(groups):
                            act.wait_ge(turned, h * len(groups) + n)
                            banks = min(2, CBANKS - 2 * n)
                            nc.scalar.activation(half[0:rows, 0:banks * CB].rearrange("p (b n) -> p b n", n=CB),
                                                 acc[0:rows, 2 * n:2 * n + banks, 0:CB], ACT.Copy).then_inc(half_ready, 1)

            @block.vector
            def _(dve):
                with on_path(dve, k, False):
                    dve.tensor_reduce(pick[0:rows, :, :],
                                      k.ident[0:rows, 0:rows].rearrange("p (x r c) -> p x c r", x=2, r=3),
                                      AX_X, ALU.add).then_inc(pick_ready, 1)
                    dve.wait_ge(exps, 1)
                    dve.tensor_scalar(src_part[:, :, :], src_part[:, :, :], 0.5, None, ALU.mult).then_inc(parts_ready, 1)
                    with dve.Fori(0, heads) as h:
                        def step(n, s, slot, free):
                            for x, (lo, hi) in enumerate(HALVES):
                                dve.wait_ge(signs, n + (x + 3))
                                dve.tensor_tensor(sign[:, slot, lo * CB:hi * CB], sign[:, slot, lo * CB:hi * CB],
                                                  k.C[:, bass.ds(s, 1), lo * CB:hi * CB].rearrange("p a n -> p (a n)"),
                                                  ALU.mult).then_inc(signed, 1)
                        each_tile(dve, h, step)
                        dve.wait_ge(stored, h * 16)
                        for n, (t, size) in enumerate(groups):
                            dve.wait_ge(turned, h * len(groups) + (n + 1))
                            shares = g.att[:, 2:4, :].rearrange("p x (t h) -> p t x h", h=heads)
                            dve.tensor_tensor(prod[:, 0:size], turn[:, 0:size],
                                              shares[:, t:t + size, :, bass.ds(h, 1)].broadcast_to([P, size, 2, w1]),
                                              ALU.mult).then_inc(prods, 1)
                            dve.wait_ge(prods, h * len(groups) + (n + 1))
                            dve.tensor_tensor(sums[:, t:t + size, :], prod[:, 0:size, 0, :], prod[:, 0:size, 1, :],
                                              ALU.add).then_inc(added, 1)
                            dve.wait_ge(added, h * len(groups) + (n + 1))

            @block.tensor
            def _(pe):
                with on_path(pe, k, False):
                    pe.sem_inc(halves_done, 2 * TILES)
                    pe.wait_ge(pick_ready, 1)
                    with pe.Fori(0, heads) as h:
                        pe.wait_ge(half_ready, h * len(groups))
                        for b in range(CBANKS):
                            pe.matmul(acc[:, b, 0:1], k.zeros[:, 0:P], k.zeros[:, 0:1], start=True, stop=False,
                                      skip_group_check=True)

                        def tile(s, slot):
                            values = v[:, bass.ds(s, 1), :, :, :].rearrange("p a x r c -> p (a x r c)")
                            for x, half_banks in enumerate(HALVES):
                                for b in range(*half_banks):
                                    pe.matmul(acc[0:rows, b, 0:CB], values[:, 0:rows],
                                              k.C[:, bass.ds(s, 1), b * CB:(b + 1) * CB].rearrange("p a n -> p (a n)"),
                                              start=False, stop=False, skip_group_check=True)
                                pe.wait_ge(signed, h * (2 * TILES) + (s * 2 + (x + 1)))
                                for b in range(*half_banks):
                                    ins = pe.matmul(acc[0:rows, b, 0:CB], values[:, rows:2 * rows],
                                                    sign[:, slot, b * CB:(b + 1) * CB],
                                                    start=False, stop=False, skip_group_check=True)
                                ins.then_inc(halves_done, 1)

                        for n, (lo, hi) in enumerate(V_PARTS):
                            pe.wait_ge(v_ready, h * len(V_PARTS) + (n + 2))
                            if n == 0:
                                tile(0, 0)
                                lo = 1
                            pe.nop(nofuse=True)
                            with pe.Fori(0, (hi - lo) // 2) as u:
                                for s in (0, 1):
                                    tile(u * 2 + (lo + s), (lo + s) % 2)
                        pe.matmul(acc[:, 0, 0:1], k.zeros[:, 0:P], k.zeros[:, 0:1], start=False, stop=True,
                                  skip_group_check=True).then_inc(acc_ready, 1)
                        for n, (t, size) in enumerate(groups):
                            pe.wait_ge(half_ready, h * len(groups) + (n + 1))
                            pe.wait_ge(prods, h * len(groups) + n)
                            for c in range(size):
                                ins = pe.matmul(turn[:, c, :, :], half[0:rows, c * P:(c + 1) * P], pick[0:rows, :, :],
                                                start=True, stop=True)
                            ins.then_inc(turned, 1)


def gat_nodes(nc, a, k, g):
    heads, hc = g.heads, D // g.heads
    with ExitStack() as ctx:
        m = Memory(nc, ctx, f"post{g.n}")
        b = m.sb("b", [P, D], F32)
        x, y, sq, out = (m.sb(n, [P, STRIP, D], F32) for n in ("x", "y", "sq", "out"))
        sums = m.sb("sums", [P, STRIP, D + heads], F32)
        st = m.sb("st", [P, 3, STRIP], F32)
        rw = m.sb("rw", [P, STRIP * heads], F32)
        consts, loaded, chain, to_act, from_act, normed, stored = (
            m.sem(n) for n in ("consts", "loaded", "chain", "to_act", "from_act", "normed", "stored"))
        first = g.n == 1
        with nc.Block() as block:
            @block.sync
            def _(sp):
                sp.dma_start(b[:, :], a[f"b{g.n}_2"].partition_broadcast(P)).then_inc(consts, 16)
                with sp.Fori(0, STRIPS) as i:
                    sp.wait_ge(normed, i)
                    sp.dma_start(x[:, :, :], strip_of(k.x2, i)).then_inc(loaded, 16)
                    sp.dma_start(sums[:, :, :], g.sums[:, bass.ds(i * STRIP, STRIP), :]).then_inc(loaded, 16)
                    sp.wait_ge(normed, i + 1)
                    sp.dma_start(strip_of(g.out, i), out[:, :, :]).then_inc(stored, 16)
                sp.wait_ge(stored, 16 * STRIPS)

            @block.scalar
            def _(act):
                with act.Fori(0, STRIPS) as i:
                    act.wait_ge(to_act, i + 1)
                    if first:
                        nc.scalar.activation(sq[:, :, :], sq[:, :, :], ACT.Exp).then_inc(from_act, 1)
                    else:
                        nc.scalar.activation(st[:, 2, :], st[:, 1, :], ACT.Sqrt).then_inc(from_act, 1)

            @block.vector
            def _(dve):
                links = 3 + 1 if first else 4 + NORM_LINKS
                dve.wait_ge(consts, 16)
                with dve.Fori(0, STRIPS) as i:
                    link = Chain(dve, chain, i * links)
                    dve.wait_ge(loaded, i * 32 + 32)
                    s4 = sums[:, :, :].rearrange("p t (h c) -> p (t h) c", h=heads)
                    link(dve.reciprocal(rw[:, :], s4[:, :, hc:hc + 1].rearrange("p h c -> p (h c)")))
                    link(dve.tensor_tensor(y[:, :, :].rearrange("p t (h c) -> p (t h) c", h=heads),
                                           s4[:, :, 0:hc], last(rw[:, :], hc), ALU.mult))
                    link(dve.tensor_tensor(y[:, :, :], y[:, :, :], mid(b[:, :], STRIP), ALU.add))

                    def act_link(ins):
                        ins.then_inc(to_act, 1)
                        dve.wait_ge(from_act, i + 1)
                    if first:
                        act_link(dve.tensor_scalar(sq[:, :, :], y[:, :, :], 0.0, None, ALU.min))
                        link(dve.scalar_tensor_tensor(out=y[:, :, :], in0=y[:, :, :], scalar=0.0,
                                                      in1=sq[:, :, :], op0=ALU.max, op1=ALU.add))
                        dve.wait_ge(stored, i * 16)
                        dve.tensor_scalar(out[:, :, :], y[:, :, :], -1.0, None, ALU.add).then_inc(normed, 1)
                    else:
                        link(dve.tensor_tensor(y[:, :, :], y[:, :, :], x[:, :, :], ALU.add))
                        dve.wait_ge(stored, i * 16)
                        normalize(link, act_link, dve, y[:, :, :], sq[:, :, :], st, out[:, :, :]).then_inc(normed, 1)
                    assert link.n == links, link.n


def sage_layers(nc, a, k, out_dram):
    with ExitStack() as ctx:
        m = Memory(nc, ctx, "sage")
        parts = m.sb("parts", [P, 2, 3, TILES, D], BF16)
        split_features(nc, k.x3, parts[:, 0], "sage_split")
        ewT_all = m.sb("ewT_all", [FE + 1, LAYERS, D], F32)
        ewT = m.sb("ewT", [FE + 1, 2, D], F32)
        w, b = m.sb("w", [P, 2, D], F32), m.sb("b", [P, 2, D], F32)
        edges = m.sb("edges", [FE + 1, SW], F32)
        aggT = m.sb("aggT", [P, SW], F32)
        y = m.sb("y", [P, STRIP, D], F32)
        ew = flat(y[:, :, :])[:, 0:LAYERS * FE].rearrange("p (l f) -> p l f", f=FE)
        st = m.sb("st", [P, 3, STRIP], F32)
        spare = parts[:, 1].rearrange("p s t f -> p (s t f)").bitcast(F32)
        x, sq, out = (spare[:, n * SW:(n + 1) * SW].rearrange("p (t f) -> p t f", f=D) for n in range(3))
        pA = m.ps("pA", [P, 2, 2 * BANK])
        pO = m.ps("pO", [P, 2 * BANK])
        pW = m.ps("pW", [FE, LAYERS, D])
        loaded, ew_in, ew_turned, ew_ready, edges_in = (
            m.sem(n) for n in ("loaded", "ew_in", "ew_turned", "ew_ready", "edges_in"))
        agg, aggT_ready, lin, y_ready = (m.sem(n) for n in ("agg", "aggT_ready", "lin", "y_ready"))
        ew_slot = m.sem("ew_slot")
        high, rest, middle, low = (m.sem(n) for n in ("high", "rest", "middle", "low"))
        x_in, chain, var, std, normed, stored = (
            m.sem(n) for n in ("x_in", "chain", "var", "std", "normed", "stored"))

        def layers(eng, fn):
            with eng.Fori(0, LAYERS // 2) as u:
                fn(u * 2, 0, False)
                fn(u * 2 + 1, 1, False)
            fn(LAYERS - 1, 0, True)

        with nc.Block() as block:
            @block.sync
            def _(sp):
                with nc.allow_non_contiguous_dma(reason="rows of 64 bytes"):
                    sp.dma_start(ew, a["ews"].rearrange("l d f -> d l f")).then_inc(ew_in, 16)
                sp.dma_start(ewT_all[FE:FE + 1, :, :], a["ebs"].rearrange("(a l) d -> a l d", a=1)).then_inc(ew_in, 16)

                def one(l, par, is_last):
                    at = bass.ds(l, 1)
                    sp.dma_start(w[:, par, :], a["Ws"][at].rearrange("a f d -> (a f) d")).then_inc(loaded, 16)
                    sp.dma_start(b[:, par, :], a["bs"][at].rearrange("a d -> (a d)").partition_broadcast(P)
                                 ).then_inc(loaded, 16)
                    for i in range(STRIPS):
                        sp.wait_ge(agg, l * STRIPS + i)
                        sp.dma_start(edges[:, :], k.edgeT[:, i * SW:(i + 1) * SW]).then_inc(edges_in, 16)
                        if is_last:
                            sp.wait_ge(normed, i)
                            sp.dma_start(x, strip_of(k.x3, i)).then_inc(x_in, 16)
                            if i:
                                sp.dma_start(strip_of(out_dram, i - 1), out).then_inc(stored, 16)
                layers(sp, one)
                sp.wait_ge(normed, STRIPS)
                sp.dma_start(strip_of(out_dram, STRIPS - 1), out).then_inc(stored, 16)
                sp.wait_ge(stored, 16 * STRIPS)

            @block.gpsimd
            def _(pool):
                pool.wait_ge(ew_ready, 1)
                for l in range(LAYERS):
                    if l > 1:
                        pool.wait_ge(agg, (l - 1) * STRIPS)
                    pool.tensor_copy(ewT[:, l % 2, :], ewT_all[:, l, :]).then_inc(ew_slot, 1)

            @block.tensor
            def _(pe):
                def linear(l, par, i):
                    it = l * STRIPS + i
                    pe.wait_ge(aggT_ready, it + 1)
                    pe.wait_ge(y_ready, it)
                    for c in range(STRIP):
                        ins = pe.matmul(pO[:, c * P:(c + 1) * P], aggT[:, c * P:(c + 1) * P], w[:, par, :],
                                        start=True, stop=True)
                    ins.then_inc(lin, 1)

                def one(l, par, is_last):
                    pe.wait_ge(loaded, l * 32 + 32)
                    for i in range(STRIPS):
                        if i > 1:
                            pe.wait_ge(aggT_ready, l * STRIPS + (i - 1))

                        def features_ready(s):
                            if i == 0:
                                pe.wait_ge(low, l * STRIPS + s + 1)
                                pe.nop(nofuse=True)

                        def edge_terms():
                            if i == 0:
                                pe.wait_ge(ew_slot, l + 1)
                            pe.wait_ge(edges_in, (l * STRIPS + i) * 16 + 16)
                            for lo, hi in halves(SW):
                                pe.matmul(pA[:, i % 2, lo:hi], ewT[:, par, :], edges[:, lo:hi], start=False, stop=False, skip_group_check=True)
                        aggregate_strip(pe, pA[:, i % 2], k, parts[:, par], i, features_ready,
                                        edge_terms).then_inc(agg, 1)
                        if i:
                            linear(l, par, i - 1)
                    linear(l, par, STRIPS - 1)
                pe.wait_ge(ew_in, 32)
                for l in range(LAYERS):
                    ins = pe.transpose(pW[:, l, :], ew[:, l, :], k.ident[:, :])
                ins.then_inc(ew_turned, 1)
                layers(pe, one)

            @block.scalar
            def _(act):
                def one(l, par, is_last):
                    def split(i):
                        it = l * STRIPS + i
                        if is_last:
                            act.wait_ge(var, i + 1)
                            nc.scalar.activation(st[:, 2, :], st[:, 1, :], ACT.Sqrt).then_inc(std, 1)
                            return
                        act.wait_ge(y_ready, it + 1)
                        nc.scalar.activation(parts[:, 1 - par, 0, i * STRIP:(i + 1) * STRIP, :], y[:, :, :],
                                             ACT.Relu).then_inc(high, 1)
                        act.wait_ge(rest, it + 1)
                        nc.scalar.activation(parts[:, 1 - par, 1, i * STRIP:(i + 1) * STRIP, :], y[:, :, :],
                                             ACT.Copy).then_inc(middle, 1)

                    for i in range(STRIPS):
                        it = l * STRIPS + i
                        act.wait_ge(agg, it + 1)
                        act.wait_ge(lin, it)
                        nc.scalar.activation(aggT[:, :], pA[:, i % 2, 0:SW], ACT.Copy).then_inc(aggT_ready, 1)
                        if i:
                            split(i - 1)
                    split(STRIPS - 1)
                layers(act, one)

            @block.vector
            def _(dve):
                links = 1 + NORM_LINKS

                def one(l, par, is_last):
                    for i in range(STRIPS):
                        it = l * STRIPS + i
                        dve.wait_ge(lin, it + 1)
                        dve.wait_ge(low, (l + 1) * STRIPS if is_last else it + STRIPS)
                        if is_last:
                            dve.wait_ge(normed, i)
                        for c in range(STRIP):
                            ins = dve.scalar_tensor_tensor(
                                out=y[:, c, :], in0=pO[:, c * D:(c + 1) * D],
                                scalar=k.rdeg[:, i * STRIP + c:i * STRIP + c + 1], in1=b[:, par, :],
                                op0=ALU.mult, op1=ALU.add)
                        ins.then_inc(y_ready, 1)
                        if is_last:
                            link = Chain(dve, chain, i * links)
                            dve.wait_ge(y_ready, it + 1)
                            dve.wait_ge(x_in, i * 16 + 16)
                            link(dve.tensor_tensor(y[:, :, :], y[:, :, :], x, ALU.add))

                            def act_link(ins):
                                ins.then_inc(var, 1)
                                dve.wait_ge(std, i + 1)
                            if i:
                                dve.wait_ge(stored, i * 16)
                            normalize(link, act_link, dve, y[:, :, :], sq, st, out).then_inc(normed, 1)
                            assert link.n == links, link.n
                            continue
                        dve.wait_ge(high, it + 1)
                        dve.scalar_tensor_tensor(out=y[:, :, :], in0=y[:, :, :], scalar=0.0,
                                                 in1=parts[:, 1 - par, 0, i * STRIP:(i + 1) * STRIP, :],
                                                 op0=ALU.max, op1=ALU.subtract).then_inc(rest, 1)
                        dve.wait_ge(middle, it + 1)
                        dve.tensor_tensor(parts[:, 1 - par, 2, i * STRIP:(i + 1) * STRIP, :], y[:, :, :],
                                          parts[:, 1 - par, 1, i * STRIP:(i + 1) * STRIP, :],
                                          ALU.subtract).then_inc(low, 1)
                dve.sem_inc(low, STRIPS)
                dve.wait_ge(ew_turned, 1)
                dve.tensor_copy(ewT_all[0:FE, :, :], pW[:, :, :]).then_inc(ew_ready, 1)
                layers(dve, one)


def attention_layer(nc, a, k, n, heads, x_dram, out_dram):
    class G:
        pass

    g = G()
    g.n, g.heads, g.x, g.out = n, heads, x_dram, out_dram
    g.table = nc.dram_tensor(f"table{n}", [P, TILES, D + heads], F32).ap()
    g.sums = nc.dram_tensor(f"att_sums{n}", [P, TILES, D + heads], F32).ap()
    g.src_rows = nc.dram_tensor(f"src_rows{n}", [heads, NP], F32).ap()
    g.dst_row = nc.dram_tensor(f"dst_row{n}", [heads, NP], F32).ap()
    g.dst_rows = [nc.dram_tensor(f"dst_rows{n}{x}", [heads, NP], F32).ap() for x in (0, 1)]
    with ExitStack() as ctx:
        m = Memory(nc, ctx, f"att{n}")
        g.att = m.sb("att", [P, 5, TILES * heads], F32)
        gat_linear(nc, a, k, g)
        source_bound(nc, k, g)
        if n == 2:
            turn_counts(nc, k, "turn_back", wide_only=True)
        store_rows(nc, k, g, [(0, g.src_rows)], f"srows{n}", True)
        gat_max(nc, k, g)
        turn_counts(nc, k, f"turn{n}", wide_only=n == 2)
        target_shares(nc, k, g)
        if n == 1:
            store_rows(nc, k, g, [(1, g.dst_row)], f"drow{n}", False)
            branch_sums(nc, k, g)
        always = None if n == 2 else True
        store_rows(nc, k, g, [(2, g.dst_rows[0]), (3, g.dst_rows[1])], f"drows{n}", always)
        gat_sums(nc, k, g, always)
        gat_nodes(nc, a, k, g)


def program(nc, a, out):
    class K:
        pass

    k = K()
    with ExitStack() as ctx:
        m = Memory(nc, ctx, "k")
        k.ranges_dram = nc.dram_tensor("ranges_dram", [TILES, 2], I32).ap()
        k.sums_dram = nc.dram_tensor("sums_dram", [TILES, P, AGG], F32).ap()
        k.edgeT = nc.dram_tensor("edgeT", [FE + 1, NP], F32).ap()
        k.x1, k.x2, k.h, k.x3 = (nc.dram_tensor(n, [NP, D], F32).ap() for n in ("x1", "x2", "h", "x3"))
        k.ident = m.sb("ident", [P, P], F32)
        k.zeros = m.sb("zeros", [P, P], BF16)
        k.rdeg = m.sb("rdeg", [P, TILES], F32)
        k.wide = m.sb("wide", [1, 1], I32)
        k.top = m.sb("top", [P, 4], F32)
        k.made = m.sem("made")
        k.C = m.sb("C", [P, TILES, NP], BF16)
        with ExitStack() as edge:
            me = Memory(nc, edge, "e")
            k.iota = me.sb("iota", [P, CW], I16)
            k.tile_base = me.sb("tile_base", [P, TILES], F32)
            k.table = {n: me.sb(f"table_{n}", [P, CHUNKS], F32) for n in ("src", "dst", "w")}
            k.src_i = me.sb("src_i", [P, CHUNKS], I32)
            k.ranges = me.sb("ranges", [1, 2 * TILES], I32)
            edge_tables(nc, a, k)
            build_counts(nc, a, k)
        gin_nodes(nc, a, k)
        mean_layer(nc, a, k)
        attention_layer(nc, a, k, 1, HEADS, k.x2, k.h)
        attention_layer(nc, a, k, 2, 1, k.h, k.x3)
        sage_layers(nc, a, k, out)


def kernel(x, src, dst, edge_attr_16, edge_weight, L0_gnn_W1, L0_gnn_b1, L0_gnn_W2, L0_gnn_b2, L0_gnn_eps,
           L1_gnn_W1, L1_gnn_b1, L1_gnn_W2, L1_gnn_b2, L2_gnn_W1, L2_gnn_att_src1, L2_gnn_att_dst1, L2_gnn_b1,
           L2_gnn_W2, L2_gnn_att_src2, L2_gnn_att_dst2, L2_gnn_b2, L3_gnn_Ws, L3_gnn_bs, L3_gnn_ews, L3_gnn_ebs):
    import numpy as np
    from concourse import bacc
    from concourse.bass_utils import run_bass_kernel_spmd

    def padded(v, n, fill=0):
        v = np.asarray(v)
        return np.concatenate([v, np.full((n - v.shape[0],) + v.shape[1:], fill, v.dtype)])

    arrays = {
        "x": padded(x, NP),
        "src": padded(src, E_PAD),
        "dst": padded(dst, E_PAD, NO_NODE),
        "w": padded(edge_weight, E_PAD),
        "edge_attr": padded(edge_attr_16, E_PAD),
        "w1_0": L0_gnn_W1, "b1_0": L0_gnn_b1, "w2_0": L0_gnn_W2, "b2_0": L0_gnn_b2, "eps": L0_gnn_eps,
        "w1_1": L1_gnn_W1, "b1_1": L1_gnn_b1, "w2_1": L1_gnn_W2, "b2_1": L1_gnn_b2,
        "w1_2": L2_gnn_W1, "b1_2": L2_gnn_b1, "att_src1": L2_gnn_att_src1, "att_dst1": L2_gnn_att_dst1,
        "w2_2": L2_gnn_W2, "b2_2": L2_gnn_b2, "att_src2": L2_gnn_att_src2, "att_dst2": L2_gnn_att_dst2,
        "Ws": L3_gnn_Ws, "bs": L3_gnn_bs, "ews": L3_gnn_ews, "ebs": L3_gnn_ebs,
    }
    arrays = {n: np.ascontiguousarray(v) for n, v in arrays.items()}
    nc = bacc.Bacc("TRN2", target_bir_lowering=False, num_devices=1)
    a = {n: nc.dram_tensor(f"in_{n}", v.shape, mybir.dt.from_np(v.dtype), kind="ExternalInput").ap()
         for n, v in arrays.items()}
    out = nc.dram_tensor("out", [NP, D], F32, kind="ExternalOutput").ap()
    program(nc, a, out)
    r = run_bass_kernel_spmd(nc, [{f"in_{n}": v for n, v in arrays.items()}], core_ids=[0])
    return r.results[0]["out"][:N_NODES]
```

```python
from contextlib import ExitStack, contextmanager

import concourse.bass as bass
from concourse import mybir

F32 = mybir.dt.float32
BF16 = mybir.dt.bfloat16
I16 = mybir.dt.int16
I32 = mybir.dt.int32
ALU = mybir.AluOpType
ACT = mybir.ActivationFunctionType
AX_X = mybir.AxisListType.X

P = 128
N_NODES = 3125
N_EDGES = 103125
D = 128
FE = 16
TILES = -(-N_NODES // P)
NP = TILES * P
STRIP = 5
STRIPS = TILES // STRIP
SW = STRIP * P
BANK = 512
CPG = 4
GROUPS = -(-N_EDGES // (CPG * P))
CHUNKS = GROUPS * CPG
E_PAD = CHUNKS * P
NO_NODE = 4095
CB = 448
CBANKS = 7
CW = CB * CBANKS
AGG = D + FE + 1
HEADS = 8
HC = D // HEADS
LAYERS = 5
LN_EPS = 1e-5
SLOPE = 0.2
FAR = 1.0e30
BIG = 3.0e38
SPREAD = 60.0
HALVES = ((0, 4), (4, CBANKS))
PERIOD = 6
DIRECT = 2
V_PARTS = ((0, 7), (7, 13), (13, 19), (19, 25))


assert CW >= N_NODES and TILES % STRIP == 0 and 2 * P >= GROUPS > P


class Memory:

    def __init__(self, nc, ctx, phase):
        self.nc, self.ctx, self.phase, self.sems = nc, ctx, phase, []
        ctx.push(self.free_sems)

    def sb(self, name, shape, dtype):
        return self.ctx.enter_context(self.nc.sbuf_tensor(f"{self.phase}_{name}", shape, dtype))

    def ps(self, name, shape, dtype=F32):
        return self.ctx.enter_context(self.nc.psum_tensor(f"{self.phase}_{name}", shape, dtype))

    def sem(self, name):
        self.sems.append(self.nc.alloc_semaphore(f"{self.phase}_{name}"))
        return self.sems[-1]

    def free_sems(self, error, *_):
        if self.sems and not error:
            self.nc.clear_and_free_semaphores(self.sems)
            with self.nc.Block():
                pass


class Chain:

    def __init__(self, eng, sem, before=0):
        self.eng, self.sem, self.n, self.before = eng, sem, 0, before

    def __call__(self, ins):
        self.n += 1
        ins.then_inc(self.sem, 1)
        self.eng.wait_ge(self.sem, self.before + self.n)


@contextmanager
def on_path(eng, k, wide):
    if wide is None:
        yield
        return
    spread = eng.value_load(k.wide[0:1, 0:1], min_val=0, max_val=1)
    with eng.If(spread > 0 if wide else spread < 1):
        yield


def mid(row, n):
    p, w = row.shape
    return row.unsqueeze(1).broadcast_to([p, n, w])


def last(cols, n):
    p, k = cols.shape
    return cols.unsqueeze(2).broadcast_to([p, k, n])


def halves(w):
    return [(0, BANK), (BANK, w)]


def edge_tables(nc, a, k):
    with ExitStack() as ctx:
        m = Memory(nc, ctx, "tab")
        names = ("src", "dst", "w")
        low = P
        high = GROUPS - P
        raw = {(n, h): m.sb(f"raw_{n}{h}", [P, CPG * P], F32 if n == "w" else I32)
               for n in names for h in (0, 1)}
        val = {(n, h): m.sb(f"val_{n}{h}", [P, CPG * P], F32) for n in names[:2] for h in (0, 1)}
        val.update({("w", h): raw["w", h] for h in (0, 1)})
        ext = m.sb("ext", [P, 4], F32)
        grp = m.sb("grp", [TILES, GROUPS], F32)
        t_lo = m.sb("t_lo", [TILES, 1], F32)
        t_hi = m.sb("t_hi", [TILES, 1], F32)
        c0 = m.sb("c0", [TILES, GROUPS], F32)
        c1 = m.sb("c1", [TILES, GROUPS], F32)
        c2 = m.sb("c2", [TILES, GROUPS], F32)
        lohi = m.sb("lohi", [TILES, 2], F32)
        lohi_i = m.sb("lohi_i", [TILES, 2], I32)
        pT = m.ps("pT", [P, 6, BANK])
        pG = m.ps("pG", [TILES, 2, 256])
        loaded, iotas, cast = m.sem("loaded"), m.sem("iotas"), m.sem("cast")
        turned, rows_done = m.sem("turned"), m.sem("rows_done")
        chain, ranges, moved = m.sem("chain"), m.sem("ranges"), m.sem("moved")
        size = [low, high]
        with nc.Block() as block:
            @block.sync
            def _(sp):
                for n in names:
                    rows = a[n].rearrange("(g e) -> g e", e=CPG * P)
                    sp.dma_start(raw[n, 0][:, :], rows[0:low]).then_inc(loaded, 16)
                    sp.dma_start(raw[n, 1][0:high, :], rows[low:GROUPS]).then_inc(loaded, 16)
                sp.wait_ge(ranges, 1)
                sp.dma_start(k.ranges_dram, lohi_i[:, :]).then_inc(moved, 16)
                sp.wait_ge(moved, 16)
                sp.dma_start(k.ranges[:, 0:2 * TILES], k.ranges_dram.rearrange("t k -> (t k)")
                             .rearrange("(a n) -> a n", a=1)).then_inc(moved, 16)
                sp.wait_ge(moved, 32)

            @block.gpsimd
            def _(pool):
                pool.memset(k.ident[:, :], 0.0).then_inc(k.made, 1)
                pool.wait_ge(k.made, 1)
                pool.affine_select(out=k.ident[:, :], in_=k.ident[:, :], compare_op=ALU.not_equal,
                                   fill=1.0, base=0, pattern=[[-1, P]], channel_multiplier=1).then_inc(k.made, 1)
                pool.iota(k.iota[:, :], [[1, CW]], base=0, channel_multiplier=0,
                          allow_small_or_imprecise_dtypes=True)
                pool.iota(k.tile_base[:, :], [[P, TILES + 1]], base=0, channel_multiplier=0,
                          allow_small_or_imprecise_dtypes=True)
                pool.iota(grp[:, :], [[1, GROUPS]], base=0, channel_multiplier=0,
                          allow_small_or_imprecise_dtypes=True)
                pool.iota(t_lo[:, :], [[1, 1]], base=0, channel_multiplier=P,
                          allow_small_or_imprecise_dtypes=True)
                pool.iota(t_hi[:, :], [[1, 1]], base=P - 1, channel_multiplier=P,
                          allow_small_or_imprecise_dtypes=True).then_inc(iotas, 1)

            @block.vector
            def _(dve):
                dve.memset(k.zeros[:, :], 0.0)
                dve.memset(k.ranges[:, 2 * TILES:2 * TILES + 1], 0)
                dve.wait_ge(loaded, 16 * 6)
                for n in names[:2]:
                    for h in (0, 1):
                        dve.tensor_copy(val[n, h][0:size[h], :], raw[n, h][0:size[h], :]).then_inc(cast, 1)
                dve.wait_ge(cast, 4)
                for h in (0, 1):
                    v = val["dst", h][0:size[h], :]
                    dve.tensor_reduce(ext[0:size[h], 2 * h:2 * h + 1], v, AX_X, ALU.min)
                    dve.tensor_reduce(ext[0:size[h], 2 * h + 1:2 * h + 2], v, AX_X, ALU.max).then_inc(cast, 1)
                link = Chain(dve, chain)
                dve.wait_ge(iotas, 1)
                dve.wait_ge(rows_done, 1)
                link(dve.tensor_scalar(c0[:, :], pG[:, 0, 0:GROUPS], t_hi[:, :], None, ALU.is_le))
                link(dve.scalar_tensor_tensor(out=c1[:, :], in0=pG[:, 1, 0:GROUPS], scalar=t_lo[:, :],
                                              in1=c0[:, :], op0=ALU.is_ge, op1=ALU.mult))
                link(dve.scalar_tensor_tensor(out=c0[:, :], in0=grp[:, :], scalar=1.0, in1=c1[:, :],
                                              op0=ALU.add, op1=ALU.mult))
                link(dve.scalar_tensor_tensor(out=c2[:, :], in0=grp[:, :], scalar=float(GROUPS), in1=c1[:, :],
                                              op0=ALU.subtract, op1=ALU.mult))
                link(dve.tensor_reduce(lohi[:, 1:2], c0[:, :], AX_X, ALU.max))
                link(dve.tensor_reduce(lohi[:, 0:1], c2[:, :], AX_X, ALU.min))
                link(dve.tensor_scalar(lohi[:, 1:2], lohi[:, 1:2], 2.0, None, ALU.max))
                link(dve.tensor_scalar(c2[:, 0:1], lohi[:, 1:2], -2.0, None, ALU.add))
                link(dve.scalar_tensor_tensor(out=lohi[:, 0:1], in0=lohi[:, 0:1], scalar=float(GROUPS),
                                              in1=c2[:, 0:1], op0=ALU.add, op1=ALU.min))
                dve.tensor_copy(lohi_i[:, :], lohi[:, :]).then_inc(ranges, 1)
                for i, (n, h) in enumerate([(n, h) for n in names for h in (0, 1)]):
                    dve.wait_ge(turned, i + 1)
                    s = size[h]
                    dst = k.table[n][:, :].rearrange("p (g q) -> p g q", q=CPG)[:, low * h:low * h + s, :]
                    dve.tensor_copy(dst, pT[:, i, 0:CPG * s].rearrange("p (q g) -> p g q", q=CPG)).then_inc(cast, 1)
                dve.wait_ge(cast, 12)
                dve.tensor_copy(k.src_i[:, :], k.table["src"][:, :])

            @block.tensor
            def _(pe):
                pe.wait_ge(k.made, 2)
                pe.wait_ge(cast, 6)
                for h in (0, 1):
                    s = size[h]
                    for j in (0, 1):
                        ins = pe.matmul(pG[:, j, low * h:low * h + s],
                                        ext[0:s, 2 * h + j:2 * h + j + 1].broadcast_to([s, TILES]),
                                        k.ident[0:s, 0:s], start=(h == 0 and j == 0), stop=True,
                                        skip_group_check=True)
                ins.then_inc(rows_done, 1)
                for i, (n, h) in enumerate([(n, h) for n in names for h in (0, 1)]):
                    s = size[h]
                    for q in range(CPG):
                        ins = pe.transpose(pT[:, i, q * s:(q + 1) * s], val[n, h][0:s, q * P:(q + 1) * P],
                                           k.ident[0:s, 0:s])
                    ins.then_inc(turned, 1)


def build_counts(nc, a, k):
    with ExitStack() as ctx:
        m = Memory(nc, ctx, "cnt")
        rows = m.sb("rows", [P, CPG, D], F32)
        row_idx = m.sb("row_idx", [P, CPG], I32)
        src_hot = m.sb("src_hot", [P, 2, CW], BF16)
        dst_hot = m.sb("dst_hot", [P, CPG, P], BF16)
        dst_hot32 = m.sb("dst_hot32", [P, CPG, P], F32)
        msg = m.sb("msg", [P, CPG, AGG], F32)
        stage = m.sb("stage", [P, AGG], F32)
        acc = m.ps("acc", [P, 8, BANK])
        rows_free, idx_ready = m.sem("rows_free"), m.sem("idx_ready")
        rows_in = [m.sem(f"rows_in{q}") for q in range(CPG)]
        feat_in = [m.sem(f"feat_in{q}") for q in range(CPG)]
        hot_ready, msg_ready = m.sem("hot_ready"), m.sem("msg_ready")
        chunks_done = m.sem("chunks_done")
        dve_out, act_out, stored = m.sem("dve_out"), m.sem("act_out"), m.sem("stored")
        ones_set = m.sem("ones_set")

        def tile_range(eng, t):
            return (eng.value_load(k.ranges[0:1, bass.ds(t * 2, 1)], min_val=0, max_val=GROUPS - 2),
                    eng.value_load(k.ranges[0:1, bass.ds(t * 2 + 1, 1)], min_val=2, max_val=GROUPS))

        def counter(eng, name):
            r = eng.alloc_register(name)
            eng.reg_mov(r, 0)
            return r

        with nc.Block() as block:
            @block.gpsimd
            def _(pool):
                n = counter(pool, "pool_chunks")
                with pool.Fori(0, TILES) as t:
                    lo, hi = tile_range(pool, t)
                    with pool.Fori(lo, hi) as g:
                        c = pool.snap(n)
                        for q in range(CPG):
                            pool.wait_ge(rows_free, c + (q + 1))
                            pool.tensor_copy(row_idx[:, q:q + 1],
                                             k.src_i[:, bass.ds(g * CPG + q, 1)]).then_inc(idx_ready, 1)
                            pool.wait_ge(idx_ready, c + (q + 1))
                            pool.nop(nofuse=True)
                            pool.indirect_dma_start(rows[:, q, :], None, a["x"],
                                                    bass.IndirectOffsetOnAxis(ap=row_idx[:, q:q + 1], axis=0)
                                                    ).then_inc(rows_in[q], 16)
                        pool.reg_add(n, n, CPG)

            @block.sync
            def _(sp):
                sp.sem_inc(stored, 16)
                n = counter(sp, "sp_chunks")
                feats = a["edge_attr"].rearrange("(c p) f -> c p f", p=P)

                def load(g, c):
                    for q in range(CPG):
                        sp.wait_ge(chunks_done, c + (q + 1))
                        sp.dma_start(msg[:, q, D:D + FE], feats[bass.ds(g * CPG + q, 1), :, :]
                                     .rearrange("a p f -> (a p) f")).then_inc(feat_in[q], 16)

                load(sp.value_load(k.ranges[0:1, 0:1], min_val=0, max_val=GROUPS - 2), 0)
                with sp.Fori(0, TILES) as t:
                    lo, hi = tile_range(sp, t)
                    sp.reg_add(n, n, CPG)
                    with sp.Fori(lo + 1, hi) as g:
                        load(g, sp.snap(n))
                        sp.reg_add(n, n, CPG)
                    after = sp.value_load(k.ranges[0:1, bass.ds(t * 2 + 2, 1)], min_val=0, max_val=GROUPS - 2)
                    load(after, sp.snap(n))
                    sp.wait_ge(act_out, t * 4 + 8)
                    sp.dma_start(k.sums_dram[bass.ds(t, 1), :, :].rearrange("a p f -> (a p) f"),
                                 stage[:, :]).then_inc(stored, 16)
                sp.wait_ge(stored, 16 * TILES + 16)
                for q in range(CPG):
                    sp.wait_ge(feat_in[q], (sp.snap(n) + CPG) * (16 // CPG))
                sp.nop(nofuse=True)

            @block.vector
            def _(dve):
                dve.memset(msg[:, :, AGG - 1:AGG], 1.0).then_inc(ones_set, 1)
                dve.memset(k.C[:, :, CW:NP], 0.0)
                dve.sem_inc(dve_out, 4)
                n = counter(dve, "dve_chunks")

                def hots(t, g, q, c):
                    dve.wait_ge(chunks_done, c + (q + CPG - 1))
                    dve.tensor_scalar(dst_hot[:, q, :], k.iota[:, 0:P], k.tile_base[:, bass.ds(t, 1)],
                                      k.table["dst"][:, bass.ds(g * CPG + q, 1)], ALU.add, ALU.is_equal)
                    dve.tensor_scalar(src_hot[:, q % 2, :], k.iota[:, :],
                                      k.table["src"][:, bass.ds(g * CPG + q, 1)], None,
                                      ALU.is_equal).then_inc(hot_ready, 1)

                hots(0, dve.value_load(k.ranges[0:1, 0:1], min_val=0, max_val=GROUPS - 2), 0, 0)
                with dve.Fori(0, TILES) as t:
                    lo, hi = tile_range(dve, t)
                    c = dve.snap(n)
                    for q in range(1, CPG):
                        hots(t, lo, q, c)
                    dve.reg_add(n, n, CPG)
                    with dve.Fori(lo + 1, hi) as g:
                        c = dve.snap(n)
                        for q in range(CPG):
                            hots(t, g, q, c)
                        dve.reg_add(n, n, CPG)
                    after = dve.value_load(k.ranges[0:1, bass.ds(t * 2 + 2, 1)], min_val=0, max_val=GROUPS - 2)
                    hots(t + 1, after, 0, dve.snap(n))
                    dve.wait_ge(chunks_done, dve.snap(n) + CPG)
                    for b in range(4):
                        dve.tensor_copy(k.C[:, bass.ds(t, 1), b * CB:(b + 1) * CB].rearrange("p a n -> p (a n)"),
                                        acc[:, b, 0:CB]).then_inc(dve_out, 1)

            @block.scalar
            def _(act):
                nc.scalar.activation(stage[:, 0:1], k.tile_base[:, 0:1], ACT.Copy)
                act.sem_inc(rows_free, CPG)
                act.sem_inc(act_out, 4)
                n = counter(act, "act_chunks")
                with act.Fori(0, TILES) as t:
                    lo, hi = tile_range(act, t)
                    with act.Fori(lo, hi) as g:
                        c = act.snap(n)
                        for q in range(CPG):
                            act.wait_ge(chunks_done, c + (q + 1))
                            act.wait_ge(rows_in[q], (c + CPG) * (16 // CPG))
                            nc.scalar.activation(msg[:, q, 0:D], rows[:, q, :], ACT.Copy,
                                                 scale=k.table["w"][:, bass.ds(g * CPG + q, 1)]
                                                 ).then_inc(rows_free, 1)
                            act.wait_ge(hot_ready, c + (q + 1))
                            nc.scalar.activation(dst_hot32[:, q, :], dst_hot[:, q, :],
                                                 ACT.Copy).then_inc(msg_ready, 1)
                        act.reg_add(n, n, CPG)
                    act.wait_ge(chunks_done, act.snap(n) + CPG)
                    for b in range(4, CBANKS):
                        nc.scalar.activation(k.C[:, bass.ds(t, 1), b * CB:(b + 1) * CB].rearrange("p a n -> p (a n)"),
                                             acc[:, b, 0:CB], ACT.Copy).then_inc(act_out, 1)
                    act.wait_ge(stored, t * 16 + 16)
                    nc.scalar.activation(stage[:, :], acc[:, 7, 0:AGG], ACT.Copy).then_inc(act_out, 1)

            @block.tensor
            def _(pe):
                pe.sem_inc(chunks_done, CPG)
                n = counter(pe, "pe_chunks")
                pe.wait_ge(ones_set, 1)

                def group(t, c, first):
                    for q in range(CPG):
                        begins = first and q == 0
                        pe.wait_ge(hot_ready, c + (q + 1))
                        for b in (0, 4, 1, 5, 2, 6, 3):
                            if begins:
                                pe.wait_ge(*((dve_out, t * 4 + (b + 1)) if b < 4 else (act_out, t * 4 + (b - 3))))
                            pe.matmul(acc[:, b, 0:CB], dst_hot[:, q, :],
                                      src_hot[:, q % 2, b * CB:(b + 1) * CB], start=begins, stop=False,
                                      skip_group_check=True)
                        pe.wait_ge(msg_ready, c + (q + 1))
                        pe.wait_ge(feat_in[q], (c + CPG) * (16 // CPG))
                        if begins:
                            pe.wait_ge(act_out, t * 4 + 4)
                        pe.matmul(acc[:, 7, 0:AGG], dst_hot32[:, q, :], msg[:, q, :], start=begins, stop=False,
                                  skip_group_check=True).then_inc(chunks_done, 1)

                with pe.Fori(0, TILES) as t:
                    lo, hi = tile_range(pe, t)
                    group(t, pe.snap(n), True)
                    pe.reg_add(n, n, CPG)
                    with pe.Fori(lo + 1, hi) as g:
                        group(t, pe.snap(n), False)
                        pe.reg_add(n, n, CPG)


def strip_of(dram, i):
    return dram.rearrange("(s t p) f -> s p t f", t=STRIP, p=P)[bass.ds(i, 1)].rearrange("a p t f -> p (a t) f")


def flat(ap):
    return ap.rearrange("p t f -> p (t f)")


def normalize(link, act_link, dve, y, sq, st, out):
    link(dve.tensor_reduce(st[:, 0, :], y, AX_X, ALU.add))
    link(dve.tensor_scalar(st[:, 0, :], st[:, 0, :], 1.0 / D, None, ALU.mult))
    link(dve.tensor_tensor(y, y, last(st[:, 0, :], D), ALU.subtract))
    link(dve.tensor_tensor(sq, y, y, ALU.mult))
    link(dve.tensor_reduce(st[:, 1, :], sq, AX_X, ALU.add))
    act_link(dve.tensor_scalar(st[:, 1, :], st[:, 1, :], 1.0 / D, LN_EPS, ALU.mult, ALU.add))
    link(dve.reciprocal(st[:, 2, :], st[:, 2, :]))
    return dve.tensor_tensor(out, y, last(st[:, 2, :], D), ALU.mult)


NORM_LINKS = 6


def gin_nodes(nc, a, k, parts):
    with ExitStack() as ctx:
        m = Memory(nc, ctx, "gin")
        w1, w2 = m.sb("w1", [P, D], F32), m.sb("w2", [P, D], F32)
        b1, b2 = m.sb("b1", [P, 1], F32), m.sb("b2", [P, D], F32)
        eps = m.sb("eps", [P, 1], F32)
        x, sums = m.sb("x", [P, 2, STRIP, D], F32), m.sb("sums", [P, STRIP, AGG], F32)
        v, y, sq, out, rest = (m.sb(n, [P, STRIP, D], F32) for n in ("v", "y", "sq", "out", "rest"))
        vT, hT = m.sb("vT", [P, SW], F32), m.sb("hT", [P, SW], F32)
        eT = m.sb("eT", [FE + 1, SW], F32)
        st = m.sb("st", [P, 3, STRIP], F32)
        pV, pH, pO, pE = (m.ps(n, [P, 2 * BANK]) for n in ("pV", "pH", "pO", "pE"))
        consts, one_eps, sums_in, rdeg_ready = (m.sem(n) for n in ("consts", "one_eps", "sums_in", "rdeg_ready"))
        x_in = [m.sem(f"x_in{s}") for s in (0, 1)]
        v_ready, turned, vT_ready = m.sem("v_ready"), m.sem("turned"), m.sem("vT_ready")
        h_ready, hT_ready, o_ready, added = m.sem("h_ready"), m.sem("hT_ready"), m.sem("o_ready"), m.sem("added")
        eT_ready, var, std = m.sem("eT_ready"), m.sem("var"), m.sem("std")
        chain, normed, stored, e_stored, split = (
            m.sem(n) for n in ("chain", "normed", "stored", "e_stored", "split"))
        with nc.Block() as block:
            @block.sync
            def _(sp):
                def load_x(i):
                    sp.dma_start(x[:, i % 2], strip_of(a["x"], i)).then_inc(x_in[i % 2], 16)

                def load_sums(i):
                    sp.dma_start(sums[:, :, :], strip_of(k.sums_dram.rearrange("t p f -> (t p) f"), i)
                                 ).then_inc(sums_in, 16)

                load_x(0)
                load_sums(0)
                sp.dma_start(eps[:, :], a["eps"].partition_broadcast(P)).then_inc(consts, 16)
                sp.dma_start(w1[:, :], a["w1_0"]).then_inc(consts, 16)
                sp.dma_start(w2[:, :], a["w2_0"]).then_inc(consts, 16)
                with nc.allow_non_contiguous_dma(reason="one value per partition"):
                    sp.dma_start(b1[:, :], a["b1_0"].rearrange("(d a) -> d a", a=1)).then_inc(consts, 16)
                sp.dma_start(b2[:, :], a["b2_0"].partition_broadcast(P)).then_inc(consts, 16)
                load_x(1)
                for i in range(STRIPS):
                    if i + 1 < STRIPS:
                        sp.wait_ge(turned, i + 1)
                        sp.wait_ge(rdeg_ready, i + 1)
                        load_sums(i + 1)
                    sp.wait_ge(eT_ready, i + 1)
                    sp.dma_start(k.edgeT[:, i * SW:(i + 1) * SW], eT[:, :]).then_inc(e_stored, 16)
                    if i + 2 < STRIPS:
                        sp.wait_ge(added, i + 1)
                        load_x(i + 2)
                    sp.wait_ge(normed, i + 1)
                    sp.dma_start(strip_of(k.x1, i), out[:, :, :]).then_inc(stored, 16)
                sp.wait_ge(stored, 16 * STRIPS)
                sp.wait_ge(e_stored, 16 * STRIPS)

            @block.gpsimd
            def _(pool):
                for i in range(STRIPS):
                    pool.wait_ge(normed, i + 1)
                    split_strip(pool, split, out, rest, parts, i)

            @block.vector
            def _(dve):
                def start(i):
                    dve.wait_ge(sums_in, i * 16 + 16)
                    dve.wait_ge(x_in[i % 2], (i // 2 + 1) * 16)
                    if i:
                        dve.wait_ge(turned, i)
                    dve.scalar_tensor_tensor(out=v[:, :, :], in0=x[:, i % 2], scalar=eps[:, :],
                                             in1=sums[:, :, 0:D], op0=ALU.mult, op1=ALU.add)
                    dve.tensor_scalar(sums[:, :, AGG - 1:AGG], sums[:, :, AGG - 1:AGG], 1.0, None,
                                      ALU.add).then_inc(v_ready, 1)
                    dve.wait_ge(v_ready, i + 1)
                    dve.reciprocal(k.rdeg[:, i * STRIP:(i + 1) * STRIP],
                                   sums[:, :, AGG - 1:AGG].rearrange("p t f -> p (t f)")).then_inc(rdeg_ready, 1)

                def finish(i):
                    link = Chain(dve, chain, i * (NORM_LINKS + 1))
                    dve.wait_ge(o_ready, i + 1)
                    if i:
                        dve.wait_ge(normed, i)
                    link(dve.tensor_tensor(y[:, :, :], pO[:, 0:SW].rearrange("p (t f) -> p t f", f=D),
                                           mid(b2[:, :], STRIP), ALU.add))
                    dve.scalar_tensor_tensor(out=y[:, :, :], in0=y[:, :, :], scalar=0.0, in1=x[:, i % 2],
                                             op0=ALU.max, op1=ALU.add).then_inc(added, 1)
                    dve.wait_ge(added, i + 1)

                    def act_link(ins):
                        ins.then_inc(var, 1)
                        dve.wait_ge(std, i + 1)
                    if i:
                        dve.wait_ge(stored, i * 16)
                        dve.wait_ge(split, i * SPLIT_STEPS)
                    normalize(link, act_link, dve, y[:, :, :], sq[:, :, :], st, out[:, :, :]).then_inc(normed, 1)

                dve.wait_ge(consts, 16 * 5)
                dve.tensor_scalar(eps[:, :], eps[:, :], 1.0, None, ALU.add).then_inc(one_eps, 1)
                dve.wait_ge(one_eps, 1)
                start(0)
                for i in range(STRIPS):
                    if i + 1 < STRIPS:
                        start(i + 1)
                    finish(i)

            @block.scalar
            def _(act):
                def turn_out(i):
                    act.wait_ge(turned, i + 1)
                    if i:
                        act.wait_ge(h_ready, i)
                    nc.scalar.activation(vT[:, :], pV[:, 0:SW], ACT.Copy).then_inc(vT_ready, 1)
                    if i:
                        act.wait_ge(e_stored, i * 16)
                    nc.scalar.activation(eT[:, :], pE[0:FE + 1, 0:SW], ACT.Copy).then_inc(eT_ready, 1)

                act.wait_ge(consts, 16 * 5)

                def hidden(i):
                    act.wait_ge(h_ready, i + 1)
                    if i:
                        act.wait_ge(o_ready, i)
                    nc.scalar.activation(hT[:, :], pH[:, 0:SW], ACT.Relu, bias=b1[:, :]).then_inc(hT_ready, 1)

                turn_out(0)
                hidden(0)
                turn_out(1)
                for i in range(STRIPS):
                    if i + 1 < STRIPS:
                        hidden(i + 1)
                    act.wait_ge(var, i + 1)
                    nc.scalar.activation(st[:, 2, :], st[:, 1, :], ACT.Sqrt).then_inc(std, 1)
                    if i + 2 < STRIPS:
                        turn_out(i + 2)

            @block.tensor
            def _(pe):
                def turn(i):
                    pe.wait_ge(v_ready, i + 1)
                    if i:
                        pe.wait_ge(vT_ready, i)
                        pe.wait_ge(eT_ready, i)
                    for c in range(STRIP):
                        pe.transpose(pV[:, c * P:(c + 1) * P], v[:, c, :], k.ident[:, :])
                    for c in range(STRIP):
                        ins = pe.transpose(pE[0:FE + 1, c * P:(c + 1) * P], sums[:, c, D:AGG], k.ident[:, :])
                    ins.then_inc(turned, 1)

                pe.wait_ge(consts, 16 * 5)
                turn(0)
                for i in range(STRIPS):
                    pe.wait_ge(vT_ready, i + 1)
                    if i:
                        pe.wait_ge(hT_ready, i)
                    for lo, hi in halves(SW):
                        ins = pe.matmul(pH[:, lo:hi], w1[:, :], vT[:, lo:hi], start=True, stop=True)
                    ins.then_inc(h_ready, 1)
                    pe.wait_ge(hT_ready, i + 1)
                    if i:
                        pe.wait_ge(added, i)
                    for c in range(STRIP):
                        ins = pe.matmul(pO[:, c * P:(c + 1) * P], hT[:, c * P:(c + 1) * P], w2[:, :],
                                        start=True, stop=True)
                    ins.then_inc(o_ready, 1)
                    if i + 1 < STRIPS:
                        turn(i + 1)


SPLIT_STEPS = 4


def split_strip(pool, done, x, rest, parts, i):
    link = Chain(pool, done, i * SPLIT_STEPS)
    at = slice(i * STRIP, (i + 1) * STRIP)
    link(pool.tensor_copy(parts[:, 0, at, :], x[:, :, :]))
    link(pool.tensor_tensor(rest[:, :, :], x[:, :, :], parts[:, 0, at, :], ALU.subtract))
    link(pool.tensor_copy(parts[:, 1, at, :], rest[:, :, :]))
    link(pool.tensor_tensor(parts[:, 2, at, :], rest[:, :, :], parts[:, 1, at, :], ALU.subtract))
    assert link.n == SPLIT_STEPS


def aggregate_strip(pe, pA, k, parts, i, features_ready=None, edge_terms=None):
    for lo, _ in halves(SW):
        pe.matmul(pA[:, lo:lo + 1], k.zeros[:, 0:P], k.zeros[:, 0:1], start=True, stop=False,
                  skip_group_check=True)
    with pe.Fori(0, STRIPS) as s:
        if features_ready:
            features_ready(s)
        for t in range(STRIP):
            for part in range(3):
                for lo, hi in halves(SW):
                    ins = pe.matmul(pA[:, lo:hi],
                                    parts[:, part, bass.ds(s * STRIP + t, 1), :].rearrange("p a f -> p (a f)"),
                                    k.C[:, bass.ds(s * STRIP + t, 1), bass.ds(i * SW + lo, hi - lo)]
                                    .rearrange("p a n -> p (a n)"),
                                    start=False, stop=False, skip_group_check=True)
    if edge_terms:
        edge_terms()
    return pe.matmul(pA[:, 0:1], k.zeros[:, 0:P], k.zeros[:, 0:1], start=False, stop=True,
                     skip_group_check=True)


def mean_layer(nc, a, k, parts):
    with ExitStack() as ctx:
        m = Memory(nc, ctx, "mean")
        wT = m.sb("wT", [P, 2, D], F32)
        b1, b2 = m.sb("b1", [P, 1], F32), m.sb("b2", [P, D], F32)
        rdeg = m.sb("rdeg", [P, NP], F32)
        ones = m.sb("ones", [P, P], BF16)
        x, y, sq, out = (m.sb(n, [P, STRIP, D], F32) for n in ("x", "y", "sq", "out"))
        w = sq[:, 0:2, :]
        aggT, hT = m.sb("aggT", [P, SW], F32), m.sb("hT", [P, SW], F32)
        st = m.sb("st", [P, 3, STRIP], F32)
        banks = m.ps("banks", [P, 8, BANK])
        pA = [banks[:, 2 * n:2 * n + 2, :].rearrange("p b n -> p (b n)") for n in (0, 1)]
        pB, pC = (banks[:, n:n + 2, :].rearrange("p b n -> p (b n)") for n in (4, 6))
        consts, loaded, w_turned, w_ready = (m.sem(n) for n in ("consts", "loaded", "w_turned", "w_ready"))
        ones_set, deg, deg_out, rdeg_ready = (m.sem(n) for n in ("ones_set", "deg", "deg_out", "rdeg_ready"))
        agg, aggT_ready, p1, hT_ready, p2, added = (
            m.sem(n) for n in ("agg", "aggT_ready", "p1", "hT_ready", "p2", "added"))
        chain, var, std, normed, stored = (m.sem(n) for n in ("chain", "var", "std", "normed", "stored"))
        with nc.Block() as block:
            @block.sync
            def _(sp):
                for j in (0, 1):
                    sp.dma_start(w[:, j, :], a[f"w{j + 1}_1"]).then_inc(consts, 16)
                with nc.allow_non_contiguous_dma(reason="one value per partition"):
                    sp.dma_start(b1[:, :], a["b1_1"].rearrange("(d a) -> d a", a=1)).then_inc(consts, 16)
                sp.dma_start(b2[:, :], a["b2_1"].partition_broadcast(P)).then_inc(consts, 16)
                sp.dma_start(x[:, :, :], strip_of(k.x1, 0)).then_inc(loaded, 16)
                for i in range(STRIPS):
                    if i + 1 < STRIPS:
                        sp.wait_ge(added, i + 1)
                        sp.dma_start(x[:, :, :], strip_of(k.x1, i + 1)).then_inc(loaded, 16)
                    sp.wait_ge(normed, i + 1)
                    sp.dma_start(strip_of(k.x2, i), out[:, :, :]).then_inc(stored, 16)
                sp.wait_ge(stored, 16 * STRIPS)

            @block.vector
            def _(dve):
                def mean(i):
                    dve.wait_ge(agg, i + 1)
                    if i:
                        dve.wait_ge(p1, i)
                    dve.tensor_tensor(aggT[:, :], pA[i % 2][:, 0:SW], rdeg[:, i * SW:(i + 1) * SW],
                                      ALU.mult).then_inc(aggT_ready, 1)

                def finish(i):
                    link = Chain(dve, chain, i * (1 + NORM_LINKS))
                    dve.wait_ge(p2, i + 1)
                    if i:
                        dve.wait_ge(normed, i)
                    dve.wait_ge(loaded, i * 16 + 16)
                    link(dve.tensor_tensor(y[:, :, :], pC[:, 0:SW].rearrange("p (t f) -> p t f", f=D),
                                           mid(b2[:, :], STRIP), ALU.add))
                    dve.tensor_tensor(y[:, :, :], y[:, :, :], x[:, :, :], ALU.add).then_inc(added, 1)
                    dve.wait_ge(added, i + 1)

                    def act_link(ins):
                        ins.then_inc(var, 1)
                        dve.wait_ge(std, i + 1)
                    if i:
                        dve.wait_ge(stored, i * 16)
                    normalize(link, act_link, dve, y[:, :, :], sq[:, :, :], st, out[:, :, :]).then_inc(normed, 1)
                    assert link.n == 1 + NORM_LINKS, link.n

                dve.memset(ones[:, :], 1.0).then_inc(ones_set, 1)
                dve.memset(rdeg[:, CW:NP], 1.0)
                dve.wait_ge(w_turned, 1)
                dve.tensor_copy(wT[:, :, :], banks[:, 7, 0:2 * D].rearrange("p (j f) -> p j f", j=2)
                                ).then_inc(w_ready, 1)
                dve.wait_ge(deg, 1)
                dve.tensor_scalar(rdeg[:, 0:CW].rearrange("p (b n) -> p b n", n=CB), banks[:, 0:CBANKS, 0:CB],
                                  1.0, None, ALU.max).then_inc(deg_out, 1)
                dve.wait_ge(deg_out, 1)
                dve.reciprocal(rdeg[:, 0:CW], rdeg[:, 0:CW]).then_inc(rdeg_ready, 1)
                dve.wait_ge(rdeg_ready, 1)
                dve.wait_ge(consts, 16 * 4)
                mean(0)
                for i in range(STRIPS):
                    if i + 1 < STRIPS:
                        mean(i + 1)
                    finish(i)

            @block.gpsimd
            def _(pool):
                pool.wait_ge(agg, STRIPS)
                with pool.Fori(0, TILES) as t:
                    diag = k.C[:, bass.ds(t, 1), bass.ds(t * P, P)].rearrange("p a n -> p (a n)")
                    pool.tensor_tensor(diag, diag, k.ident[:, :], ALU.add)

            @block.scalar
            def _(act):
                def root(i):
                    act.wait_ge(var, i + 1)
                    nc.scalar.activation(st[:, 2, :], st[:, 1, :], ACT.Sqrt).then_inc(std, 1)

                act.wait_ge(consts, 16 * 4)
                for i in range(STRIPS):
                    act.wait_ge(p1, i + 1)
                    if i:
                        act.wait_ge(p2, i)
                    nc.scalar.activation(hT[:, :], pB[:, 0:SW], ACT.Relu, bias=b1[:, :]).then_inc(hT_ready, 1)
                    if i:
                        root(i - 1)
                root(STRIPS - 1)

            @block.tensor
            def _(pe):
                pe.wait_ge(consts, 16 * 4)
                for j in (0, 1):
                    ins = pe.transpose(banks[:, 7, j * D:(j + 1) * D], w[:, j, :], k.ident[:, :])
                ins.then_inc(w_turned, 1)
                pe.wait_ge(ones_set, 1)
                for b in range(CBANKS):
                    pe.matmul(banks[:, b, 0:1], k.zeros[:, 0:P], k.zeros[:, 0:1], start=True, stop=False,
                              skip_group_check=True)
                with pe.Fori(0, TILES) as t:
                    for b in range(CBANKS):
                        pe.matmul(banks[:, b, 0:CB], ones[:, :],
                                  k.C[:, bass.ds(t, 1), b * CB:(b + 1) * CB].rearrange("p a n -> p (a n)"),
                                  start=False, stop=False, skip_group_check=True)
                pe.matmul(banks[:, 0, 0:1], k.zeros[:, 0:P], k.zeros[:, 0:1], start=False, stop=True,
                          skip_group_check=True).then_inc(deg, 1)
                pe.wait_ge(w_ready, 1)
                pe.wait_ge(deg_out, 1)

                def first(i):
                    pe.wait_ge(aggT_ready, i + 1)
                    if i:
                        pe.wait_ge(hT_ready, i)
                    for lo, hi in halves(SW):
                        ins = pe.matmul(pB[:, lo:hi], wT[:, 0, :], aggT[:, lo:hi], start=True, stop=True)
                    ins.then_inc(p1, 1)

                def second(i):
                    pe.wait_ge(hT_ready, i + 1)
                    if i:
                        pe.wait_ge(added, i)
                    for c in range(STRIP):
                        ins = pe.matmul(pC[:, c * P:(c + 1) * P], hT[:, c * P:(c + 1) * P], wT[:, 1, :],
                                        start=True, stop=True)
                    ins.then_inc(p2, 1)

                for i in range(STRIPS):
                    if i > 1:
                        pe.wait_ge(aggT_ready, i - 1)
                    aggregate_strip(pe, pA[i % 2], k, parts, i).then_inc(agg, 1)
                    if i:
                        first(i - 1)
                        second(i - 1)
                first(STRIPS - 1)
                second(STRIPS - 1)


def gat_linear(nc, a, k, g):
    heads, hc = g.heads, D // g.heads
    with ExitStack() as ctx:
        m = Memory(nc, ctx, f"lin{g.n}")
        w = m.sb("w", [P, D], F32)
        att = m.sb("att", [P, 2, D], F32)
        x = m.sb("x", [P, 2, STRIP, D], F32)
        xT = m.sb("xT", [P, 2, SW], F32)
        tab = m.sb("tab", [P, 2, STRIP, heads, hc + 1], F32)
        prod = m.sb("prod", [P, 2, STRIP, D], F32)
        pT, pX = m.ps("pT", [P, 2, 2 * BANK]), m.ps("pX", [P, 2, 2 * BANK])
        consts, ones_set, turned, xT_ready, xh, tab_ready, terms, chain = (
            m.sem(n) for n in ("consts", "ones_set", "turned", "xT_ready", "xh", "tab_ready", "terms", "chain"))
        loaded, stored = ([m.sem(f"{n}{s}") for s in (0, 1)] for n in ("loaded", "stored"))
        with nc.Block() as block:
            @block.sync
            def _(sp):
                def load(i):
                    if i > 1:
                        sp.wait_ge(turned, i - 1)
                    sp.dma_start(x[:, i % 2], strip_of(g.x, i)).then_inc(loaded[i % 2], 16)

                load(0)
                sp.dma_start(w[:, :], a[f"w{g.n}_2"]).then_inc(consts, 16)
                for j, n in enumerate(("att_src", "att_dst")):
                    sp.dma_start(att[:, j, :], a[f"{n}{g.n}"].rearrange("h c -> (h c)").partition_broadcast(P)
                                 ).then_inc(consts, 16)
                load(1)
                for i in range(STRIPS):
                    if i + 2 < STRIPS:
                        load(i + 2)
                    sp.wait_ge(tab_ready, i + 1)
                    sp.dma_start(g.table[:, i * STRIP:(i + 1) * STRIP, :],
                                 tab[:, i % 2].rearrange("p t h c -> p t (h c)")).then_inc(stored[i % 2], 16)
                for s in (0, 1):
                    sp.wait_ge(stored[s], 16 * len(range(s, STRIPS, 2)))

            @block.scalar
            def _(act):
                def turn_out(i):
                    act.wait_ge(turned, i + 1)
                    if i > 1:
                        act.wait_ge(xh, i - 1)
                    nc.scalar.activation(xT[:, i % 2, :], pT[:, i % 2, 0:SW], ACT.Copy).then_inc(xT_ready, 1)

                act.wait_ge(ones_set, 1)
                turn_out(0)
                for i in range(STRIPS):
                    if i + 1 < STRIPS:
                        turn_out(i + 1)
                    act.wait_ge(xh, i + 1)
                    if i > 1:
                        act.wait_ge(stored[i % 2], i // 2 * 16)
                    for c in range(STRIP):
                        ins = nc.scalar.activation(tab[:, i % 2, c, :, 0:hc], pX[:, i % 2, c * D:(c + 1) * D]
                                                   .rearrange("p (h c) -> p h c", h=heads), ACT.Copy)
                    ins.then_inc(tab_ready, 1)

            @block.vector
            def _(dve):
                dve.memset(tab[:, :, :, :, hc:hc + 1], 1.0).then_inc(ones_set, 1)
                dve.wait_ge(consts, 16 * 3)
                for i in range(STRIPS):
                    at = slice(i * STRIP * heads, (i + 1) * STRIP * heads)
                    dve.wait_ge(tab_ready, i + 1)
                    link = Chain(dve, chain, i * 3)
                    for j in (0, 1):
                        link(dve.tensor_tensor(prod[:, j, :, :], pX[:, i % 2, 0:SW].rearrange("p (t f) -> p t f", f=D),
                                               mid(att[:, j, :], STRIP), ALU.mult))
                    for j in (0, 1):
                        ins = dve.tensor_reduce(g.att[:, j, at], prod[:, j, :, :]
                                                .rearrange("p t (h c) -> p (t h) c", h=heads), AX_X, ALU.add)
                    link(ins)
                    dve.tensor_scalar(g.att[:, 4, at], g.att[:, 0, at], SLOPE, None, ALU.mult).then_inc(terms, 1)

            @block.tensor
            def _(pe):
                def turn(i):
                    pe.wait_ge(loaded[i % 2], (i // 2 + 1) * 16)
                    if i > 1:
                        pe.wait_ge(xT_ready, i - 1)
                    for c in range(STRIP):
                        ins = pe.transpose(pT[:, i % 2, c * P:(c + 1) * P], x[:, i % 2, c, :], k.ident[:, :])
                    ins.then_inc(turned, 1)

                turn(0)
                pe.wait_ge(consts, 16 * 3)
                for i in range(STRIPS):
                    if i + 1 < STRIPS:
                        turn(i + 1)
                    pe.wait_ge(xT_ready, i + 1)
                    if i > 1:
                        pe.wait_ge(tab_ready, i - 1)
                        pe.wait_ge(terms, i - 1)
                    for c in range(STRIP):
                        ins = pe.matmul(pX[:, i % 2, c * D:(c + 1) * D], xT[:, i % 2, c * P:(c + 1) * P], w[:, :],
                                        start=True, stop=True)
                    ins.then_inc(xh, 1)


def store_rows(nc, k, g, shares, tag, path):
    heads = g.heads
    with ExitStack() as ctx:
        m = Memory(nc, ctx, tag)
        rows = m.sb("rows", [TILES, len(shares), heads, P], F32)
        pT = m.ps("pT", [TILES, len(shares), 2 * BANK])
        turned, ready, stored = m.sem("turned"), m.sem("ready"), m.sem("stored")
        with nc.Block() as block:
            @block.tensor
            def _(pe):
                with on_path(pe, k, path):
                    for i, (j, _) in enumerate(shares):
                        by_head = g.att[:, j, :].rearrange("p (t h) -> p h t", h=heads)
                        for h in range(heads):
                            ins = pe.transpose(pT[:, i, h * P:(h + 1) * P], by_head[:, h, :], k.ident[:, :])
                    ins.then_inc(turned, 1)

            @block.scalar
            def _(act):
                with on_path(act, k, path):
                    act.wait_ge(turned, 1)
                    for i in range(len(shares)):
                        nc.scalar.activation(rows[:, i, :, :].rearrange("t h p -> t (h p)"),
                                             pT[:, i, 0:heads * P], ACT.Copy).then_inc(ready, 1)

            @block.sync
            def _(sp):
                with on_path(sp, k, path):
                    for i, (_, dram) in enumerate(shares):
                        sp.wait_ge(ready, i + 1)
                        sp.dma_start(dram.rearrange("h (t p) -> t h p", p=P), rows[:, i, :, :]).then_inc(stored, 16)
                    sp.wait_ge(stored, 16 * len(shares))


def gat_max(nc, k, g):
    heads = g.heads
    with ExitStack() as ctx:
        m = Memory(nc, ctx, f"max{g.n}")
        row = m.sb("row", [P, NP], F32)
        far = m.sb("far", [P, 2, NP], BF16)
        scratch = m.ps("scratch", [P, NP])
        bias = m.sb("bias", [P, 1], F32)
        one = m.sb("one", [P, 1], F32)
        bias_set, loaded, far_ready, far_used, kept = (
            m.sem(n) for n in ("bias_set", "loaded", "far_ready", "far_used", "kept"))
        with nc.Block() as block:
            @block.sync
            def _(sp):
                with on_path(sp, k, True):
                    with sp.Fori(0, heads) as h:
                        sp.wait_ge(far_used, h * TILES + 1)
                        sp.dma_start(row[:, :], g.src_rows[bass.ds(h, 1), :].rearrange("a n -> (a n)")
                                     .partition_broadcast(P)).then_inc(loaded, 16)

            @block.scalar
            def _(act):
                with on_path(act, k, True):
                    act.wait_ge(bias_set, 1)

                    def mask(n, t, slot):
                        nc.scalar.activation(far[:, slot, :], k.C[:, bass.ds(t, 1), :].rearrange("p a n -> p (a n)"),
                                             ACT.Relu, bias=bias[:, :], scale=-FAR).then_inc(far_ready, 1)

                    with act.Fori(0, heads) as h:
                        with act.Fori(0, TILES // 2) as u:
                            for s in (0, 1):
                                n = h * TILES + u * 2 + s
                                if s == 0:
                                    act.wait_ge(far_used, n + 1)
                                else:
                                    act.wait_ge(far_used, h * TILES + u * 2 + 1)
                                mask(n, u * 2 + s, s)
                        act.wait_ge(far_used, h * TILES + TILES)
                        mask(None, TILES - 1, 0)

            @block.vector
            def _(dve):
                with on_path(dve, k, True):
                    dve.memset(bias[:, :], FAR).then_inc(bias_set, 1)
                    dve.sem_inc(far_used, 1)
                    dve.sem_inc(kept, 1)

                    def greatest(n, h, t, slot):
                        dve.wait_ge(far_ready, n + 1)
                        dve.wait_ge(kept, n + 1)
                        dve.nop(nofuse=True)
                        dve.tensor_tensor_reduce(scratch[:, :], row[:, :], far[:, slot, :], 1.0, -BIG,
                                                 ALU.subtract, ALU.max, one[:, :]).then_inc(far_used, 1)
                        dve.wait_ge(far_used, n + 2)
                        dve.tensor_copy(g.att[:, 2, bass.ds(t * heads + h, 1)], one[:, :]).then_inc(kept, 1)

                    with dve.Fori(0, heads) as h:
                        dve.wait_ge(loaded, h * 16 + 16)
                        dve.nop(nofuse=True)
                        with dve.Fori(0, TILES // 2) as u:
                            for s in (0, 1):
                                greatest(h * TILES + u * 2 + s, h, u * 2 + s, s)
                        greatest(h * TILES + (TILES - 1), h, TILES - 1, 0)


def target_shares(nc, k, g):
    with ExitStack() as ctx:
        m = Memory(nc, ctx, f"shares{g.n}")
        z = m.sb("z", [P, 2, TILES * g.heads], F32)
        chain = m.sem("chain")
        with nc.Block() as block:
            @block.vector
            def _(dve):
                link = Chain(dve, chain)
                link(dve.tensor_tensor(z[:, 0, :], g.att[:, 2, :], g.att[:, 1, :], ALU.add))
                link(dve.scalar_tensor_tensor(out=z[:, 1, :], in0=z[:, 0, :], scalar=SLOPE, in1=z[:, 0, :],
                                              op0=ALU.mult, op1=ALU.max))
                dve.tensor_tensor(g.att[:, 2, :], g.att[:, 1, :], z[:, 1, :], ALU.subtract)
                dve.scalar_tensor_tensor(out=g.att[:, 3, :], in0=g.att[:, 1, :], scalar=SLOPE, in1=z[:, 1, :],
                                         op0=ALU.mult, op1=ALU.subtract)


def source_bound(nc, k, g):
    with ExitStack() as ctx:
        m = Memory(nc, ctx, f"bound{g.n}")
        ends = m.sb("ends", [P, 2], F32)
        end = m.sb("end", [1, 3], F32)
        ones = m.sb("ones", [1, P], F32)
        pT, pB = m.ps("pT", [1, 2, P]), m.ps("pB", [P, 1])
        chain, ends_ready, turned, end_ready, spread = (
            m.sem(n) for n in ("chain", "ends_ready", "turned", "end_ready", "spread"))
        with nc.Block() as block:
            @block.vector
            def _(dve):
                link = Chain(dve, chain)
                dve.memset(ones[:, :], 1.0)
                dve.tensor_reduce(ends[:, 0:1], g.att[:, 0, :], AX_X, ALU.max)
                link(dve.tensor_reduce(ends[:, 1:2], g.att[:, 0, :], AX_X, ALU.min))
                dve.tensor_scalar(ends[:, 1:2], ends[:, 1:2], -1.0, None, ALU.mult).then_inc(ends_ready, 1)
                dve.wait_ge(turned, 1)
                dve.tensor_reduce(end[:, 0:2], pT[:, :, :], AX_X, ALU.max).then_inc(end_ready, 1)
                dve.wait_ge(end_ready, 1)
                link(dve.tensor_tensor(end[:, 2:3], end[:, 0:1], end[:, 1:2], ALU.add))
                dve.tensor_scalar(k.wide[:, :], end[:, 2:3], SPREAD, None, ALU.is_gt)
                dve.wait_ge(spread, 1)
                for j, scale in enumerate((1.0, SLOPE, -1.0, -SLOPE)):
                    dve.tensor_scalar(k.top[:, j:j + 1], pB[:, :], scale, None, ALU.mult)
                dve.tensor_copy(g.att[:, 2, :], pB[:, 0:1].broadcast_to([P, TILES * g.heads]))

            @block.tensor
            def _(pe):
                pe.wait_ge(ends_ready, 1)
                for j in (0, 1):
                    ins = pe.transpose(pT[:, j, :], ends[:, j:j + 1], k.ident[:, :])
                ins.then_inc(turned, 1)
                pe.wait_ge(end_ready, 1)
                pe.matmul(pB[:, :], ones[:, :], end[:, 0:1], start=True, stop=True).then_inc(spread, 1)


def turn_counts(nc, k, tag, wide_only=False):
    with ExitStack() as ctx:
        m = Memory(nc, ctx, tag)
        pI = m.ps("pI", [P, STRIP, 2 * BANK], BF16)
        identb = m.sb("identb", [P, P], BF16)
        made, turned, upper, lower = m.sem("made"), m.sem("turned"), m.sem("upper"), m.sem("lower")
        d_turned, d_put, d_put_act = m.sem("d_turned"), m.sem("d_put"), m.sem("d_put_act")

        def block_of(r, c):
            return k.C[:, bass.ds(r, 1), bass.ds(c * P, P)].rearrange("p a n -> p (a n)")

        pairs = [(x, y) for y in range(1, STRIPS) for x in range(y)]
        path = True if wide_only else None
        DVE_ROWS = 3

        def each_row(eng, n, fn):
            fn(0, n * STRIP, 0, n * STRIP + 1)
            with eng.Fori(0, STRIP // 2) as u:
                for r in (1, 2):
                    fn(u * 2 + r, u * 2 + (n * STRIP + r), r % 2, u * 2 + (n * STRIP + r))

        with nc.Block() as block:
            @block.vector
            def _(dve):
                with on_path(dve, k, path):
                    dve.tensor_copy(identb[:, :], k.ident[:, :]).then_inc(made, 1)
                    dve.sem_inc(upper, 1)
                    dve.sem_inc(d_put, 1)
                    for n, (x, y) in enumerate(pairs):
                        def row(r, step, slot, free):
                            dve.wait_ge(turned, step + 1)
                            dve.tensor_copy(k.C[:, y * STRIP:(y + 1) * STRIP, bass.ds((r + x * STRIP) * P, P)],
                                            pI[:, 2 * slot, 0:SW].rearrange("p (c n) -> p c n", n=P)
                                            ).then_inc(upper, 1)
                        each_row(dve, n, row)
                    with dve.Fori(0, STRIPS) as x:
                        dve.wait_ge(d_turned, x + 1)
                        for r in range(DVE_ROWS):
                            ins = dve.tensor_copy(k.C[:, bass.ds(x * STRIP + r, 1), bass.ds(x * SW, SW)]
                                                  .rearrange("p a n -> p (a n)"), pI[:, r, 0:SW])
                        ins.then_inc(d_put, 1)

            @block.scalar
            def _(act):
                with on_path(act, k, path):
                    act.sem_inc(lower, 1)
                    act.sem_inc(d_put_act, 1)
                    for n, (x, y) in enumerate(pairs):
                        def row(r, step, slot, free):
                            act.wait_ge(turned, step + 1)
                            nc.scalar.activation(k.C[:, bass.ds(r + x * STRIP, 1), y * SW:(y + 1) * SW]
                                                 .rearrange("p a n -> p (a n)"), pI[:, 2 * slot + 1, 0:SW],
                                                 ACT.Copy).then_inc(lower, 1)
                        each_row(act, n, row)
                    with act.Fori(0, STRIPS) as x:
                        act.wait_ge(d_turned, x + 1)
                        for r in range(DVE_ROWS, STRIP):
                            ins = nc.scalar.activation(k.C[:, bass.ds(x * STRIP + r, 1), bass.ds(x * SW, SW)]
                                                       .rearrange("p a n -> p (a n)"), pI[:, r, 0:SW], ACT.Copy)
                        ins.then_inc(d_put_act, 1)

            @block.tensor
            def _(pe):
                with on_path(pe, k, path):
                    pe.wait_ge(made, 1)
                    for n, (x, y) in enumerate(pairs):
                        def row(r, step, slot, free):
                            pe.wait_ge(upper, free)
                            pe.wait_ge(lower, free)
                            for c in range(STRIP):
                                pe.transpose(pI[:, 2 * slot, c * P:(c + 1) * P],
                                             block_of(r + x * STRIP, y * STRIP + c), identb[:, :])
                            for c in range(STRIP):
                                ins = pe.transpose(pI[:, 2 * slot + 1, c * P:(c + 1) * P],
                                                   block_of(y * STRIP + c, r + x * STRIP), identb[:, :])
                            ins.then_inc(turned, 1)
                        each_row(pe, n, row)
                    pe.wait_ge(upper, len(pairs) * STRIP + 1)
                    pe.wait_ge(lower, len(pairs) * STRIP + 1)
                    with pe.Fori(0, STRIPS) as x:
                        pe.wait_ge(d_put, x + 1)
                        pe.wait_ge(d_put_act, x + 1)
                        for r in range(STRIP):
                            for c in range(STRIP):
                                ins = pe.transpose(pI[:, r, c * P:(c + 1) * P],
                                                   block_of(x * STRIP + c, x * STRIP + r), identb[:, :])
                        ins.then_inc(d_turned, 1)


def gat_sums(nc, k, g, path):
    heads, w1 = g.heads, D // g.heads + 1
    per_bank = min(STRIP, BANK // w1)
    SLOTS = 5
    assert TILES % SLOTS == 0
    with ExitStack() as ctx:
        m = Memory(nc, ctx, f"sum{g.n}")
        tab = m.sb("tab", [P, TILES, w1], F32)
        shares = m.sb("shares", [P, 2, 2, SW], F32)
        e = m.sb("e", [P, SLOTS, 2, SW], F32)
        sums = m.sb("sums", [P, STRIP, w1], F32)
        acc = m.ps("acc", [P, 2, 2 * BANK])
        tab_in, stored = m.sem("tab_in"), m.sem("stored")
        shares_in = [[m.sem(f"shares_in{s}{x}") for x in (0, 1)] for s in (0, 1)]
        exps, larger, weights, steps_done, acc_ready, acc_out = (
            m.sem(n) for n in ("exps", "larger", "weights", "steps_done", "acc_ready", "acc_out"))

        def acc_tile(slot, c):
            at = (c // per_bank) * BANK + (c % per_bank) * w1
            return acc[:, slot, at:at + w1]

        def each_step(eng, fn, h, j):
            first = h * (STRIPS * TILES) + j * TILES
            with eng.Fori(0, TILES // SLOTS) as u:
                for s in range(SLOTS + len(fn) - 1):
                    for lag, f in enumerate(fn):
                        if 0 <= s - lag < SLOTS:
                            f(first + u * SLOTS + (s - lag), u * SLOTS + (s - lag), s - lag)

        def loads(h, j):
            return (h * (3 - j % 2) + (j // 2 + 1)) * 16

        with nc.Block() as block:
            @block.sync
            def _(sp):
                with on_path(sp, k, path):
                    def store(h, j):
                        sp.wait_ge(acc_out, h * STRIPS + (j + 2))
                        sp.dma_start(g.sums[:, j * STRIP:(j + 1) * STRIP, bass.ds(h * w1, w1)],
                                     sums[:, :, :]).then_inc(stored, 16)

                    with sp.Fori(0, heads) as h:
                        sp.wait_ge(steps_done, h * (STRIPS * TILES) + SLOTS)
                        sp.dma_start(tab[:, :, :], g.table[:, :, bass.ds(h * w1, w1)]).then_inc(tab_in, 16)
                        for j in range(STRIPS):
                            if j > 1:
                                sp.wait_ge(exps, h * (STRIPS * TILES) + (j - 1) * TILES)
                            for x in (0, 1):
                                row = g.dst_rows[x][bass.ds(h, 1), j * SW:(j + 1) * SW].rearrange("a n -> (a n)")
                                sp.dma_start(shares[:, j % 2, x, :], row.partition_broadcast(P)
                                             ).then_inc(shares_in[j % 2][x], 16)
                            if j:
                                store(h, j - 1)
                        store(h, STRIPS - 1)
                    sp.wait_ge(stored, 16 * heads * STRIPS)

            @block.scalar
            def _(act):
                with on_path(act, k, path):
                    with act.Fori(0, heads) as h:
                        for j in range(STRIPS):
                            for x in (0, 1):
                                act.wait_ge(shares_in[j % 2][x], loads(h, j))
                            act.nop(nofuse=True)

                            def step(n, s, slot):
                                act.wait_ge(steps_done, n + 1)
                                act.nop(nofuse=True)
                                for x, term in ((0, 0), (1, 4)):
                                    ins = nc.scalar.activation(e[:, slot, x, :], shares[:, j % 2, x, :], ACT.Exp,
                                                               bias=g.att[:, term, bass.ds(s * heads + h, 1)])
                                ins.then_inc(exps, 1)
                            each_step(act, [step], h, j)

            @block.vector
            def _(dve):
                with on_path(dve, k, path):
                    with dve.Fori(0, heads) as h:
                        for j in range(STRIPS):
                            def greater(n, s, slot):
                                dve.wait_ge(exps, n + 1)
                                dve.tensor_tensor(e[:, slot, 0, :], e[:, slot, 0, :], e[:, slot, 1, :],
                                                  ALU.max).then_inc(larger, 1)

                            def weight(n, s, slot):
                                dve.wait_ge(larger, n + 1)
                                dve.scalar_tensor_tensor(
                                    out=e[:, slot, 0, :], in0=e[:, slot, 0, :], scalar=BIG,
                                    in1=k.C[:, bass.ds(s, 1), j * SW:(j + 1) * SW].rearrange("p a n -> p (a n)"),
                                    op0=ALU.min, op1=ALU.mult).then_inc(weights, 1)
                            each_step(dve, [greater, weight], h, j)
                            dve.wait_ge(acc_ready, h * STRIPS + (j + 1))
                            if j:
                                dve.wait_ge(stored, h * (16 * STRIPS) + 16 * j)
                            for c in range(0, STRIP, per_bank):
                                c1 = min(STRIP, c + per_bank)
                                at = c // per_bank * BANK
                                ins = dve.tensor_copy(
                                    sums[:, c:c1, :],
                                    acc[:, j % 2, at:at + (c1 - c) * w1].rearrange("p (t c) -> p t c", c=w1))
                            ins.then_inc(acc_out, 1)
                        dve.wait_ge(stored, h * (16 * STRIPS) + 16 * STRIPS)

            @block.tensor
            def _(pe):
                with on_path(pe, k, path):
                    pe.sem_inc(steps_done, SLOTS)
                    pe.sem_inc(acc_out, 1)
                    with pe.Fori(0, heads) as h:
                        pe.wait_ge(tab_in, h * 16 + 16)
                        for j in range(STRIPS):
                            if j != 1:
                                pe.wait_ge(acc_out, h * STRIPS + max(1, j))
                            for x in range(-(-STRIP // per_bank)):
                                pe.matmul(acc[:, j % 2, x * BANK:x * BANK + 1], k.zeros[:, :], k.zeros[:, 0:1],
                                          start=True, stop=False, skip_group_check=True)

                            def step(n, s, slot):
                                pe.wait_ge(weights, n + 1)
                                for c in range(STRIP):
                                    ins = pe.matmul(acc_tile(j % 2, c), e[:, slot, 0, c * P:(c + 1) * P],
                                                    tab[:, bass.ds(s, 1), :].rearrange("p a c -> p (a c)"),
                                                    start=False, stop=False, skip_group_check=True)
                                ins.then_inc(steps_done, 1)
                            each_step(pe, [step], h, j)
                            pe.matmul(acc[:, j % 2, 0:1], k.zeros[:, :], k.zeros[:, 0:1], start=False, stop=True,
                                      skip_group_check=True).then_inc(acc_ready, 1)


def branch_sums(nc, k, g):
    heads, w1 = g.heads, D // g.heads + 1
    rows = 2 * 3 * w1
    GROUP = 2 * CB // P
    groups = [(n * GROUP, min(GROUP, TILES - n * GROUP)) for n in range(-(-TILES // GROUP))]
    with ExitStack() as ctx:
        m = Memory(nc, ctx, "branch")
        row = m.sb("row", [P, CW], F32)
        sign = m.sb("sign", [P, 2, CW], BF16)
        v = m.sb("v", [P, TILES, 4, 3, w1], BF16)
        rest = m.sb("rest", [P, V_PARTS[0][1], 2, w1], F32)
        tab = m.sb("tab", [P, TILES, w1], F32)
        src_part = m.sb("src_part", [P, 2, TILES * heads], F32)
        cols = sign[:, :, :].rearrange("p s n -> p (s n)").bitcast(F32)
        pick = m.sb("pick", [P, 2, w1], F32)
        prod = m.sb("prod", [P, GROUP, 2, w1], F32)
        sums = m.sb("sums", [P, TILES, w1], F32)
        acc = m.ps("acc", [P, CBANKS, BANK])
        turn_bank = m.ps("turn", [P, BANK])
        turn = [bank[:, 0:GROUP * 2 * w1].rearrange("p (t x c) -> p t x c", x=2, c=w1)
                for bank in (turn_bank, acc[:, 0, :])]
        row_in, tab_in, stored = [m.sem(f"row_in{x}") for x in (0, 1)], m.sem("tab_in"), m.sem("stored")
        exps, parts_ready, pick_ready, v_chain, v_ready = (
            m.sem(n) for n in ("exps", "parts_ready", "pick_ready", "v_chain", "v_ready"))
        signs, signed, halves_done = m.sem("signs"), m.sem("signed"), m.sem("halves_done")
        acc_ready, act_out, dve_out, turned, prods, added = (
            m.sem(n) for n in ("acc_ready", "act_out", "dve_out", "turned", "prods", "added"))

        periods = (TILES - 1) // PERIOD
        head_signs = 2 * (TILES - periods)
        assert 1 + periods * PERIOD == TILES and PERIOD % 2 == 0

        def each_tile(eng, h, fn):
            first = h * (2 * TILES)
            fn(first, h * head_signs, 0, 0, first + (2 * TILES - 1), None)
            with eng.Fori(0, periods) as u:
                for j in range(PERIOD):
                    n = first + u * (2 * PERIOD) + 2 * (1 + j)
                    by_act = h * head_signs + u * (2 * PERIOD - 2) + 2 * (1 + j - (j > DIRECT))
                    fn(n, by_act, u * PERIOD + (1 + j), (1 + j) % 2, n + (2 * TILES - 3), j)

        with nc.Block() as block:
            @block.sync
            def _(sp):
                with on_path(sp, k, False):
                    def load(h):
                        sp.wait_ge(v_ready, h * len(V_PARTS) + 1)
                        sp.dma_start(tab[:, :, :], g.table[:, :, bass.ds(h * w1, w1)]).then_inc(tab_in, 16)
                        for x, (lo, hi) in enumerate(HALVES):
                            sp.wait_ge(signs, h * head_signs + (x + 1))
                            sp.wait_ge(signed, h * (2 * TILES) + 2)
                            sp.dma_start(row[:, lo * CB:hi * CB], g.dst_row[bass.ds(h, 1), lo * CB:hi * CB]
                                         .rearrange("a n -> (a n)").partition_broadcast(P)).then_inc(row_in[x], 16)

                    def store(h):
                        sp.wait_ge(added, (h + 1) * len(groups))
                        sp.dma_start(g.sums[:, :, bass.ds(h * w1, w1)], sums[:, :, :]).then_inc(stored, 16)

                    sp.sem_inc(stored, 16)
                    load(0)
                    with sp.Fori(1, heads) as h:
                        load(h)
                        store(h - 1)
                    store(heads - 1)
                    sp.wait_ge(stored, 16 * heads + 16)

            @block.gpsimd
            def _(pool):
                with on_path(pool, k, False):
                    pool.sem_inc(v_ready, 1)
                    pool.wait_ge(parts_ready, 2)
                    with pool.Fori(0, heads) as h:
                        link = Chain(pool, v_chain, h * (len(V_PARTS) * 8))
                        pool.wait_ge(tab_in, h * 16 + 16)
                        for n, (lo, hi) in enumerate(V_PARTS):
                            pool.wait_ge(halves_done, h * (2 * TILES) + 2 * hi)
                            r = rest[:, 0:hi - lo]
                            for x in (0, 1):
                                share = src_part[:, x, :].rearrange("p (t h) -> p t h", h=heads)
                                share = share[:, lo:hi, bass.ds(h, 1)]
                                link(pool.tensor_tensor(r[:, :, x, :], tab[:, lo:hi, :],
                                                        share.broadcast_to([P, hi - lo, w1]), ALU.mult))
                            for part in (0, 1):
                                pool.nop(nofuse=True)
                                link(pool.tensor_copy(v[:, lo:hi, 0:2, part, :], r))
                                link(pool.tensor_tensor(r, r, v[:, lo:hi, 0:2, part, :], ALU.subtract))
                            pool.nop(nofuse=True)
                            link(pool.tensor_copy(v[:, lo:hi, 0:2, 2, :], r))
                            pool.nop(nofuse=True)
                            link(pool.tensor_copy(v[:, lo:hi, 2, :, :], v[:, lo:hi, 0, :, :]))
                            direct = 1 + n * PERIOD + DIRECT
                            assert lo <= direct < hi
                            pool.nop(nofuse=True)
                            pool.memset(v[:, direct, 0, :, :], 0.0)
                            pool.tensor_scalar(v[:, lo:hi, 3, :, :], v[:, lo:hi, 1, :, :], -1.0, None,
                                               ALU.mult).then_inc(v_ready, 1)

            @block.scalar
            def _(act):
                with on_path(act, k, False):
                    for x in (0, 1):
                        nc.scalar.activation(src_part[:, x, :], g.att[:, 4 * x, :], ACT.Exp, bias=k.top[:, 2 + x:3 + x])
                        ins = nc.scalar.activation(g.att[:, 2 + x, :], g.att[:, 2 + x, :], ACT.Exp,
                                                   bias=k.top[:, x:x + 1])
                    ins.then_inc(exps, 1)
                    act.sem_inc(signs, 2)
                    with act.Fori(0, heads) as h:
                        for x in (0, 1):
                            act.wait_ge(row_in[x], h * 16 + 16)

                        def step(n, by_act, s, slot, free, j):
                            if j == DIRECT:
                                return
                            if j == 0:
                                act.wait_ge(turned, h * len(groups) + len(groups))
                            for x, (lo, hi) in enumerate(HALVES):
                                if j is None:
                                    act.wait_ge(turned, h * len(groups) + (x + 1))
                                act.wait_ge(halves_done, free + x)
                                act.nop(nofuse=True)
                                nc.scalar.activation(sign[:, slot, lo * CB:hi * CB], row[:, lo * CB:hi * CB], ACT.Sign,
                                                     bias=g.att[:, 0, bass.ds(s * heads + h, 1)]).then_inc(signs, 1)
                        each_tile(act, h, step)
                        act.wait_ge(acc_ready, h + 1)
                        nc.scalar.activation(cols[0:rows, 0:4 * CB].rearrange("p (b n) -> p b n", n=CB),
                                             acc[0:rows, 0:4, 0:CB], ACT.Copy).then_inc(act_out, 1)

            @block.vector
            def _(dve):
                with on_path(dve, k, False):
                    dve.tensor_reduce(pick[0:rows, :, :],
                                      k.ident[0:rows, 0:rows].rearrange("p (x r c) -> p x c r", x=2, r=3),
                                      AX_X, ALU.add).then_inc(pick_ready, 1)
                    dve.wait_ge(exps, 1)
                    dve.sem_inc(signed, 8)
                    dve.tensor_scalar(g.att[:, 4, :], g.att[:, 0, :], -1.0, None, ALU.mult)
                    dve.tensor_scalar(src_part[:, :, :], src_part[:, :, :], 0.5, None,
                                      ALU.mult).then_inc(parts_ready, 1)
                    dve.wait_ge(parts_ready, 1)
                    whole = src_part[:, :, :].rearrange("p x (t h) -> p x t h", h=heads)[:, :, 1 + DIRECT::PERIOD, :]
                    dve.tensor_scalar(whole, whole, 2.0, None, ALU.mult).then_inc(parts_ready, 1)
                    dve.wait_ge(parts_ready, 2)
                    with dve.Fori(0, heads) as h:
                        for x in (0, 1):
                            dve.wait_ge(row_in[x], h * 16 + 16)

                        def step(n, by_act, s, slot, free, j):
                            for x, (lo, hi) in enumerate(HALVES):
                                if j == DIRECT:
                                    dve.wait_ge(halves_done, free + x)
                                    dve.nop(nofuse=True)
                                    dve.scalar_tensor_tensor(
                                        out=sign[:, slot, lo * CB:hi * CB], in0=row[:, lo * CB:hi * CB],
                                        scalar=g.att[:, 4, bass.ds(s * heads + h, 1)],
                                        in1=k.C[:, bass.ds(s, 1), lo * CB:hi * CB].rearrange("p a n -> p (a n)"),
                                        op0=ALU.is_gt, op1=ALU.mult).then_inc(signed, 1)
                                    continue
                                dve.wait_ge(signs, by_act + (x + 3))
                                dve.tensor_tensor(sign[:, slot, lo * CB:hi * CB], sign[:, slot, lo * CB:hi * CB],
                                                  k.C[:, bass.ds(s, 1), lo * CB:hi * CB].rearrange("p a n -> p (a n)"),
                                                  ALU.mult).then_inc(signed, 1)
                        each_tile(dve, h, step)
                        dve.wait_ge(acc_ready, h + 1)
                        dve.nop(nofuse=True)
                        dve.tensor_copy(cols[0:rows, 4 * CB:CW].rearrange("p (b n) -> p b n", n=CB),
                                        acc[0:rows, 4:CBANKS, 0:CB]).then_inc(dve_out, 1)
                        dve.wait_ge(stored, h * 16 + 16)
                        for n, (t, size) in enumerate(groups):
                            dve.wait_ge(turned, h * len(groups) + (n + 1 + len(groups)))
                            shares = g.att[:, 2:4, :].rearrange("p x (t h) -> p t x h", h=heads)
                            dve.tensor_tensor(prod[:, 0:size], turn[n % 2][:, 0:size],
                                              shares[:, t:t + size, :, bass.ds(h, 1)].broadcast_to([P, size, 2, w1]),
                                              ALU.mult).then_inc(prods, 1)
                            dve.wait_ge(prods, h * len(groups) + (n + 1))
                            dve.tensor_tensor(sums[:, t:t + size, :], prod[:, 0:size, 0, :], prod[:, 0:size, 1, :],
                                              ALU.add).then_inc(added, 1)
                            dve.wait_ge(added, h * len(groups) + (n + 1))

            @block.tensor
            def _(pe):
                with on_path(pe, k, False):
                    pe.sem_inc(halves_done, 2 * TILES)
                    pe.sem_inc(turned, len(groups))
                    pe.wait_ge(pick_ready, 1)
                    with pe.Fori(0, heads) as h:
                        for b in range(CBANKS):
                            pe.matmul(acc[:, b, 0:1], k.zeros[:, 0:P], k.zeros[:, 0:1], start=True, stop=False,
                                      skip_group_check=True)

                        def tile(s, slot):
                            values = v[:, bass.ds(s, 1), :, :, :].rearrange("p a x r c -> p (a x r c)")
                            for x, half_banks in enumerate(HALVES):
                                for b in range(*half_banks):
                                    pe.matmul(acc[0:rows, b, 0:CB], values[:, 0:rows],
                                              k.C[:, bass.ds(s, 1), b * CB:(b + 1) * CB].rearrange("p a n -> p (a n)"),
                                              start=False, stop=False, skip_group_check=True)
                                pe.wait_ge(signed, h * (2 * TILES) + (s * 2 + (x + 9)))
                                for b in range(*half_banks):
                                    ins = pe.matmul(acc[0:rows, b, 0:CB], values[:, rows:2 * rows],
                                                    sign[:, slot, b * CB:(b + 1) * CB],
                                                    start=False, stop=False, skip_group_check=True)
                                ins.then_inc(halves_done, 1)

                        for n, (lo, hi) in enumerate(V_PARTS):
                            pe.wait_ge(v_ready, h * len(V_PARTS) + (n + 2))
                            if n == 0:
                                tile(0, 0)
                                lo = 1
                            pe.nop(nofuse=True)
                            with pe.Fori(0, (hi - lo) // 2) as u:
                                for s in (0, 1):
                                    tile(u * 2 + (lo + s), (lo + s) % 2)
                        pe.matmul(acc[:, 0, 0:1], k.zeros[:, 0:P], k.zeros[:, 0:1], start=False, stop=True,
                                  skip_group_check=True).then_inc(acc_ready, 1)
                        for n, (t, size) in enumerate(groups):
                            if n == 0:
                                pe.wait_ge(act_out, h + 1)
                            if (t + size) * P > 4 * CB:
                                pe.wait_ge(dve_out, h + 1)
                            if n > 1:
                                pe.wait_ge(prods, h * len(groups) + (n - 1))
                            for c in range(size):
                                lo, hi = (t + c) * P, min((t + c + 1) * P, CW)
                                ins = pe.matmul(turn[n % 2][0:hi - lo, c, :, :], cols[0:rows, lo:hi],
                                                pick[0:rows, :, :], start=True, stop=True)
                            ins.then_inc(turned, 1)
                        pe.wait_ge(prods, (h + 1) * len(groups))


def gat_nodes(nc, a, k, g, parts):
    heads, hc, first = g.heads, D // g.heads, g.n == 1
    with ExitStack() as ctx:
        m = Memory(nc, ctx, f"post{g.n}")
        b = m.sb("b", [P, D], F32)
        y, sq, rest = (m.sb(n, [P, STRIP, D], F32) for n in ("y", "sq", "rest"))
        x, out = (m.sb(n, [P, 2, STRIP, D], F32) for n in ("x", "out"))
        sums = m.sb("sums", [P, 2, STRIP, D + heads], F32)
        st = m.sb("st", [P, 3, STRIP], F32)
        rw = m.sb("rw", [P, STRIP * heads], F32)
        consts, used, chain, to_act, from_act, normed, split = (
            m.sem(n) for n in ("consts", "used", "chain", "to_act", "from_act", "normed", "split"))
        x_in, sums_in, stored = ([m.sem(f"{n}{s}") for s in (0, 1)] for n in ("x_in", "sums_in", "stored"))
        with nc.Block() as block:
            @block.sync
            def _(sp):
                def load(i):
                    if i > 1:
                        sp.wait_ge(used, i - 1)
                    sp.dma_start(sums[:, i % 2], g.sums[:, i * STRIP:(i + 1) * STRIP, :]).then_inc(sums_in[i % 2], 16)
                    if not first:
                        sp.dma_start(x[:, i % 2], strip_of(k.x2, i)).then_inc(x_in[i % 2], 16)

                load(0)
                sp.dma_start(b[:, :], a[f"b{g.n}_2"].partition_broadcast(P)).then_inc(consts, 16)
                load(1)
                for i in range(STRIPS):
                    if i + 2 < STRIPS:
                        load(i + 2)
                    sp.wait_ge(normed, i + 1)
                    sp.dma_start(strip_of(g.out, i), out[:, i % 2]).then_inc(stored[i % 2], 16)
                for s in (0, 1):
                    sp.wait_ge(stored[s], 16 * len(range(s, STRIPS, 2)))

            if parts is not None:
                @block.gpsimd
                def _(pool):
                    for i in range(STRIPS):
                        pool.wait_ge(normed, i + 1)
                        split_strip(pool, split, out[:, i % 2], rest, parts, i)

            @block.scalar
            def _(act):
                for i in range(STRIPS):
                    act.wait_ge(to_act, i + 1)
                    if first:
                        nc.scalar.activation(sq[:, :, :], sq[:, :, :], ACT.Exp).then_inc(from_act, 1)
                    else:
                        nc.scalar.activation(st[:, 2, :], st[:, 1, :], ACT.Sqrt).then_inc(from_act, 1)

            @block.vector
            def _(dve):
                links = 3 if first else 3 + NORM_LINKS
                dve.wait_ge(consts, 16)
                for i in range(STRIPS):
                    link = Chain(dve, chain, i * links)
                    dve.wait_ge(sums_in[i % 2], (i // 2 + 1) * 16)
                    if i:
                        dve.wait_ge(normed, i)
                    s4 = sums[:, i % 2].rearrange("p t (h c) -> p (t h) c", h=heads)
                    link(dve.reciprocal(rw[:, :], s4[:, :, hc:hc + 1].rearrange("p h c -> p (h c)")))
                    link(dve.tensor_tensor(y[:, :, :].rearrange("p t (h c) -> p (t h) c", h=heads),
                                           s4[:, :, 0:hc], last(rw[:, :], hc), ALU.mult))
                    ins = dve.tensor_tensor(y[:, :, :], y[:, :, :], mid(b[:, :], STRIP), ALU.add)
                    if first:
                        ins.then_inc(used, 1)
                        dve.wait_ge(used, i + 1)
                    else:
                        link(ins)
                        dve.wait_ge(x_in[i % 2], (i // 2 + 1) * 16)
                        dve.tensor_tensor(y[:, :, :], y[:, :, :], x[:, i % 2], ALU.add).then_inc(used, 1)
                        dve.wait_ge(used, i + 1)

                    def act_link(ins):
                        ins.then_inc(to_act, 1)
                        dve.wait_ge(from_act, i + 1)
                    if i > 1:
                        dve.wait_ge(stored[i % 2], i // 2 * 16)
                        if not first:
                            dve.wait_ge(split, (i - 1) * SPLIT_STEPS)
                    if first:
                        act_link(dve.tensor_scalar(sq[:, :, :], y[:, :, :], 0.0, None, ALU.min))
                        link(dve.scalar_tensor_tensor(out=y[:, :, :], in0=y[:, :, :], scalar=0.0,
                                                      in1=sq[:, :, :], op0=ALU.max, op1=ALU.add))
                        dve.tensor_scalar(out[:, i % 2], y[:, :, :], -1.0, None, ALU.add).then_inc(normed, 1)
                    else:
                        normalize(link, act_link, dve, y[:, :, :], sq[:, :, :], st, out[:, i % 2]).then_inc(normed, 1)
                    assert link.n == links, link.n


def sage_layers(nc, a, k, out_dram, first_parts):
    with ExitStack() as ctx:
        m = Memory(nc, ctx, "sage")
        parts = [first_parts, m.sb("parts", [P, 3, TILES, D], BF16)]
        ewT_all = m.sb("ewT_all", [FE + 1, LAYERS, D], F32)
        ewT = m.sb("ewT", [FE + 1, 2, D], F32)
        w, b = m.sb("w", [P, 2, D], F32), m.sb("b", [P, 2, D], F32)
        edges = m.sb("edges", [FE + 1, SW], F32)
        aggT = m.sb("aggT", [P, SW], F32)
        y = m.sb("y", [P, STRIP, D], F32)
        ew = flat(y[:, :, :])[:, 0:LAYERS * FE].rearrange("p (l f) -> p l f", f=FE)
        st = m.sb("st", [P, 3, STRIP], F32)
        spare = parts[1].rearrange("p s t f -> p (s t f)").bitcast(F32)
        x, sq, out = (spare[:, n * SW:(n + 1) * SW].rearrange("p (t f) -> p t f", f=D) for n in range(3))
        pA = m.ps("pA", [P, 2, 2 * BANK])
        pO = m.ps("pO", [P, 2 * BANK])
        pW = m.ps("pW", [FE, LAYERS, D])
        loaded, ew_in, ew_turned, ew_ready, edges_in = (
            m.sem(n) for n in ("loaded", "ew_in", "ew_turned", "ew_ready", "edges_in"))
        agg, aggT_ready, lin, y_ready = (m.sem(n) for n in ("agg", "aggT_ready", "lin", "y_ready"))
        ew_slot = m.sem("ew_slot")
        high, rest, middle, low = (m.sem(n) for n in ("high", "rest", "middle", "low"))
        x_in, chain, var, std, normed, stored = (
            m.sem(n) for n in ("x_in", "chain", "var", "std", "normed", "stored"))

        def layers(eng, fn):
            with eng.Fori(0, LAYERS // 2) as u:
                fn(u * 2, 0, False)
                fn(u * 2 + 1, 1, False)
            fn(LAYERS - 1, 0, True)

        with nc.Block() as block:
            @block.sync
            def _(sp):
                with nc.allow_non_contiguous_dma(reason="rows of 64 bytes"):
                    sp.dma_start(ew, a["ews"].rearrange("l d f -> d l f")).then_inc(ew_in, 16)
                sp.dma_start(ewT_all[FE:FE + 1, :, :], a["ebs"].rearrange("(a l) d -> a l d", a=1)).then_inc(ew_in, 16)

                def one(l, par, is_last):
                    at = bass.ds(l, 1)
                    sp.dma_start(w[:, par, :], a["Ws"][at].rearrange("a f d -> (a f) d")).then_inc(loaded, 16)
                    sp.dma_start(b[:, par, :], a["bs"][at].rearrange("a d -> (a d)").partition_broadcast(P)
                                 ).then_inc(loaded, 16)
                    for i in range(STRIPS):
                        sp.wait_ge(agg, l * STRIPS + (i + 1))
                        sp.dma_start(edges[:, :], k.edgeT[:, i * SW:(i + 1) * SW]).then_inc(edges_in, 16)
                        if is_last:
                            if i:
                                sp.wait_ge(normed, i)
                            sp.dma_start(x, strip_of(k.x3, i)).then_inc(x_in, 16)
                            if i:
                                sp.dma_start(strip_of(out_dram, i - 1), out).then_inc(stored, 16)
                layers(sp, one)
                sp.wait_ge(normed, STRIPS)
                sp.dma_start(strip_of(out_dram, STRIPS - 1), out).then_inc(stored, 16)
                sp.wait_ge(stored, 16 * STRIPS)

            @block.gpsimd
            def _(pool):
                pool.wait_ge(ew_ready, 1)
                for l in range(LAYERS):
                    if l > 1:
                        pool.wait_ge(agg, (l - 1) * STRIPS + 1)
                    pool.tensor_copy(ewT[:, l % 2, :], ewT_all[:, l, :]).then_inc(ew_slot, 1)

            @block.tensor
            def _(pe):
                def linear(l, par, i):
                    it = l * STRIPS + i
                    pe.wait_ge(aggT_ready, it + 1)
                    pe.wait_ge(y_ready, it + 1)
                    for c in range(STRIP):
                        ins = pe.matmul(pO[:, c * P:(c + 1) * P], aggT[:, c * P:(c + 1) * P], w[:, par, :],
                                        start=True, stop=True)
                    ins.then_inc(lin, 1)

                def one(l, par, is_last):
                    pe.wait_ge(loaded, l * 32 + 32)
                    for i in range(STRIPS):
                        if i > 1:
                            pe.wait_ge(aggT_ready, l * STRIPS + (i - 1))

                        def features_ready(s):
                            if i == 0:
                                pe.wait_ge(low, l * STRIPS + s + 1)
                                pe.nop(nofuse=True)

                        def edge_terms():
                            if i == 0:
                                pe.wait_ge(ew_slot, l + 1)
                            pe.wait_ge(edges_in, (l * STRIPS + i) * 16 + 16)
                            for lo, hi in halves(SW):
                                pe.matmul(pA[:, i % 2, lo:hi], ewT[:, par, :], edges[:, lo:hi],
                                          start=False, stop=False, skip_group_check=True)
                        aggregate_strip(pe, pA[:, i % 2], k, parts[par], i, features_ready,
                                        edge_terms).then_inc(agg, 1)
                        if i:
                            linear(l, par, i - 1)
                    linear(l, par, STRIPS - 1)
                pe.sem_inc(agg, 1)
                pe.sem_inc(lin, 1)
                pe.wait_ge(ew_in, 32)
                for l in range(LAYERS):
                    ins = pe.transpose(pW[:, l, :], ew[:, l, :], k.ident[:, :])
                ins.then_inc(ew_turned, 1)
                layers(pe, one)

            @block.scalar
            def _(act):
                def one(l, par, is_last):
                    def split(i):
                        it = l * STRIPS + i
                        if is_last:
                            act.wait_ge(var, i + 1)
                            nc.scalar.activation(st[:, 2, :], st[:, 1, :], ACT.Sqrt).then_inc(std, 1)
                            return
                        act.wait_ge(y_ready, it + 2)
                        nc.scalar.activation(parts[1 - par][:, 0, i * STRIP:(i + 1) * STRIP, :], y[:, :, :],
                                             ACT.Relu).then_inc(high, 1)
                        act.wait_ge(rest, it + 1)
                        nc.scalar.activation(parts[1 - par][:, 1, i * STRIP:(i + 1) * STRIP, :], y[:, :, :],
                                             ACT.Copy).then_inc(middle, 1)

                    for i in range(STRIPS):
                        it = l * STRIPS + i
                        act.wait_ge(agg, it + 2)
                        act.wait_ge(lin, it + 1)
                        nc.scalar.activation(aggT[:, :], pA[:, i % 2, 0:SW], ACT.Copy).then_inc(aggT_ready, 1)
                        if i:
                            split(i - 1)
                    split(STRIPS - 1)
                layers(act, one)

            @block.vector
            def _(dve):
                links = 1 + NORM_LINKS

                def one(l, par, is_last):
                    for i in range(STRIPS):
                        it = l * STRIPS + i
                        dve.wait_ge(lin, it + 2)
                        dve.wait_ge(low, (l + 1) * STRIPS if is_last else it + STRIPS)
                        if is_last and i:
                            dve.wait_ge(normed, i)
                        for c in range(STRIP):
                            ins = dve.scalar_tensor_tensor(
                                out=y[:, c, :], in0=pO[:, c * D:(c + 1) * D],
                                scalar=k.rdeg[:, i * STRIP + c:i * STRIP + c + 1], in1=b[:, par, :],
                                op0=ALU.mult, op1=ALU.add)
                        ins.then_inc(y_ready, 1)
                        if is_last:
                            link = Chain(dve, chain, i * links)
                            dve.wait_ge(y_ready, it + 2)
                            dve.wait_ge(x_in, i * 16 + 16)
                            link(dve.tensor_tensor(y[:, :, :], y[:, :, :], x, ALU.add))

                            def act_link(ins):
                                ins.then_inc(var, 1)
                                dve.wait_ge(std, i + 1)
                            if i:
                                dve.wait_ge(stored, i * 16)
                            normalize(link, act_link, dve, y[:, :, :], sq, st, out).then_inc(normed, 1)
                            assert link.n == links, link.n
                            continue
                        dve.wait_ge(high, it + 1)
                        dve.scalar_tensor_tensor(out=y[:, :, :], in0=y[:, :, :], scalar=0.0,
                                                 in1=parts[1 - par][:, 0, i * STRIP:(i + 1) * STRIP, :],
                                                 op0=ALU.max, op1=ALU.subtract).then_inc(rest, 1)
                        dve.wait_ge(middle, it + 1)
                        dve.tensor_tensor(parts[1 - par][:, 2, i * STRIP:(i + 1) * STRIP, :], y[:, :, :],
                                          parts[1 - par][:, 1, i * STRIP:(i + 1) * STRIP, :],
                                          ALU.subtract).then_inc(low, 1)
                dve.sem_inc(low, STRIPS)
                dve.sem_inc(y_ready, 1)
                dve.wait_ge(ew_turned, 1)
                dve.tensor_copy(ewT_all[0:FE, :, :], pW[:, :, :]).then_inc(ew_ready, 1)
                layers(dve, one)


def attention_sums(nc, a, k, n, heads, x_dram, out_dram):
    class G:
        pass

    g = G()
    g.n, g.heads, g.x, g.out = n, heads, x_dram, out_dram
    g.table = nc.dram_tensor(f"table{n}", [P, TILES, D + heads], F32).ap()
    g.sums = nc.dram_tensor(f"att_sums{n}", [P, TILES, D + heads], F32).ap()
    g.src_rows = nc.dram_tensor(f"src_rows{n}", [heads, NP], F32).ap()
    g.dst_row = nc.dram_tensor(f"dst_row{n}", [heads, NP], F32).ap()
    g.dst_rows = [nc.dram_tensor(f"dst_rows{n}{x}", [heads, NP], F32).ap() for x in (0, 1)]
    with ExitStack() as ctx:
        m = Memory(nc, ctx, f"att{n}")
        g.att = m.sb("att", [P, 5, TILES * heads], F32)
        gat_linear(nc, a, k, g)
        source_bound(nc, k, g)
        if n == 2:
            turn_counts(nc, k, "turn_back", wide_only=True)
        store_rows(nc, k, g, [(0, g.src_rows)], f"srows{n}", True)
        gat_max(nc, k, g)
        turn_counts(nc, k, f"turn{n}", wide_only=n == 2)
        target_shares(nc, k, g)
        if n == 1:
            store_rows(nc, k, g, [(1, g.dst_row)], f"drow{n}", False)
            branch_sums(nc, k, g)
        always = None if n == 2 else True
        store_rows(nc, k, g, [(2, g.dst_rows[0]), (3, g.dst_rows[1])], f"drows{n}", always)
        gat_sums(nc, k, g, always)
    return g


def program(nc, a, out):
    class K:
        pass

    k = K()
    with ExitStack() as ctx:
        m = Memory(nc, ctx, "k")
        k.ranges_dram = nc.dram_tensor("ranges_dram", [TILES, 2], I32).ap()
        k.sums_dram = nc.dram_tensor("sums_dram", [TILES, P, AGG], F32).ap()
        k.edgeT = nc.dram_tensor("edgeT", [FE + 1, NP], F32).ap()
        k.x1, k.x2, k.h, k.x3 = (nc.dram_tensor(n, [NP, D], F32).ap() for n in ("x1", "x2", "h", "x3"))
        k.ident = m.sb("ident", [P, P], F32)
        k.zeros = m.sb("zeros", [P, P], BF16)
        k.rdeg = m.sb("rdeg", [P, TILES], F32)
        k.wide = m.sb("wide", [1, 1], I32)
        k.top = m.sb("top", [P, 4], F32)
        k.made = m.sem("made")
        k.C = m.sb("C", [P, TILES, NP], BF16)
        with ExitStack() as edge:
            me = Memory(nc, edge, "e")
            k.iota = me.sb("iota", [P, CW], I16)
            k.tile_base = me.sb("tile_base", [P, TILES + 1], F32)
            k.table = {n: me.sb(f"table_{n}", [P, CHUNKS], F32) for n in ("src", "dst", "w")}
            k.src_i = me.sb("src_i", [P, CHUNKS], I32)
            k.ranges = me.sb("ranges", [1, 2 * TILES + 1], I32)
            edge_tables(nc, a, k)
            build_counts(nc, a, k)
        with ExitStack() as layers_0_1:
            parts = Memory(nc, layers_0_1, "x1").sb("parts", [P, 3, TILES, D], BF16)
            gin_nodes(nc, a, k, parts)
            mean_layer(nc, a, k, parts)
        gat_nodes(nc, a, k, attention_sums(nc, a, k, 1, HEADS, k.x2, k.h), None)
        g = attention_sums(nc, a, k, 2, 1, k.h, k.x3)
        parts = m.sb("x3_parts", [P, 3, TILES, D], BF16)
        gat_nodes(nc, a, k, g, parts)
        sage_layers(nc, a, k, out, parts)


def kernel(x, src, dst, edge_attr_16, edge_weight, L0_gnn_W1, L0_gnn_b1, L0_gnn_W2, L0_gnn_b2, L0_gnn_eps,
           L1_gnn_W1, L1_gnn_b1, L1_gnn_W2, L1_gnn_b2, L2_gnn_W1, L2_gnn_att_src1, L2_gnn_att_dst1, L2_gnn_b1,
           L2_gnn_W2, L2_gnn_att_src2, L2_gnn_att_dst2, L2_gnn_b2, L3_gnn_Ws, L3_gnn_bs, L3_gnn_ews, L3_gnn_ebs):
    import numpy as np
    from concourse import bacc
    from concourse.bass_utils import run_bass_kernel_spmd

    def padded(v, n, fill=0):
        v = np.asarray(v)
        return np.concatenate([v, np.full((n - v.shape[0],) + v.shape[1:], fill, v.dtype)])

    arrays = {
        "x": padded(x, NP),
        "src": padded(src, E_PAD),
        "dst": padded(dst, E_PAD, NO_NODE),
        "w": padded(edge_weight, E_PAD),
        "edge_attr": padded(edge_attr_16, E_PAD),
        "w1_0": L0_gnn_W1, "b1_0": L0_gnn_b1, "w2_0": L0_gnn_W2, "b2_0": L0_gnn_b2, "eps": L0_gnn_eps,
        "w1_1": L1_gnn_W1, "b1_1": L1_gnn_b1, "w2_1": L1_gnn_W2, "b2_1": L1_gnn_b2,
        "w1_2": L2_gnn_W1, "b1_2": L2_gnn_b1, "att_src1": L2_gnn_att_src1, "att_dst1": L2_gnn_att_dst1,
        "w2_2": L2_gnn_W2, "b2_2": L2_gnn_b2, "att_src2": L2_gnn_att_src2, "att_dst2": L2_gnn_att_dst2,
        "Ws": L3_gnn_Ws, "bs": L3_gnn_bs, "ews": L3_gnn_ews, "ebs": L3_gnn_ebs,
    }
    arrays = {n: np.ascontiguousarray(v) for n, v in arrays.items()}
    nc = bacc.Bacc("TRN2", target_bir_lowering=False, num_devices=1)
    a = {n: nc.dram_tensor(f"in_{n}", v.shape, mybir.dt.from_np(v.dtype), kind="ExternalInput").ap()
         for n, v in arrays.items()}
    out = nc.dram_tensor("out", [NP, D], F32, kind="ExternalOutput").ap()
    program(nc, a, out)
    r = run_bass_kernel_spmd(nc, [{f"in_{n}": v for n, v in arrays.items()}], core_ids=[0])
    return r.results[0]["out"][:N_NODES]
```
